# Optimizing a Trainium2 kernel written in Bass

```python
import numpy as np
import jax
import jax.numpy as jnp

def _softmax(x, axis=-1):
    return jax.nn.softmax(x, axis=axis)

def _gelu(x):
    return jax.nn.gelu(x, approximate=True)

def _silu(x):
    return jax.nn.silu(x)

def _sigmoid(x):
    return jax.nn.sigmoid(x)

def _layernorm(x, axis=-1, eps=1e-05):
    m = jnp.mean(x, axis=axis, keepdims=True)
    v = jnp.var(x, axis=axis, keepdims=True)
    return (x - m) / jnp.sqrt(v + eps)

def _scatter_add(tgt, idx, src, axis=0):
    return tgt.at[idx].add(src)

def _segment_sum(src, seg, n):
    return jax.ops.segment_sum(src, seg, n)
kernel_name = 'mk_sandwich_d1_jaxref_r4_62c996'

def setup_inputs(seed: int=0):
    np.random.seed(seed)
    _w = jnp.asarray

    def _L0_attn_setup():
        import jax, jax.numpy as jnp
        import numpy as np
        B, N, D_MODEL, HEADS, DFF, M = (4, 1024, 256, 16, 1024, 64)
        DH = D_MODEL // HEADS
        EPS_K = 0.0001
        LN_EPS = 1e-05

        def softmax_kernel(x, proj, is_query):
            norm = x.shape[-1] ** (-0.25)
            ratio = proj.shape[0] ** (-0.5)
            xp = jnp.einsum('bhnd,md->bhnm', x * norm, proj)
            diag = jnp.sum(jnp.square(x), axis=-1, keepdims=True) * 0.5 * (norm * norm)
            if is_query:
                stab = jnp.max(xp, axis=-1, keepdims=True)
            else:
                stab = jnp.max(xp, axis=(-1, -2), keepdims=True)
            return ratio * (jnp.exp(xp - diag - stab) + EPS_K)

        def layer_norm(x, g, b):
            mu = jnp.mean(x, axis=-1, keepdims=True)
            var = jnp.mean(jnp.square(x - mu), axis=-1, keepdims=True)
            return (x - mu) * jax.lax.rsqrt(var + LN_EPS) * g + b
        key = jax.random.key(seed)
        ks = jax.random.split(key, 12)
        s = 0.02
        return {'video': jax.random.normal(ks[0], (B, N, D_MODEL), jnp.float32), 'Wq': jax.random.normal(ks[1], (D_MODEL, D_MODEL), jnp.float32) * s, 'bq': jnp.zeros((D_MODEL,), jnp.float32), 'Wk': jax.random.normal(ks[2], (D_MODEL, D_MODEL), jnp.float32) * s, 'bk': jnp.zeros((D_MODEL,), jnp.float32), 'Wv': jax.random.normal(ks[3], (D_MODEL, D_MODEL), jnp.float32) * s, 'bv': jnp.zeros((D_MODEL,), jnp.float32), 'Wo': jax.random.normal(ks[4], (D_MODEL, D_MODEL), jnp.float32) * s, 'bo': jnp.zeros((D_MODEL,), jnp.float32), 'proj': jax.random.normal(ks[5], (M, DH), jnp.float32), 'W1': jax.random.normal(ks[6], (DFF, D_MODEL), jnp.float32) * s, 'b1': jnp.zeros((DFF,), jnp.float32), 'W2': jax.random.normal(ks[7], (D_MODEL, DFF), jnp.float32) * s, 'b2': jnp.zeros((D_MODEL,), jnp.float32), 'g2': jnp.ones((D_MODEL,), jnp.float32), 'be2': jnp.zeros((D_MODEL,), jnp.float32), 'g3': jnp.ones((D_MODEL,), jnp.float32), 'be3': jnp.zeros((D_MODEL,), jnp.float32)}
    _L0_attn_in = _L0_attn_setup()

    def _L0_ffn_setup():
        import jax, jax.numpy as jnp
        import numpy as np
        B, S, D = (4, 1024, 256)
        DD = 4 * D
        N_EXPERTS = 8
        CAPACITY = 1.0
        LN_EPS = 1e-05
        key = jax.random.key(seed)
        ks = jax.random.split(key, 8)
        s1 = 1.0 / np.sqrt(D)
        s2 = 1.0 / np.sqrt(DD)
        return {'x': jax.random.normal(ks[0], (B, S, D), jnp.float32), 'gate_w': jax.random.normal(ks[1], (N_EXPERTS, D), jnp.float32) * 0.02, 'ln_w': jnp.ones((D,), jnp.float32), 'ln_b': jnp.zeros((D,), jnp.float32), 'fc1s': jax.random.normal(ks[2], (N_EXPERTS, DD, D), jnp.float32) * s1, 'b1s': jax.random.normal(ks[3], (N_EXPERTS, DD), jnp.float32) * s1, 'fc2s': jax.random.normal(ks[4], (N_EXPERTS, D, DD), jnp.float32) * s2, 'b2s': jax.random.normal(ks[5], (N_EXPERTS, D), jnp.float32) * s2}
    _L0_ffn_in = _L0_ffn_setup()
    _d = {'L0_attn_video': _L0_attn_in['video'], 'L0_attn_Wq': _L0_attn_in['Wq'], 'L0_attn_bq': _L0_attn_in['bq'], 'L0_attn_Wk': _L0_attn_in['Wk'], 'L0_attn_bk': _L0_attn_in['bk'], 'L0_attn_Wv': _L0_attn_in['Wv'], 'L0_attn_bv': _L0_attn_in['bv'], 'L0_attn_Wo': _L0_attn_in['Wo'], 'L0_attn_bo': _L0_attn_in['bo'], 'L0_attn_proj': _L0_attn_in['proj'], 'L0_attn_W1': _L0_attn_in['W1'], 'L0_attn_b1': _L0_attn_in['b1'], 'L0_attn_W2': _L0_attn_in['W2'], 'L0_attn_b2': _L0_attn_in['b2'], 'L0_attn_g2': _L0_attn_in['g2'], 'L0_attn_be2': _L0_attn_in['be2'], 'L0_attn_g3': _L0_attn_in['g3'], 'L0_attn_be3': _L0_attn_in['be3'], 'L0_ffn_gate_w': _L0_ffn_in['gate_w'], 'L0_ffn_ln_w': _L0_ffn_in['ln_w'], 'L0_ffn_ln_b': _L0_ffn_in['ln_b'], 'L0_ffn_fc1s': _L0_ffn_in['fc1s'], 'L0_ffn_b1s': _L0_ffn_in['b1s'], 'L0_ffn_fc2s': _L0_ffn_in['fc2s'], 'L0_ffn_b2s': _L0_ffn_in['b2s']}
    _x0 = _d['L0_attn_video']
    _d['L0_attn_video'] = jax.random.normal(jax.random.fold_in(jax.random.key(seed), 1), (8, 512, 256), dtype=_x0.dtype)
    del _x0
    return _d

def reference(L0_attn_video, L0_attn_Wq, L0_attn_bq, L0_attn_Wk, L0_attn_bk, L0_attn_Wv, L0_attn_bv, L0_attn_Wo, L0_attn_bo, L0_attn_proj, L0_attn_W1, L0_attn_b1, L0_attn_W2, L0_attn_b2, L0_attn_g2, L0_attn_be2, L0_attn_g3, L0_attn_be3, L0_ffn_gate_w, L0_ffn_ln_w, L0_ffn_ln_b, L0_ffn_fc1s, L0_ffn_b1s, L0_ffn_fc2s, L0_ffn_b2s):

    def _L0_attn_ref(video, Wq, bq, Wk, bk, Wv, bv, Wo, bo, proj, W1, b1, W2, b2, g2, be2, g3, be3):
        import jax, jax.numpy as jnp
        import numpy as np
        B, N, D_MODEL, HEADS, DFF, M = (4, 1024, 256, 16, 1024, 64)
        DH = D_MODEL // HEADS
        EPS_K = 0.0001
        LN_EPS = 1e-05

        def softmax_kernel(x, proj, is_query):
            norm = x.shape[-1] ** (-0.25)
            ratio = proj.shape[0] ** (-0.5)
            xp = jnp.einsum('bhnd,md->bhnm', x * norm, proj)
            diag = jnp.sum(jnp.square(x), axis=-1, keepdims=True) * 0.5 * (norm * norm)
            if is_query:
                stab = jnp.max(xp, axis=-1, keepdims=True)
            else:
                stab = jnp.max(xp, axis=(-1, -2), keepdims=True)
            return ratio * (jnp.exp(xp - diag - stab) + EPS_K)

        def layer_norm(x, g, b):
            mu = jnp.mean(x, axis=-1, keepdims=True)
            var = jnp.mean(jnp.square(x - mu), axis=-1, keepdims=True)
            return (x - mu) * jax.lax.rsqrt(var + LN_EPS) * g + b
        b, n, d = video.shape
        split = lambda t: t.reshape(b, n, HEADS, DH).transpose(0, 2, 1, 3)
        q = split(video @ Wq.T + bq)
        k = split(video @ Wk.T + bk)
        v = split(video @ Wv.T + bv)
        qp = softmax_kernel(q, proj, is_query=True)
        kp = softmax_kernel(k, proj, is_query=False)
        k_sum = jnp.sum(kp, axis=2)
        denom = jnp.einsum('bhnm,bhm->bhn', qp, k_sum)
        ctx = jnp.einsum('bhnm,bhnd->bhmd', kp, v)
        out = jnp.einsum('bhnm,bhmd->bhnd', qp, ctx) / denom[..., None]
        attn = out.transpose(0, 2, 1, 3).reshape(b, n, d) @ Wo.T + bo
        x = layer_norm(video + attn, g2, be2)
        ff = jax.nn.relu(x @ W1.T + b1) @ W2.T + b2
        return layer_norm(x + ff, g3, be3)

    def _L0_ffn_ref(x, gate_w, ln_w, ln_b, fc1s, b1s, fc2s, b2s):
        import jax, jax.numpy as jnp
        import numpy as np
        B, S, D = (4, 1024, 256)
        DD = 4 * D
        N_EXPERTS = 8
        CAPACITY = 1.0
        LN_EPS = 1e-05
        og_shape = x.shape
        d = og_shape[-1]
        xf = x.reshape(-1, d)
        bs = xf.shape[0]
        n = gate_w.shape[0]
        k = int(bs * CAPACITY) // n
        scores = jax.nn.softmax(xf @ gate_w.T, axis=-1)
        vals, idx = jax.lax.top_k(scores.T, k)
        kept_w = vals.T
        kept_idx = idx.T
        flat_idx = kept_idx.reshape(-1)
        y = xf[flat_idx].reshape(k, n, d)
        mu = y.mean(-1, keepdims=True)
        var = ((y - mu) ** 2).mean(-1, keepdims=True)
        y = (y - mu) * jax.lax.rsqrt(var + LN_EPS) * ln_w + ln_b
        h = jnp.einsum('knd,nfd->knf', y, fc1s) + b1s
        h = jax.nn.gelu(h, approximate=True)
        out = jnp.einsum('knf,ndf->knd', h, fc2s) + b2s
        out = out * kept_w[..., None]
        xf = xf.at[flat_idx].add(out.reshape(k * n, d))
        return xf.reshape(og_shape)
    x = L0_attn_video
    x = x + _layernorm(_L0_attn_ref(_layernorm(x, axis=-1), L0_attn_Wq, L0_attn_bq, L0_attn_Wk, L0_attn_bk, L0_attn_Wv, L0_attn_bv, L0_attn_Wo, L0_attn_bo, L0_attn_proj, L0_attn_W1, L0_attn_b1, L0_attn_W2, L0_attn_b2, L0_attn_g2, L0_attn_be2, L0_attn_g3, L0_attn_be3), axis=-1)
    x = x + _layernorm(_L0_ffn_ref(_layernorm(x, axis=-1), L0_ffn_gate_w, L0_ffn_ln_w, L0_ffn_ln_b, L0_ffn_fc1s, L0_ffn_b1s, L0_ffn_fc2s, L0_ffn_b2s), axis=-1)
    return x

_drawn_inputs = setup_inputs


def setup_inputs(seed=0):
    import zlib

    import numpy as np

    out = dict(_drawn_inputs(seed))
    spreads = {'L0_attn_bq': (0.0, 2.0),
     'L0_attn_bk': (0.0, 2.0),
     'L0_attn_bv': (0.0, 0.525),
     'L0_attn_bo': (0.0, 0.1),
     'L0_attn_b1': (0.0, 0.361),
     'L0_attn_b2': (0.0, 0.1),
     'L0_attn_g2': (1.0, 0.2),
     'L0_attn_be2': (0.0, 0.1),
     'L0_attn_g3': (1.0, 0.2),
     'L0_attn_be3': (0.0, 0.1),
     'L0_ffn_ln_w': (1.0, 0.6),
     'L0_ffn_ln_b': (0.0, 0.8)}
    factors = {'L0_attn_Wq': 64.0,
     'L0_attn_Wk': 64.0,
     'L0_attn_Wv': 8.0,
     'L0_attn_Wo': 3.702,
     'L0_attn_proj': 64.0,
     'L0_ffn_b1s': 8.0,
     'L0_ffn_b2s': 26.312}
    for name, (base, spread) in spreads.items():
        noise = np.random.default_rng([zlib.crc32(name.encode()), seed]).standard_normal(out[name].shape)
        drawn = base * np.exp(spread * noise) if base else spread * noise
        out[name] = jnp.asarray(drawn.astype(out[name].dtype))
    for name, factor in factors.items():
        out[name] = (out[name] * factor).astype(out[name].dtype)
    return out
```

```python
from contextlib import ExitStack

import numpy as np
import concourse.bass as bass
from concourse import mybir

ALU = mybir.AluOpType
ACT = mybir.ActivationFunctionType
F32 = mybir.dt.float32
BF16 = mybir.dt.bfloat16
I32 = mybir.dt.int32
U32 = mybir.dt.uint32
AX_X = mybir.AxisListType.X
RMAX = bass.bass_isa.ReduceOp.max

P = 128
B, N, D = 8, 512, 256
T = B * N
TT = N // P
C = D // P
H, DH, M = 16, 16, 64
G = 2
HG = H // G
PAIRS = H // 2
FF = 1024
FC = FF // P
EPS_K = 1e-4
N_CONST = 12
N_SEL = 15
LN_EPS = 1e-5
LNS = 6
NORM = DH ** -0.25
E = 8
KEEP = T // E
SEG = P // E
SEGW = T // SEG
ROW = D + E
GT = KEEP // P

ROUNDS, CANDS = 10, 7
SA, SB = 32, 16
SR = P // SA
M_JOBS, M_SLOTS = 12, 4
J_MX, J_MH, J_MY = 0, 2, 10

A_JOBS, X_JOBS, F_JOBS = 26, 12, 16
(J_XT, J_K, J_Q, J_V, J_DK, J_DQ, J_CTX, J_KSUM, J_CTXT, J_OUT, J_OT, J_AT, J_WO) = (
    0, 2, 4, 6, 8, 10, 12, 13, 14, 15, 18, 22, 24)
J_XK, J_XQ, J_TQ = 0, 4, 8
J_X2T, J_H, J_Y, J_XFT, J_G = 0, 2, 10, 12, 14


def wait(eng, sem, value):
    if isinstance(value, int) and value <= 0:
        return
    eng.wait_ge(sem, value)


class Steps:

    def __init__(self, eng, sem, per, i):
        self.eng, self.sem, self.per, self.i, self.n = eng, sem, per, i, 0

    def put(self, ins):
        ins.then_inc(self.sem, 1)
        self.n += 1

    def sync(self):
        self.eng.wait_ge(self.sem, self.i * self.per + self.n)

    def link(self, ins):
        self.put(ins)
        self.sync()

    def end(self):
        assert self.n == self.per, (self.sem, self.n, self.per)


def build(nc, video, WqT, bq, WkT, bk, WvT, bv, WoT, bo, projT, W1T, b1, W2T, b2, g2, be2, g3, be3,
          gateT, ln_w, ln_b, fc1T, b1s, fc2T, b2s, out, stop=None):
    with ExitStack() as ctx:
        def sb(name, shape, dt=F32):
            return ctx.enter_context(nc.sbuf_tensor(name, shape, dt))

        def sem(name):
            return ctx.enter_context(nc.semaphore(name))

        pA = [ctx.enter_context(nc.psum_tensor(f"pA{s}", [P, 512], F32)) for s in range(2)]
        pX = [ctx.enter_context(nc.psum_tensor(f"pX{s}", [P, 2, 512], F32)) for s in range(2)]
        pF = [ctx.enter_context(nc.psum_tensor(f"pF{s}", [P, 512], F32)) for s in range(2)]

        pM = [pX[k // 2][:, k % 2, :] for k in range(4)]
        x1_d = nc.dram_tensor("x1_scratch", (T, D), F32, kind="Internal").ap()
        acc_d = nc.dram_tensor("acc_scratch", (T, D), F32, kind="Internal").ap()
        row_d = nc.dram_tensor("row_scratch", (T, ROW), F32, kind="Internal").ap()

        wq, wk, wv, wo = (sb(n, [P, C, D]) for n in ("wq", "wk", "wv", "wo"))
        w1 = sb("w1", [P, C, FF])
        w2 = sb("w2", [P, FC, D])
        gate = sb("gate", [P, C, P])
        projbd = sb("projbd", [P, HG * M])
        bqk = sb("bqk", [P, 2, G])
        b1c = sb("b1c", [P, FC])
        bv_b, bo_b, b2_b, g2_b, be2_b, g3_b, be3_b, lnw_b, lnb_b = (
            sb(n, [P, D]) for n in ("bv_b", "bo_b", "b2_b", "g2_b", "be2_b", "g3_b", "be3_b", "lnw_b", "lnb_b"))
        ident = sb("ident", [P, P])
        ones32 = sb("ones32", [P, 32])
        mhalf = sb("mhalf", [P, TT])
        epsk_c = sb("epsk_c", [P, 1])
        headmask = sb("headmask", [P, 32])
        denmask = sb("denmask", [P, PAIRS, 32])
        xin = sb("xin", [P, TT, D])
        xn = sb("xn", [P, TT, D])
        xnb = sb("xnb", [P, TT, D])
        xT = sb("xT", [P, C, N])
        kT = sb("kT", [P, G, N])
        qT = sb("qT", [P, G, N])
        v = sb("v", [P, TT, D])
        sq = sb("sq", [P, 2, 2, D])
        dgk = sb("dgk", [P, TT, H])
        dgq = sb("dgq", [P, TT, H])
        mxk = sb("mxk", [P, TT, H])
        mxq = sb("mxq", [P, TT, H])
        kmax = sb("kmax", [P, H])
        stabk = sb("stabk", [P, H])
        kbias = sb("kbias", [P, TT, H])
        qbias = sb("qbias", [P, TT, H])
        kp = sb("kp", [P, TT, H * M])
        qe = sb("qe", [P, TT, H * M])
        qp = sb("qp", [P, PAIRS, N])
        cs = sb("cs", [P, 2, G * P])
        ctxbd = sb("ctxbd", [P, PAIRS, 32])
        denbd = sb("denbd", [P, PAIRS, 32])
        oT = sb("oT", [P, 3, N])
        rden = sb("rden", [P, TT, H])
        at = sb("at", [P, TT, D])
        aT = sb("aT", [P, C, N])
        r = sb("r", [P, TT, D])
        x2 = sb("x2", [P, TT, D])
        x2b = sb("x2b", [P, TT, D])
        x2T = sb("x2T", [P, C, N])
        h = sb("h", [P, FC, N])
        z = sb("z", [P, TT, D])
        z4 = sb("z4", [P, TT, D])
        xres = sb("xres", [P, TT, D])
        x1 = sb("x1", [P, TT, D])
        xf = sb("xf", [P, TT, D])
        y = sb("y", [P, TT, D])
        xfT = x2T
        lg = sb("lg", [P, TT, E])
        lmx = sb("lmx", [P, TT])
        lsum = sb("lsum", [P, TT])
        lrec = sb("lrec", [P, TT])
        sct = sb("sct", [P, TT, E])
        sc = sb("sc", [P, C, E, SEG])
        st = [sb(f"st{k}", [P, TT, 6]) for k in range(LNS)]
        mv = [sb(f"mv{k}", [P, TT, 2]) for k in range(LNS)]
        ve = [sb(f"ve{k}", [P, TT]) for k in range(LNS)]
        rstd = [sb(f"rstd{k}", [P, TT]) for k in range(LNS)]

        kp_f, qe_f, qp_f = (a[:].rearrange("p a b -> p (a b)") for a in (kp, qe, qp))
        S, gt, eq, gin, ein, place = (kp_f[:, k * SEGW:(k + 1) * SEGW] for k in range(6))
        flags = kp_f[:, 8 * SEGW:(8 + CANDS) * SEGW].rearrange("p (k j) -> p k j", k=CANDS)
        placei, dig_a, dig_b = (kp_f[:, k * SEGW:(k + 1) * SEGW].bitcast(I32).rearrange("p (c e s) -> p c e s", c=C, e=E) for k in (8, 9, 10))
        thr = sb("thr", [P, 1], U32)
        step = sb("step", [P, CANDS], U32)
        cand = sb("cand", [P, CANDS], U32)
        cnt = sb("cnt", [P, CANDS])
        passed = sb("passed", [P, CANDS])
        npass = sb("npass", [P, 1])
        up = sb("up", [P, 1], U32)
        ones_row = sb("ones_row", [P, SEGW])
        blockones = sb("blockones", [P, P])
        blockbelow = sb("blockbelow", [P, P])
        pair_cnt = sb("pair_cnt", [P, 2])
        offs = sb("offs", [P, 3])
        eoff = sb("eoff", [P, 1])
        iota_row = sb("iota_row", [P, SA], I32)
        iotaf = sb("iotaf", [P, SA])
        tilef = sb("tilef", [P, C, SEG])
        pcol = sb("pcol", [P, 1])
        oneA = qp_f.bitcast(BF16).rearrange("p (c s e a) -> p c s e a", c=C, s=SEG, e=E)
        oneB = qe_f.bitcast(BF16).rearrange("p (c s e k b) -> p c s e k b", c=C, s=SEG, e=E, k=2)
        spread = sb("spread", [P, P], BF16)
        rmask = sb("rmask", [P, SR])
        pmod = sb("pmod", [P, 1], I32)
        pmodf = sb("pmodf", [P, 1])
        spread_one = sb("spread_one", [P, SA])
        pint = sb("pint", [P, 1], I32)
        tint = sb("tint", [P, C, SEG], I32)
        Rbd = sb("Rbd", [P, 2, 4, 2 * SB], BF16)
        idm = sb("idm", [P, E * 2, SR, GT])
        idf = sb("idf", [P, E, 2, GT])
        idx = sb("idx", [P, E, GT])
        w1e, w2e, xgT, og = w1, w2, kT, at
        b1e = sb("b1e", [P, E, FC])
        b1cur = sb("b1cur", [P, FC])
        b2cur = sb("b2cur", [P, D])
        xg = sb("xg", [P, GT, ROW])
        idx_g = sb("idx_g", [P, GT], U32)
        idx_s = sb("idx_s", [P, GT], U32)
        wnext = sb("wnext", [P, GT])
        wcur = sb("wcur", [P, GT])
        zero4 = sb("zero4", [P, FC])
        acc_s, x1_s, o_s = (a.rearrange("p (k t d) -> p k t d", k=2, t=TT) for a in (qp_f[:, 0:2 * TT * D], qp_f[:, 2 * TT * D:], qe_f[:, 0:2 * TT * D]))
        stl = sb("stl", [P, 2, TT, 6])
        mvl = sb("mvl", [P, 2, TT, 2])
        vel = sb("vel", [P, 2, TT])
        rsl = sb("rsl", [P, 2, TT])


        w_in = sem("w_in")
        wff_in = sem("wff_in")
        wproj_in = sem("wproj_in")
        const_step, const_ready, proj_ready = sem("const_step"), sem("const_ready"), sem("proj_ready")
        a_ready, x_ready, f_ready = sem("a_ready"), sem("x_ready"), sem("f_ready")
        var_ready = [sem(f"var_ready{k}") for k in range(LNS)]
        ve_ready = [sem(f"ve_ready{k}") for k in range(LNS)]
        rstd_ready = [sem(f"rstd_ready{k}") for k in range(LNS)]
        xin_in, xres_in = sem("xin_in"), sem("xres_in")
        xn_ready, xnb_ready = sem("xn_ready"), sem("xnb_ready")
        xT_ready, kT_ready, qT_ready, v_ready = sem("xT_ready"), sem("kT_ready"), sem("qT_ready"), sem("v_ready")
        sq_ready, dg_ready = sem("sq_ready"), sem("dg_ready")
        xk_ready, kmx_ready, kmax_ready, stab_ready = sem("xk_ready"), sem("kmx_ready"), sem("kmax_ready"), sem("stab_ready")
        ks_ready, ke_ready, kp_ready = sem("ks_ready"), sem("ke_ready"), sem("kp_ready")
        qs_ready, qe_ready, qpa_ready, qpv_ready = sem("qs_ready"), sem("qe_ready"), sem("qpa_ready"), sem("qpv_ready")
        cs_ready, cx_ready, oT_ready = sem("cs_ready"), sem("cx_ready"), sem("oT_ready")
        at_ready, aT_ready, r_ready = sem("at_ready"), sem("aT_ready"), sem("r_ready")
        x2_ready, x2b_ready, x2T_ready, h_ready = sem("x2_ready"), sem("x2b_ready"), sem("x2T_ready"), sem("h_ready")
        z_ready, x1_ready, xf_ready, y_ready = sem("z_ready"), sem("x1_ready"), sem("xf_ready"), sem("y_ready")
        xfT_ready, lg_ready = sem("xfT_ready"), sem("lg_ready")
        ls_ready, le_ready, sc_ready = sem("ls_ready"), sem("le_ready"), sem("sc_ready")
        x1_out, xf_out, y_out, sc_out = sem("x1_out"), sem("xf_out"), sem("y_out"), sem("sc_out")
        dve_n, dve_a, dve_f = sem("dve_n"), sem("dve_a"), sem("dve_f")
        sel_const, sel_step, s_turned, s_ready = sem("sel_const"), sem("sel_step"), sem("s_turned"), sem("s_ready")
        cnt_ready, tot_ready, dve_s = sem("cnt_ready"), sem("tot_ready"), sem("dve_s")
        pair_ready, off_ready, place_ready, place_turned = sem("pair_ready"), sem("off_ready"), sem("place_ready"), sem("place_turned")
        onehot_ready, ids_ready, rbd_ready, spread_ready, idx_ready = (
            sem("onehot_ready"), sem("ids_ready"), sem("rbd_ready"), sem("spread_ready"), sem("idx_ready"))
        m_ready, xgT_ready, he_ready, yo_ready = sem("m_ready"), sem("xgT_ready"), sem("he_ready"), sem("yo_ready")
        w1e_in, w2e_in, b1e_in, b2e_in = sem("w1e_in"), sem("w2e_in"), sem("b1e_in"), sem("b2e_in")
        idxg_ready, idxs_ready, b1cur_ready, wnext_ready, wcur_ready = (
            sem("idxg_ready"), sem("idxs_ready"), sem("b1cur_ready"), sem("wnext_ready"), sem("wcur_ready"))
        gathered, scattered, og_ready = sem("gathered"), sem("scattered"), sem("og_ready")
        acc_in = [sem(f"acc_in{k}") for k in range(2)]
        x1_in = [sem(f"x1_in{k}") for k in range(2)]
        out_done = [sem(f"out_done{k}") for k in range(2)]
        stl_ready, vl_ready, vel_ready, rl_ready, nl_ready, ol_ready = (
            sem("stl_ready"), sem("vl_ready"), sem("vel_ready"), sem("rl_ready"), sem("nl_ready"), sem("ol_ready"))
        STEPS_N, STEPS_A, STEPS_F = 1, 13, 16
        SEL_STEPS = 4

        vid_d = video.rearrange("(b t p) d -> b p t d", t=TT, p=P)
        x1_t = x1_d.rearrange("(b t p) d -> b p t d", t=TT, p=P)
        acc_t = acc_d.rearrange("(b t p) d -> b p t d", t=TT, p=P)
        row_t = row_d.rearrange("(b t p) r -> b p t r", t=TT, p=P)

        def batches(eng, body):
            body(0, None)
            body(1, 0)
            with eng.Fori(2, B - 1) as i:
                body(i, i - 1)
            body(B - 1, B - 2)
            body(None, B - 1)

        out_t = out.rearrange("(b t p) d -> b p t d", t=TT, p=P)

        def experts(eng, body):
            body(0, True)
            with eng.Fori(1, E - 1) as e:
                body(e, True)
            body(E - 1, False)

        waits_met = sem("waits_met")

        def settled(eng):
            eng.sem_inc(waits_met, 1)

        block = ctx.enter_context(nc.Block())

        @block.sync
        def _(sp):
            def load_x(i):
                wait(sp, xn_ready, i * TT)
                sp.dma_start(xin[:], vid_d[i]).then_inc(xin_in, 16)

            def body(i, f):
                if i is not None and not (isinstance(i, int) and i == B - 1):
                    load_x(i + 1)
                if f is not None:
                    wait(sp, x1_ready, f)
                    sp.dma_start(xres[:], vid_d[f]).then_inc(xres_in, 16)
                    for ready, done, dst, src in ((x1_ready, x1_out, x1_t[f], x1[:]), (xf_ready, xf_out, acc_t[f], xf[:]),
                                                  (y_ready, y_out, row_t[f][:, :, 0:D], y[:]),
                                                  (sc_ready, sc_out, row_t[f][:, :, D:ROW], sct[:])):
                        sp.wait_ge(ready, f + 1)
                        sp.dma_start(dst, src).then_inc(done, 16)

            load_x(0)
            for w, src in ((wk, WkT), (wq, WqT), (wv, WvT)):
                sp.dma_start(w[:], src.rearrange("(c p) n -> p c n", p=P)).then_inc(w_in, 16)
            for w, src in ((wo, WoT), (w1, W1T), (w2, W2T)):
                sp.dma_start(w[:], src.rearrange("(c p) n -> p c n", p=P)).then_inc(wff_in, 16)
            batches(sp, body)
            if stop != "x1":
                sp.dma_start(b1e[:], b1s).then_inc(b1e_in, 16)

                def load_expert(e):
                    wait(sp, m_ready, (e - 1) * M_JOBS + J_MY)
                    sp.dma_start(w1e[:], fc1T[e].rearrange("(c p) n -> p c n", p=P)).then_inc(w1e_in, 16)
                    wait(sp, m_ready, e * M_JOBS)
                    sp.dma_start(w2e[:], fc2T[e].rearrange("(c p) n -> p c n", p=P)).then_inc(w2e_in, 16)
                    wait(sp, yo_ready, e * 2)
                    sp.dma_start(b2cur[:], b2s[e].partition_broadcast(P)).then_inc(b2e_in, 16)

                sp.wait_ge(f_ready, (B - 1) * F_JOBS + J_Y + 2)
                load_expert(0)
                with sp.Fori(1, E) as e:
                    load_expert(e)

                for s in (x1_out, xf_out, y_out, sc_out):
                    sp.wait_ge(s, 16 * B)
                sp.wait_ge(scattered, 16 * GT * E)

                def last(j, k, q):
                    wait(sp, ol_ready, j - 1)
                    sp.dma_start(acc_s[:, k], acc_t[j]).then_inc(acc_in[k], 16)
                    sp.dma_start(x1_s[:, k], x1_t[j]).then_inc(x1_in[k], 16)

                def put(j, k):
                    sp.wait_ge(ol_ready, j + 1)
                    sp.dma_start(out_t[j], o_s[:, k]).then_inc(out_done[k], 16)

                last(0, 0, 0)
                last(1, 1, 0)
                with sp.Fori(0, B // 2 - 1) as j2:
                    for k in range(2):
                        put(j2 * 2 + k, k)
                        last(j2 * 2 + k + 2, k, 0)
                for k in range(2):
                    put(B - 2 + k, k)
                for k in range(2):
                    sp.wait_ge(out_done[k], 16 * (B // 2))
            if stop == "x1":
                for s in (x1_out, xf_out, y_out, sc_out):
                    sp.wait_ge(s, 16 * B)
                sp.dma_start(out, {"x1": x1_d}[stop]).then_inc(x1_out, 16)
                sp.wait_ge(x1_out, 16 * B + 16)

        @block.scalar
        def _(act):
            act.dma_start(bqk[:, 0, :], bq).then_inc(w_in, 16)
            act.dma_start(bqk[:, 1, :], bk).then_inc(w_in, 16)
            act.dma_start(bv_b[:], bv.partition_broadcast(P)).then_inc(w_in, 16)
            act.dma_start(bo_b[:], bo.partition_broadcast(P)).then_inc(w_in, 16)
            act.wait_ge(const_ready, 2)
            for g in range(HG):
                act.dma_start(projbd[DH * g:DH * g + DH, M * g:M * g + M], projT).then_inc(wproj_in, 16)
            for c in range(C):
                act.dma_start(gate[:, c, 0:E], gateT[c * P:(c + 1) * P, :]).then_inc(wff_in, 16)
            act.dma_start(b1c[:], b1).then_inc(wff_in, 16)
            for dst, src in ((b2_b, b2), (g2_b, g2), (be2_b, be2), (g3_b, g3), (be3_b, be3), (lnw_b, ln_w), (lnb_b, ln_b)):
                act.dma_start(dst[:], src.partition_broadcast(P)).then_inc(wff_in, 16)

            def take_a(i, n, dst, func, done, **kw):
                act.wait_ge(a_ready, i * A_JOBS + n + 1)
                nc.scalar.activation(dst, pA[n % 2][:], func, **kw).then_inc(done, 1)

            def take_f(f, n, dst, func, done, **kw):
                act.wait_ge(f_ready, f * F_JOBS + n + 1)
                nc.scalar.activation(dst, pF[n % 2][:], func, **kw).then_inc(done, 1)

            def xk_copy(i, t):
                act.wait_ge(x_ready, i * X_JOBS + J_XK + t + 1)
                nc.scalar.activation(kp[:, t, :], pX[t % 2][:].rearrange("p a b -> p (a b)"), ACT.Copy).then_inc(xk_ready, 1)

            def squares(i, m):
                wait(act, dg_ready, i * 4 + m - 1)
                take_a(i, J_DK + m, sq[:, m % 2].rearrange("p a b -> p (a b)"), ACT.Square, sq_ready)

            def relu(f, n):
                take_f(f, J_H + n, h[:, n, :], ACT.Relu, h_ready, bias=b1c[:, n:n + 1])

            def exps(i, t):
                act.wait_ge(ks_ready, i * TT + t + 1)
                nc.scalar.activation(kp[:, t, :], kp[:, t, :], ACT.Exp).then_inc(ke_ready, 1)
                act.wait_ge(qs_ready, i * TT + t + 1)
                nc.scalar.activation(qe[:, t, :], qe[:, t, :], ACT.Exp).then_inc(qe_ready, 1)

            def body(i, f):
                if i is not None:
                    for c in range(C):
                        take_a(i, J_XT + c, xT[:, c, :], ACT.Copy, xT_ready)
                    for c in range(G):
                        take_a(i, J_K + c, kT[:, c, :], ACT.Identity, kT_ready, bias=bqk[:, 1, c:c + 1])
                    for c in range(G):
                        take_a(i, J_Q + c, qT[:, c, :], ACT.Identity, qT_ready, bias=bqk[:, 0, c:c + 1])
                    xk_copy(i, 0)
                    xk_copy(i, 1)
                    squares(i, 0)
                    squares(i, 1)
                    xk_copy(i, 2)
                    squares(i, 2)
                    squares(i, 3)
                    xk_copy(i, 3)
                if f is not None:
                    for c in range(C):
                        take_f(f, J_X2T + c, x2T[:, c, :], ACT.Copy, x2T_ready)
                    relu(f, 0)
                for t in range(TT):
                    if i is not None:
                        exps(i, t)
                    if f is not None:
                        relu(f, t + 1)
                if f is not None:
                    for n in range(TT + 1, FC):
                        relu(f, n)
                if i is not None:
                    for n in range(2):
                        act.wait_ge(a_ready, i * A_JOBS + J_CTX + n + 1)
                        nc.scalar.activation(cs[:, n, :], pA[n][:, 0:G * P], ACT.Copy).then_inc(cs_ready, 1)
                    for n in range(TT):
                        act.wait_ge(x_ready, i * X_JOBS + J_TQ + n + 1)
                        nc.scalar.activation(qp[:, 2 * n, :], pX[n % 2][:, 0, :], ACT.Identity, bias=epsk_c[:, 0:1]).then_inc(qpa_ready, 1)
                    for n in range(3):
                        take_a(i, J_OUT + n, oT[:, n, :], ACT.Copy, oT_ready)
                    for c in range(C):
                        take_a(i, J_AT + c, aT[:, c, :], ACT.Copy, aT_ready)
                if f is not None:
                    for c in range(C):
                        take_f(f, J_XFT + c, x2T[:, c, :], ACT.Copy, xfT_ready)
                    act.wait_ge(ls_ready, f + 1)
                    nc.scalar.activation(lg[:], lg[:], ACT.Exp).then_inc(le_ready, 1)

            act.wait_ge(w_in, 16 * 7)
            act.wait_ge(wff_in, 16 * 13)
            act.wait_ge(const_ready, N_CONST)
            batches(act, body)
            if stop == "x1":
                return

            def take_m(e, n, dst, func, done, **kw):
                act.wait_ge(m_ready, e * M_JOBS + n + 1)
                nc.scalar.activation(dst, pM[n % M_SLOTS], func, **kw).then_inc(done, 1)

            def turned(e):
                for c in range(C):
                    take_m(e, J_MX + c, xgT[:, c, :], ACT.Copy, xgT_ready)

            def expert(e, more):
                act.wait_ge(b1cur_ready, e + 1)
                for n in range(FC):
                    take_m(e, J_MH + n, h[:, n, :], ACT.Gelu_apprx_tanh, he_ready, bias=b1cur[:, n:n + 1])
                if more:
                    turned(e + 1)

            turned(0)
            experts(act, expert)

        @block.gpsimd
        def _(pool):
            nc.gpsimd.memset(projbd[:], 0.0).then_inc(const_ready, 1)
            nc.gpsimd.memset(gate[:], 0.0).then_inc(const_ready, 1)
            nc.gpsimd.memset(ident[:], 0.0).then_inc(const_step, 1)
            pool.wait_ge(const_step, 1)
            nc.gpsimd.affine_select(out=ident[:], in_=ident[:], compare_op=ALU.not_equal, fill=1.0, base=0,
                                    pattern=[[-1, P]], channel_multiplier=1).then_inc(const_ready, 1)
            nc.gpsimd.memset(ones32[:], 1.0).then_inc(const_ready, 1)
            nc.gpsimd.memset(mhalf[:], -0.5).then_inc(const_ready, 1)
            nc.gpsimd.memset(epsk_c[:], EPS_K).then_inc(const_ready, 1)
            nc.gpsimd.memset(headmask[:], 0.0).then_inc(const_step, 1)
            nc.gpsimd.memset(denmask[:], 0.0).then_inc(const_step, 1)
            pool.wait_ge(const_step, 3)
            for k in range(2):
                rows = slice(M * k, M * k + M)
                nc.gpsimd.memset(headmask[rows, DH * k:DH * k + DH], 1.0).then_inc(const_ready, 1)
                for g in range(G):
                    nc.gpsimd.memset(denmask[rows, 4 * g:4 * g + 4, 2 * g + k:2 * g + k + 1], 1.0).then_inc(const_ready, 1)

            def selection_constants():
                nc.gpsimd.memset(ones_row[:], 1.0).then_inc(sel_const, 1)
                nc.gpsimd.memset(zero4[:], 0.0).then_inc(sel_const, 1)
                nc.gpsimd.memset(Rbd[:], 0.0).then_inc(sel_const, 1)
                for k in range(CANDS):
                    nc.gpsimd.memset(step[:, k:k + 1], (k + 1) << 27).then_inc(sel_const, 1)
                nc.gpsimd.memset(thr[:], 0).then_inc(sel_const, 1)
                for m in (blockones, blockbelow, spread, rmask):
                    nc.gpsimd.memset(m[:], 1.0).then_inc(sel_step, 1)
                nc.gpsimd.iota(iota_row[:], [[1, SA]], base=0, channel_multiplier=0).then_inc(sel_step, 1)
                pool.wait_ge(sel_step, 5)

                def keep_where(m, view, pattern, base, mult, n):
                    nc.gpsimd.affine_select(out=view, in_=view, compare_op=ALU.is_ge, fill=0.0, base=base, pattern=pattern,
                                            channel_multiplier=mult).then_inc(sel_step, 1)
                    pool.wait_ge(sel_step, n)

                n = 5
                for m in (blockones, blockbelow):
                    v3 = m[:].rearrange("p (e s) -> p e s", s=SEG)
                    n += 1
                    keep_where(m, v3, [[-SEG, E], [0, SEG]], 0, 1, n)
                    n += 1
                    keep_where(m, v3, [[SEG, E], [0, SEG]], SEG - 1, -1, n)
                n += 1
                keep_where(blockbelow, blockbelow[:], [[1, P]], -1, -1, n)
                v4 = spread[:].rearrange("p (a r) -> p a r", r=SR)
                sp1 = spread_one
                nc.gpsimd.memset(sp1[:], 0.0).then_inc(sel_step, 1)
                n += 1
                pool.wait_ge(sel_step, n)
                for q in range(4):
                    nc.gpsimd.affine_select(out=sp1[:], in_=sp1[:], compare_op=ALU.not_equal, fill=1.0, base=-SA * q,
                                            pattern=[[-1, SA]], channel_multiplier=1).then_inc(sel_step, 1)
                    n += 1
                    pool.wait_ge(sel_step, n)
                nc.gpsimd.tensor_copy(v4, sp1[:].unsqueeze(2).to_broadcast([P, SA, SR])).then_inc(sel_const, 1)
                nc.gpsimd.iota(pint[:], [[0, 1]], base=0, channel_multiplier=1).then_inc(sel_step, 1)
                nc.gpsimd.iota(tint[:], [[1, C], [C, SEG]], base=0, channel_multiplier=0).then_inc(sel_step, 1)
                n += 2
                pool.wait_ge(sel_step, n)
                nc.gpsimd.tensor_copy(pcol[:], pint[:]).then_inc(sel_const, 1)
                nc.gpsimd.tensor_copy(tilef[:], tint[:]).then_inc(sel_const, 1)
                nc.gpsimd.tensor_copy(iotaf[:], iota_row[:]).then_inc(sel_const, 1)

            def root(k, i):
                pool.wait_ge(var_ready[k], i + 1)
                settled(pool)
                nc.gpsimd.tensor_scalar(ve[k][:], mv[k][:, :, 1], LN_EPS, None, ALU.add).then_inc(ve_ready[k], 1)
                pool.wait_ge(ve_ready[k], i + 1)
                nc.gpsimd.tensor_tensor(rstd[k][:], ve[k][:], mhalf[:], ALU.pow).then_inc(rstd_ready[k], 1)

            def body(i, f):
                if f is not None:
                    root(1, f)
                if i is not None:
                    wait(pool, r_ready, i * 2)
                    pool.wait_ge(xn_ready, (i + 1) * TT)
                    nc.gpsimd.tensor_tensor(xnb[:], xn[:], bo_b[:].unsqueeze(1).to_broadcast([P, TT, D]), ALU.add).then_inc(xnb_ready, 1)
                if f is not None:
                    wait(pool, z_ready, f * 2)
                    pool.wait_ge(x2_ready, f + 1)
                    nc.gpsimd.tensor_tensor(x2b[:], x2[:], b2_b[:].unsqueeze(1).to_broadcast([P, TT, D]), ALU.add).then_inc(x2b_ready, 1)
                if i is not None:
                    pool.wait_ge(kmax_ready, i + 1)
                    settled(pool)
                    nc.gpsimd.partition_all_reduce(stabk[:], kmax[:], P, RMAX).then_inc(stab_ready, 1)
                    for t in range(TT):
                        pool.wait_ge(ke_ready, i * TT + t + 1)
                        settled(pool)
                        nc.gpsimd.tensor_scalar(kp[:, t, :], kp[:, t, :], EPS_K, None, ALU.add).then_inc(kp_ready, 1)
                if f is not None:
                    for k in (2, 3, 4):
                        root(k, f)
                if i is not None and not (isinstance(i, int) and i == B - 1):
                    root(0, i + 1)
                if f is not None:
                    root(5, f)

            pool.wait_ge(w_in, 16 * 7)
            pool.wait_ge(wff_in, 16 * 13)
            root(0, 0)
            selection_constants()
            batches(pool, body)
            if stop == "x1":
                return

            def gather(e):
                pool.wait_ge(idxg_ready, e + 1)
                settled(pool)
                for g in range(GT):
                    pool.indirect_dma_start(xg[:, g, :], None, row_d, bass.IndirectOffsetOnAxis(ap=idx_g[:, g:g + 1], axis=0)
                                            ).then_inc(gathered, 16)

            def scatter(e):
                wait(pool, scattered, e * 16 * GT)
                pool.wait_ge(idxs_ready, e + 1)
                for g in range(GT):
                    pool.wait_ge(og_ready, e * GT + g + 1)
                    settled(pool)
                    pool.indirect_dma_start(acc_d, bass.IndirectOffsetOnAxis(ap=idx_s[:, g:g + 1], axis=0), og[:, g, :], None,
                                            compute_op=ALU.add).then_inc(scattered, 16)

            for s in (xf_out, y_out, sc_out):
                pool.wait_ge(s, 16 * B)
            gather(0)

            def expert(e, more):
                if more:
                    gather(e + 1)
                scatter(e)

            experts(pool, expert)

            def last(j, k):
                pool.wait_ge(vl_ready, j + 1)
                settled(pool)
                nc.gpsimd.tensor_scalar(vel[:, k], mvl[:, k, :, 1], LN_EPS, None, ALU.add).then_inc(vel_ready, 1)
                pool.wait_ge(vel_ready, j + 1)
                nc.gpsimd.tensor_tensor(rsl[:, k], vel[:, k], mhalf[:], ALU.pow).then_inc(rl_ready, 1)

            with pool.Fori(0, B // 2) as j2:
                for k in range(2):
                    last(j2 * 2 + k, k)

        @block.vector
        def _(dve):
            dve.wait_ge(wproj_in, 16 * HG)
            nc.vector.tensor_scalar(projbd[:], projbd[:], NORM, None, ALU.mult).then_inc(proj_ready, 1)
            dve.wait_ge(w_in, 16 * 7)
            dve.wait_ge(wff_in, 16 * 13)
            dve.wait_ge(const_ready, N_CONST)

            def over_tiles(row):
                return row[:].unsqueeze(1).to_broadcast([P, TT, D])

            def stats(k, steps, src):
                for t in range(TT):
                    ins = nc.vector.bn_stats(st[k][:, t, :], src[:, t, :])
                steps.link(ins)
                settled(dve)
                for t in range(TT):
                    ins = nc.vector.bn_aggr(mv[k][:, t, :], st[k][:, t, :])
                ins.then_inc(var_ready[k], 1)

            def normed(k, i, dst, src):
                dve.wait_ge(rstd_ready[k], i + 1)
                for t in range(TT):
                    ins = nc.vector.tensor_scalar(dst[:, t, :], src[:, t, :], mv[k][:, t, 0:1], rstd[k][:, t:t + 1],
                                                  ALU.subtract, ALU.mult)
                return ins

            def ln1(i):
                steps = Steps(dve, dve_n, STEPS_N, i)
                dve.wait_ge(xin_in, (i + 1) * 16)
                stats(0, steps, xin)
                wait(dve, xnb_ready, i)
                dve.wait_ge(rstd_ready[0], i + 1)
                for t in range(TT):
                    nc.vector.tensor_scalar(xn[:, t, :], xin[:, t, :], mv[0][:, t, 0:1], rstd[0][:, t:t + 1],
                                            ALU.subtract, ALU.mult).then_inc(xn_ready, 1)
                steps.end()

            def k_max(i, t):
                dve.wait_ge(xk_ready, i * TT + t + 1)
                nc.vector.tensor_reduce(mxk[:, t, :], kp[:, t, :].rearrange("p (h m) -> p h m", m=M), AX_X,
                                        ALU.max).then_inc(kmx_ready, 1)

            def norms(i, m, dg):
                dve.wait_ge(sq_ready, i * 4 + m + 1)
                m2 = m % 2
                nc.vector.tensor_reduce(dg[:, 2 * m2:2 * m2 + 2, :], sq[:, m2].rearrange("p a (h d) -> p a h d", d=DH), AX_X,
                                        ALU.add).then_inc(dg_ready, 1)

            def k_shift(i, steps):
                dve.wait_ge(stab_ready, i + 1)
                steps.link(nc.vector.scalar_tensor_tensor(
                    out=kbias[:], in0=dgk[:], scalar=0.5 * NORM * NORM, in1=stabk[:].unsqueeze(1).to_broadcast([P, TT, H]),
                    op0=ALU.mult, op1=ALU.add))

            def k_sub(i, t):
                kt = kp[:, t, :].rearrange("p (h m) -> p h m", m=M)
                nc.vector.tensor_tensor(kt, kt, kbias[:, t, :].unsqueeze(2).to_broadcast([P, H, M]), ALU.subtract).then_inc(ks_ready, 1)

            def q_sub(i, t, steps):
                dve.wait_ge(x_ready, i * X_JOBS + J_XQ + t + 1)
                xq = pX[t % 2][:].rearrange("p a (h m) -> p (a h) m", m=M)
                steps.link(nc.vector.tensor_reduce(mxq[:, t, :], xq, AX_X, ALU.max))
                steps.link(nc.vector.scalar_tensor_tensor(out=qbias[:, t, :], in0=dgq[:, t, :], scalar=0.5 * NORM * NORM,
                                                          in1=mxq[:, t, :], op0=ALU.mult, op1=ALU.add))
                nc.vector.tensor_tensor(qe[:, t, :].rearrange("p (h m) -> p h m", m=M), xq,
                                        qbias[:, t, :].unsqueeze(2).to_broadcast([P, H, M]), ALU.subtract).then_inc(qs_ready, 1)

            def body(i, f):
                if f is not None:
                    sf = Steps(dve, dve_f, STEPS_F, f)
                    dve.wait_ge(r_ready, 2 * (f + 1))
                    stats(1, sf, r)
                    wait(dve, x2b_ready, f)
                    sf.link(normed(1, f, x2, r))
                    sf.link(nc.vector.tensor_tensor(x2[:], x2[:], over_tiles(g2_b), ALU.mult))
                    nc.vector.tensor_tensor(x2[:], x2[:], over_tiles(be2_b), ALU.add).then_inc(x2_ready, 1)
                if i is not None:
                    sa = Steps(dve, dve_a, STEPS_A, i)
                    for m in range(2):
                        dve.wait_ge(a_ready, i * A_JOBS + J_V + m + 1)
                        nc.vector.tensor_tensor(v[:, 2 * m:2 * m + 2, :], pA[m][:].rearrange("p (a b) -> p a b", a=2),
                                                bv_b[:].unsqueeze(1).to_broadcast([P, 2, D]), ALU.add).then_inc(v_ready, 1)
                    k_max(i, 0)
                    k_max(i, 1)
                    norms(i, 0, dgk)
                    norms(i, 1, dgk)
                    k_max(i, 2)
                    norms(i, 2, dgq)
                    norms(i, 3, dgq)
                    k_max(i, 3)
                    dve.wait_ge(kmx_ready, (i + 1) * TT)
                    nc.vector.tensor_reduce(kmax[:], mxk[:].rearrange("p t h -> p h t"), AX_X, ALU.max).then_inc(kmax_ready, 1)
                    dve.wait_ge(dg_ready, (i + 1) * 4)
                    k_shift(i, sa)
                    for t in range(TT):
                        k_sub(i, t)
                        q_sub(i, t, sa)

                def add_ff(m):
                    dve.wait_ge(f_ready, f * F_JOBS + J_Y + m + 1)
                    dve.wait_ge(x2b_ready, f + 1)
                    nc.vector.tensor_tensor(z[:, 2 * m:2 * m + 2, :], pF[m][:].rearrange("p (a b) -> p a b", a=2),
                                            x2b[:, 2 * m:2 * m + 2, :], ALU.add).then_inc(z_ready, 1)

                if f is not None:
                    add_ff(0)
                if i is not None:
                    for n in range(TT):
                        dve.wait_ge(x_ready, i * X_JOBS + J_TQ + n + 1)
                        nc.vector.tensor_scalar(qp[:, 2 * n + 1, :], pX[n % 2][:, 1, :], EPS_K, None, ALU.add).then_inc(qpv_ready, 1)
                    dve.wait_ge(a_ready, i * A_JOBS + J_CTXT + 1)
                    nc.vector.tensor_tensor(ctxbd[:], pA[0][:, 0:G * P].rearrange("p (a b) -> p a b", b=32),
                                            headmask[:].unsqueeze(1).to_broadcast([P, PAIRS, 32]), ALU.mult).then_inc(cx_ready, 1)
                    nc.vector.tensor_tensor(denbd[:], pA[0][:, G * P:512].rearrange("p (a b) -> p a b", b=32),
                                            denmask[:], ALU.mult).then_inc(cx_ready, 1)
                if f is not None:
                    add_ff(1)
                if i is not None:
                    for t in range(TT):
                        dve.wait_ge(a_ready, i * A_JOBS + J_OT + t + 1)
                        s = pA[(J_OT + t) % 2]
                        sa.link(nc.vector.reciprocal(
                            rden[:, t, :].rearrange("p (g r k) -> p g r k", g=G, k=2),
                            s[:, 2 * P:3 * P].rearrange("p (r c) -> p r c", c=32)[:, :, 0:4].rearrange("p r (g k) -> p g r k", k=2)))
                        nc.vector.tensor_tensor(at[:, t, :].rearrange("p (h d) -> p h d", d=DH),
                                                s[:, 0:2 * P].rearrange("p (h d) -> p h d", d=DH),
                                                rden[:, t, :].unsqueeze(2).to_broadcast([P, H, DH]), ALU.mult).then_inc(at_ready, 1)
                    dve.wait_ge(xnb_ready, i + 1)
                    for m in range(2):
                        dve.wait_ge(a_ready, i * A_JOBS + J_WO + m + 1)
                        nc.vector.tensor_tensor(r[:, 2 * m:2 * m + 2, :], pA[m][:].rearrange("p (a b) -> p a b", a=2),
                                                xnb[:, 2 * m:2 * m + 2, :], ALU.add).then_inc(r_ready, 1)
                    sa.end()
                if f is not None:
                    dve.wait_ge(z_ready, 2 * (f + 1))
                    stats(2, sf, z)
                    sf.link(normed(2, f, z, z))
                    sf.link(nc.vector.tensor_tensor(z[:], z[:], over_tiles(g3_b), ALU.mult))
                    sf.link(nc.vector.tensor_tensor(z[:], z[:], over_tiles(be3_b), ALU.add))
                    stats(3, sf, z)
                    sf.link(normed(3, f, z4, z))
                    dve.wait_ge(xres_in, 16 * (f + 1))
                    wait(dve, x1_out, 16 * f)
                    nc.vector.tensor_tensor(x1[:], z4[:], xres[:], ALU.add).then_inc(x1_ready, 1)
                    dve.wait_ge(x1_ready, f + 1)
                    stats(4, sf, x1)
                    wait(dve, xf_out, 16 * f)
                    normed(4, f, xf, x1).then_inc(xf_ready, 1)
                if i is not None and not (isinstance(i, int) and i == B - 1):
                    ln1(i + 1)
                if f is not None:
                    dve.wait_ge(xf_ready, f + 1)
                    stats(5, sf, xf)
                    wait(dve, y_out, 16 * f)
                    sf.link(normed(5, f, y, xf))
                    sf.link(nc.vector.tensor_tensor(y[:], y[:], over_tiles(lnw_b), ALU.mult))
                    nc.vector.tensor_tensor(y[:], y[:], over_tiles(lnb_b), ALU.add).then_inc(y_ready, 1)
                    for m in range(2):
                        dve.wait_ge(f_ready, f * F_JOBS + J_G + m + 1)
                        nc.vector.tensor_copy(lg[:, 2 * m:2 * m + 2, :],
                                              pF[m][:, 0:2 * P].rearrange("p (a b) -> p a b", a=2)[:, :, 0:E]).then_inc(lg_ready, 1)
                    dve.wait_ge(lg_ready, 2 * (f + 1))
                    sf.link(nc.vector.tensor_reduce(lmx[:], lg[:], AX_X, ALU.max))
                    nc.vector.tensor_tensor(lg[:], lg[:], lmx[:].unsqueeze(2).to_broadcast([P, TT, E]), ALU.subtract).then_inc(ls_ready, 1)
                    dve.wait_ge(le_ready, f + 1)
                    sf.link(nc.vector.tensor_reduce(lsum[:], lg[:], AX_X, ALU.add))
                    sf.link(nc.vector.reciprocal(lrec[:], lsum[:]))
                    wait(dve, sc_out, 16 * f)
                    lr = lrec[:].unsqueeze(2).to_broadcast([P, TT, E])
                    for c in range(C):
                        nc.vector.tensor_tensor(sc[:, c, :, bass.ts(f, 2)].rearrange("p e s -> p s e"),
                                                lg[:].rearrange("p (s c) e -> p c s e", c=C)[:, c],
                                                lrec[:].rearrange("p (s c) -> p c s", c=C)[:, c].unsqueeze(2).to_broadcast([P, 2, E]), ALU.mult)
                    nc.vector.tensor_tensor(sct[:], lg[:], lr, ALU.mult).then_inc(sc_ready, 1)
                    sf.end()

            ln1(0)
            batches(dve, body)
            if stop == "x1":
                return

            dve.wait_ge(sel_const, N_SEL)
            dve.wait_ge(s_turned, 1)
            nc.vector.tensor_copy(S, pA[0][:, 0:SEGW]).then_inc(s_ready, 1)
            dve.wait_ge(s_ready, 1)

            def search(rd):
                ss = Steps(dve, dve_s, SEL_STEPS, rd)
                ss.link(nc.vector.tensor_tensor(cand[:], step[:], thr[:].to_broadcast([P, CANDS]), ALU.bitwise_or))
                for k in range(CANDS):
                    nc.vector.tensor_scalar(flags[:, k], S, cand[:, k:k + 1].bitcast(F32), None, ALU.is_ge, ALU.add,
                                            accum_out=cnt[:, k:k + 1]).then_inc(cnt_ready, 1)
                dve.wait_ge(tot_ready, rd + 1)
                ss.link(nc.vector.tensor_scalar(passed[:], pA[1][:, 0:CANDS], KEEP - 0.5, None, ALU.is_ge, ALU.add,
                                                accum_out=npass[:]))
                ss.link(nc.vector.tensor_scalar(up[:], step[:, 0:1], npass[:, 0:1], None, ALU.mult))
                nc.vector.tensor_tensor(thr[:], thr[:], up[:], ALU.bitwise_or)
                ss.link(nc.vector.tensor_scalar(step[:], step[:], 3, None, ALU.logical_shift_right))
                ss.end()

            with dve.Fori(0, ROUNDS) as rd:
                search(rd)
            t0 = SEL_STEPS * ROUNDS
            done = Steps(dve, dve_s, 0, 0)
            done.n = t0
            cut = thr[:, 0:1].bitcast(F32)
            nc.vector.tensor_scalar(gt, S, cut, None, ALU.is_gt, ALU.add, accum_out=pair_cnt[:, 0:1])
            nc.vector.tensor_scalar(eq, S, cut, None, ALU.is_equal, ALU.add, accum_out=pair_cnt[:, 1:2]).then_inc(pair_ready, 1)
            dve.wait_ge(pair_ready, 1)
            nc.vector.tensor_tensor_scan(gin, ones_row[:], gt, 0.0, ALU.mult, ALU.add)
            nc.vector.tensor_tensor_scan(ein, ones_row[:], eq, 0.0, ALU.mult, ALU.add)
            dve.wait_ge(off_ready, 1)
            done.link(nc.vector.tensor_copy(offs[:], pA[0][:, 0:3]))
            done.link(nc.vector.tensor_tensor(eoff[:], offs[:, 1:2], offs[:, 2:3], ALU.add))
            done.link(nc.vector.tensor_scalar(ein, ein, eoff[:, 0:1], None, ALU.add))
            done.link(nc.vector.tensor_tensor(eq, eq, ein, ALU.mult))
            done.link(nc.vector.scalar_tensor_tensor(out=eq, in0=ein, scalar=KEEP + 0.5, in1=eq, op0=ALU.is_le, op1=ALU.mult))
            done.link(nc.vector.scalar_tensor_tensor(out=gin, in0=gin, scalar=offs[:, 0:1], in1=gt, op0=ALU.add, op1=ALU.mult))
            nc.vector.tensor_tensor(place, gin, eq, ALU.add).then_inc(place_ready, 1)
            dve.wait_ge(place_turned, 1)
            done.link(nc.vector.tensor_scalar(placei.rearrange("p c e s -> p (c e s)"), pA[1][:, 0:SEGW], 1.0, None, ALU.subtract))
            nc.vector.tensor_scalar(dig_a, placei, 4, None, ALU.arith_shift_right)
            done.link(nc.vector.tensor_scalar(dig_b, placei, SB - 1, None, ALU.bitwise_and))
            nc.vector.tensor_scalar(pmod[:], pint[:], SR - 1, None, ALU.bitwise_and)
            done.link(nc.vector.tensor_scalar(dig_b, dig_b, 0, None, ALU.add))
            done.link(nc.vector.tensor_copy(pmodf[:], pmod[:]))
            nc.vector.tensor_scalar(rmask[:], iotaf[:, 0:SR], pmodf[:, 0:1], None, ALU.is_equal)
            for c in range(C):
                for s0 in range(0, SEG, 4):
                    ss_ = slice(s0, s0 + 4)
                    nc.vector.tensor_tensor(oneA[:, c, ss_], dig_a[:, c, :, ss_].rearrange("p e s -> p s e").unsqueeze(3).to_broadcast([P, 4, E, SA]),
                                            iota_row[:].unsqueeze(1).unsqueeze(1).to_broadcast([P, 4, E, SA]), ALU.is_equal)
                    done.link(nc.vector.tensor_tensor(oneB[:, c, ss_, :, 0, :], dig_b[:, c, :, ss_].rearrange("p e s -> p s e").unsqueeze(3).to_broadcast([P, 4, E, SB]),
                                            iota_row[:, 0:SB].unsqueeze(1).unsqueeze(1).to_broadcast([P, 4, E, SB]), ALU.is_equal))
                    nc.vector.tensor_tensor(oneB[:, c, ss_, :, 1, :], oneB[:, c, ss_, :, 0, :],
                                            tilef[:, c, ss_].unsqueeze(2).unsqueeze(3).to_broadcast([P, 4, E, SB]), ALU.mult)
                    done.sync()
                    done.link(nc.vector.tensor_scalar(oneB[:, c, ss_, :, 0, :], oneB[:, c, ss_, :, 0, :], pcol[:, 0:1], None, ALU.mult))
                    nc.vector.tensor_scalar(zero4[:], zero4[:], 0.0, None, ALU.mult).then_inc(onehot_ready, 1)
            dve.wait_ge(ids_ready, 1)
            for k in range(2):
                for q in range(4):
                    ins = nc.vector.tensor_copy(Rbd[SA * q:SA * q + SA, k, q, :],
                                                pX[0][SA * q:SA * q + SA, k, 2 * SB * q:2 * SB * (q + 1)])
            ins.then_inc(rbd_ready, 1)
            dve.wait_ge(spread_ready, 1)
            done.link(nc.vector.tensor_tensor(idm[:], pX[1][:, 0, 0:E * 2 * SB].rearrange("p (x r g) -> p x r g", r=SR, g=GT),
                                              rmask[:].unsqueeze(1).unsqueeze(3).to_broadcast([P, E * 2, SR, GT]), ALU.mult))
            done.link(nc.vector.tensor_reduce(idf[:].rearrange("p e k g -> p (e k) g"), idm[:].rearrange("p x r g -> p x g r"), AX_X, ALU.add))
            nc.vector.scalar_tensor_tensor(out=idx[:], in0=idf[:, :, 1, :], scalar=float(P), in1=idf[:, :, 0, :], op0=ALU.mult,
                                           op1=ALU.add).then_inc(idx_ready, 1)
            dve.wait_ge(idx_ready, 1)

            def idx_for_gather(e):
                wait(dve, gathered, e * 16 * GT)
                nc.vector.tensor_tensor(idx_g[:], idx[:, bass.ds(e, 1), :].rearrange("p a g -> p (a g)"), zero4[:, 0:GT], ALU.add).then_inc(idxg_ready, 1)

            def next_weights(e):
                dve.wait_ge(gathered, (e + 1) * 16 * GT)
                wait(dve, wcur_ready, e)
                nc.vector.tensor_tensor(wnext[:], xg[:, :, bass.ds(e + D, 1)].rearrange("p g a -> p (g a)"), zero4[:, 0:GT], ALU.add).then_inc(wnext_ready, 1)

            def expert(e, more):
                if more:
                    dve.wait_ge(m_ready, e * M_JOBS + J_MX + 2)
                    idx_for_gather(e + 1)
                dve.wait_ge(wnext_ready, e + 1)
                wait(dve, og_ready, e * GT)
                nc.vector.tensor_copy(wcur[:], wnext[:]).then_inc(wcur_ready, 1)
                wait(dve, scattered, e * 16 * GT)
                nc.vector.tensor_tensor(idx_s[:], idx[:, bass.ds(e, 1), :].rearrange("p a g -> p (a g)"), zero4[:, 0:GT], ALU.add).then_inc(idxs_ready, 1)
                dve.wait_ge(b2e_in, 16 * (e + 1))
                dve.wait_ge(wcur_ready, e + 1)
                for m in range(2):
                    dve.wait_ge(m_ready, e * M_JOBS + J_MY + m + 1)
                    nc.vector.tensor_tensor(og[:, 2 * m:2 * m + 2, :], pM[(J_MY + m) % M_SLOTS].rearrange("p (a b) -> p a b", a=2),
                                            b2cur[:].unsqueeze(1).to_broadcast([P, 2, D]), ALU.add).then_inc(yo_ready, 1)
                    dve.wait_ge(yo_ready, e * 2 + m + 1)
                    for g in (2 * m, 2 * m + 1):
                        nc.vector.tensor_scalar(og[:, g, :], og[:, g, :], wcur[:, g:g + 1], None, ALU.mult).then_inc(og_ready, 1)
                    if m == 0 and more:
                        next_weights(e + 1)
                if more:
                    biases(e + 1)

            def biases(e):
                wait(dve, he_ready, e * FC)
                nc.vector.tensor_tensor(b1cur[:], b1e[:, bass.ds(e, 1), :].rearrange("p a n -> p (a n)"), zero4[:], ALU.add).then_inc(b1cur_ready, 1)

            dve.wait_ge(b1e_in, 16)
            idx_for_gather(0)
            biases(0)
            next_weights(0)
            experts(dve, expert)

            def last(j, k, j2):
                dve.wait_ge(acc_in[k], 16 * (j2 + 1))
                for t in range(TT):
                    ins = nc.vector.bn_stats(stl[:, k, t, :], acc_s[:, k, t, :])
                ins.then_inc(stl_ready, 1)
                dve.wait_ge(stl_ready, j + 1)
                settled(dve)
                for t in range(TT):
                    ins = nc.vector.bn_aggr(mvl[:, k, t, :], stl[:, k, t, :])
                ins.then_inc(vl_ready, 1)

            def last2(j, k, j2):
                dve.wait_ge(rl_ready, j + 1)
                for t in range(TT):
                    ins = nc.vector.tensor_scalar(acc_s[:, k, t, :], acc_s[:, k, t, :], mvl[:, k, t, 0:1], rsl[:, k, t:t + 1],
                                                  ALU.subtract, ALU.mult)
                ins.then_inc(nl_ready, 1)
                dve.wait_ge(nl_ready, j + 1)
                dve.wait_ge(x1_in[k], 16 * (j2 + 1))
                wait(dve, out_done[k], 16 * j2)
                nc.vector.tensor_tensor(o_s[:, k], acc_s[:, k], x1_s[:, k], ALU.add).then_inc(ol_ready, 1)

            def two_batches(j2):
                for k in range(2):
                    last(j2 * 2 + k, k, j2)
                for k in range(2):
                    last2(j2 * 2 + k, k, j2)

            two_batches(0)
            with dve.Fori(1, B // 2) as j2:
                two_batches(j2)

        @block.tensor
        def _(pe):
            a_taker = ([(xT_ready, 2, c) for c in range(2)] + [(kT_ready, 2, c) for c in range(2)] + [(qT_ready, 2, c) for c in range(2)]
                       + [(v_ready, 2, m) for m in range(2)] + [(sq_ready, 4, m) for m in range(4)] + [(cs_ready, 2, m) for m in range(2)]
                       + [(cx_ready, 2, 1)] + [(oT_ready, 3, m) for m in range(3)] + [(at_ready, 4, t) for t in range(4)]
                       + [(aT_ready, 2, c) for c in range(2)] + [(r_ready, 2, m) for m in range(2)])
            f_taker = ([(x2T_ready, 2, c) for c in range(2)] + [(h_ready, FC, n) for n in range(FC)] + [(z_ready, 2, m) for m in range(2)]
                       + [(xfT_ready, 2, c) for c in range(2)] + [(lg_ready, 2, m) for m in range(2)])
            assert len(a_taker) == A_JOBS and len(f_taker) == F_JOBS

            def slot(takers, jobs, i, n):
                if n < 2:
                    s, per, k = takers[jobs + n - 2]
                    wait(pe, s, (i - 1) * per + k + 1)
                else:
                    s, per, k = takers[n - 2]
                    wait(pe, s, i * per + k + 1)

            def slot_a(i, n):
                slot(a_taker, A_JOBS, i, n)
                return pA[n % 2]

            def slot_f(f, n):
                slot(f_taker, F_JOBS, f, n)
                return pF[n % 2]

            def slot_x(i, n):
                if n < 2:
                    wait(pe, qpa_ready, (i - 1) * TT + TT - 1 + n)
                    wait(pe, qpv_ready, (i - 1) * TT + TT - 1 + n)
                elif n < 6:
                    pe.wait_ge(xk_ready, i * TT + n - 1)
                elif n < 10:
                    pe.wait_ge(qs_ready, i * TT + n - 5)
                else:
                    pe.wait_ge(qpa_ready, i * TT + n - 9)
                    pe.wait_ge(qpv_ready, i * TT + n - 9)
                return pX[n % 2]

            def turn(dst, src):
                return nc.tensor.transpose(dst, src, ident[:])

            def tok(t):
                return slice(t * P, (t + 1) * P)

            def turn_tokens(dst, src, c):
                for t in range(TT):
                    ins = turn(dst[:, tok(t)], src[:, t, tok(c)])
                return ins

            def by_tokens(dst, xt, w, m, ks):
                for t2 in range(2):
                    for k in range(ks):
                        ins = nc.tensor.matmul(dst[:, t2 * D:(t2 + 1) * D], xt[:, k, tok(2 * m + t2)], w[:, k, :],
                                               start=(k == 0), stop=(k == ks - 1))
                return ins

            def by_features(dst, w, xt, n, ks):
                for k in range(ks):
                    ins = nc.tensor.matmul(dst[:], w[:, k, tok(n)], xt[:, k, :], start=(k == 0), stop=(k == ks - 1))
                return ins

            def features(i, n, src, t):
                s = slot_x(i, n)
                for g in range(G):
                    ins = nc.tensor.matmul(s[:, g, :], src[:, g, tok(t)], projbd[:], start=True, stop=True)
                ins.then_inc(x_ready, 1)

            def turn_heads(i, m, src):
                s = slot_a(i, J_DK + m)
                for t2 in range(2):
                    for g in range(G):
                        ins = turn(s[:, t2 * D + g * P:t2 * D + (g + 1) * P], src[:, g, tok(2 * (m % 2) + t2)])
                ins.then_inc(a_ready, 1)

            def hidden(f, n):
                s = slot_f(f, J_H + n)
                by_features(s, w1, x2T, n, C).then_inc(f_ready, 1)

            def ff_out(f, m):
                pe.wait_ge(h_ready, (f + 1) * FC)
                s = slot_f(f, J_Y + m)
                by_tokens(s, h, w2, m, FC).then_inc(f_ready, 1)

            def body(i, f):
                att, ff = i is not None, f is not None
                if att:
                    pe.wait_ge(xn_ready, (i + 1) * TT)
                    for c in range(C):
                        turn_tokens(slot_a(i, J_XT + c), xn, c).then_inc(a_ready, 1)
                    pe.wait_ge(xT_ready, (i + 1) * C)
                    for j0, w in ((J_K, wk), (J_Q, wq)):
                        for c in range(G):
                            by_features(slot_a(i, j0 + c), w, xT, c, C).then_inc(a_ready, 1)
                    for m in range(2):
                        by_tokens(slot_a(i, J_V + m), xT, wv, m, C).then_inc(a_ready, 1)
                    pe.wait_ge(kT_ready, (i + 1) * G)
                    features(i, J_XK, kT, 0)
                    features(i, J_XK + 1, kT, 1)
                    turn_heads(i, 0, kT)
                    turn_heads(i, 1, kT)
                    features(i, J_XK + 2, kT, 2)
                    pe.wait_ge(qT_ready, (i + 1) * G)
                    turn_heads(i, 2, qT)
                    turn_heads(i, 3, qT)
                    features(i, J_XK + 3, kT, 3)
                if ff:
                    pe.wait_ge(x2_ready, f + 1)
                    for c in range(C):
                        turn_tokens(slot_f(f, J_X2T + c), x2, c).then_inc(f_ready, 1)
                    pe.wait_ge(x2T_ready, (f + 1) * C)
                    hidden(f, 0)
                for t in range(TT):
                    if att:
                        features(i, J_XQ + t, qT, t)
                    if ff:
                        hidden(f, t + 1)
                if ff:
                    for n in range(TT + 1, FC):
                        hidden(f, n)
                if att:
                    pe.wait_ge(kp_ready, (i + 1) * TT)
                    pe.wait_ge(v_ready, (i + 1) * 2)
                    for j, lhs in ((J_CTX, v), (J_KSUM, None)):
                        s = slot_a(i, j)
                        for g in range(G):
                            for t in range(TT):
                                for q in range(4):
                                    pair = 4 * g + q
                                    ins = nc.tensor.matmul(
                                        s[32 * q:32 * q + 32, g * P:(g + 1) * P],
                                        ones32[:] if lhs is None else lhs[:, t, 32 * pair:32 * pair + 32],
                                        kp[:, t, P * pair:P * pair + P], start=(t == 0), stop=(t == TT - 1),
                                        tile_position=(0, 32 * q))
                        ins.then_inc(a_ready, 1)
                if ff:
                    ff_out(f, 0)
                if att:
                    pe.wait_ge(qe_ready, (i + 1) * TT)
                    for n in range(TT):
                        s = slot_x(i, J_TQ + n)
                        for k in range(2):
                            for t in range(TT):
                                ins = turn(s[:, k, tok(t)], qe[:, t, tok(2 * n + k)])
                        ins.then_inc(x_ready, 1)
                    pe.wait_ge(cs_ready, (i + 1) * 2)
                    s = slot_a(i, J_CTXT)
                    for n in range(2):
                        for g in range(G):
                            ins = turn(s[:, (2 * n + g) * P:(2 * n + g + 1) * P], cs[:, n, tok(g)])
                    ins.then_inc(a_ready, 1)
                if ff:
                    ff_out(f, 1)
                if att:
                    pe.wait_ge(cx_ready, (i + 1) * 2)
                    pe.wait_ge(qpa_ready, (i + 1) * TT)
                    pe.wait_ge(qpv_ready, (i + 1) * TT)
                    for g in range(G):
                        s = slot_a(i, J_OUT + g)
                        for q in range(4):
                            ins = nc.tensor.matmul(s[32 * q:32 * q + 32, :], ctxbd[:, 4 * g + q, :], qp[:, 4 * g + q, :],
                                                   start=True, stop=True, tile_position=(0, 32 * q))
                        ins.then_inc(a_ready, 1)
                    s = slot_a(i, J_OUT + 2)
                    for g in range(G):
                        for q in range(4):
                            ins = nc.tensor.matmul(s[32 * q:32 * q + 32, :], denbd[:, 4 * g + q, :], qp[:, 4 * g + q, :],
                                                   start=(g == 0), stop=(g == 1), tile_position=(0, 32 * q))
                    ins.then_inc(a_ready, 1)
                    pe.wait_ge(oT_ready, (i + 1) * 3)
                    for t in range(TT):
                        s = slot_a(i, J_OT + t)
                        for n in range(3):
                            ins = turn(s[:, tok(n)], oT[:, n, tok(t)])
                        ins.then_inc(a_ready, 1)
                    pe.wait_ge(at_ready, (i + 1) * TT)
                    for c in range(C):
                        turn_tokens(slot_a(i, J_AT + c), at, c).then_inc(a_ready, 1)
                    pe.wait_ge(aT_ready, (i + 1) * C)
                    for m in range(2):
                        by_tokens(slot_a(i, J_WO + m), aT, wo, m, C).then_inc(a_ready, 1)
                if ff:
                    pe.wait_ge(xf_ready, f + 1)
                    for c in range(C):
                        turn_tokens(slot_f(f, J_XFT + c), xf, c).then_inc(f_ready, 1)
                    pe.wait_ge(xfT_ready, (f + 1) * C)
                    for m in range(2):
                        s = slot_f(f, J_G + m)
                        for t2 in range(2):
                            for c in range(C):
                                ins = nc.tensor.matmul(s[:, tok(t2)], x2T[:, c, tok(2 * m + t2)], gate[:, c, :],
                                                       start=(c == 0), stop=(c == C - 1))
                        ins.then_inc(f_ready, 1)

            pe.wait_ge(const_ready, N_CONST)
            pe.wait_ge(proj_ready, 1)
            pe.wait_ge(w_in, 16 * 7)
            pe.wait_ge(wff_in, 16 * 13)
            batches(pe, body)
            if stop == "x1":
                return

            pe.wait_ge(sel_const, N_SEL)
            pe.wait_ge(sc_ready, B)
            pe.wait_ge(r_ready, 2 * B)
            for c in range(C):
                ins = turn(pA[0][:, tok(c)], sc[:, c].rearrange("p e s -> p (e s)"))
            ins.then_inc(s_turned, 1)

            with pe.Fori(0, ROUNDS) as rd:
                pe.wait_ge(cnt_ready, (rd + 1) * CANDS)
                nc.tensor.matmul(pA[1][:, 0:CANDS], blockones[:], cnt[:], start=True, stop=True).then_inc(tot_ready, 1)
            pe.wait_ge(pair_ready, 1)
            pe.wait_ge(s_ready, 1)
            nc.tensor.matmul(pA[0][:, 0:2], blockbelow[:], pair_cnt[:], start=True, stop=True)
            nc.tensor.matmul(pA[0][:, 2:3], blockones[:], pair_cnt[:, 0:1], start=True, stop=True).then_inc(off_ready, 1)
            pe.wait_ge(place_ready, 1)
            for c in range(C):
                ins = turn(pA[1][:, tok(c)], place[:, tok(c)])
            ins.then_inc(place_turned, 1)
            n = 0
            for c in range(C):
                for s0 in range(0, SEG, 4):
                    n += 1
                    pe.wait_ge(onehot_ready, n)
                    for s_ in range(s0, s0 + 4):
                        first, final = n == 1 and s_ == 0, c == C - 1 and s_ == SEG - 1
                        for k in range(2):
                            ins = nc.tensor.matmul(pX[0][:, k, 0:P], oneA[:, c, s_, 4 * k:4 * k + 4, :].rearrange("p e a -> p (e a)"),
                                                   oneB[:, c, s_, 4 * k:4 * k + 4].rearrange("p e k b -> p (e k b)"), start=first, stop=final)
            ins.then_inc(ids_ready, 1)
            pe.wait_ge(rbd_ready, 1)
            for k in range(2):
                ins = nc.tensor.matmul(pX[1][:, 0, tok(k)], spread[:], Rbd[:, k].rearrange("p q b -> p (q b)"), start=True, stop=True)
            ins.then_inc(spread_ready, 1)
            pe.wait_ge(idx_ready, 1)

            m_taker = ([(xgT_ready, 2, c) for c in range(2)] + [(he_ready, FC, n) for n in range(FC)] + [(yo_ready, 2, m) for m in range(2)])

            def slot_m(e, n):
                s, per, k = m_taker[(n - M_SLOTS) % M_JOBS]
                wait(pe, s, (e if n >= M_SLOTS else e - 1) * per + k + 1)
                return pM[n % M_SLOTS]

            def turn_rows(e):
                pe.wait_ge(gathered, (e + 1) * 16 * GT)
                for c in range(C):
                    turn_tokens(slot_m(e, J_MX + c), xg, c).then_inc(m_ready, 1)

            def expert(e, more):
                pe.wait_ge(w1e_in, 16 * (e + 1))
                pe.wait_ge(xgT_ready, (e + 1) * C)
                for n in range(FC):
                    by_features(slot_m(e, J_MH + n), w1e, xgT, n, C).then_inc(m_ready, 1)
                pe.wait_ge(w2e_in, 16 * (e + 1))
                pe.wait_ge(he_ready, (e + 1) * FC)
                for m in range(2):
                    by_tokens(slot_m(e, J_MY + m), h, w2e, m, FC).then_inc(m_ready, 1)
                if more:
                    turn_rows(e + 1)

            turn_rows(0)
            experts(pe, expert)


_COL = lambda a: a.reshape(-1, P).T
_LAYOUT = {
    "video": ("L0_attn_video", lambda a: a.reshape(T, D)),
    "WqT": ("L0_attn_Wq", lambda a: a.T), "bq": ("L0_attn_bq", _COL),
    "WkT": ("L0_attn_Wk", lambda a: a.T), "bk": ("L0_attn_bk", _COL),
    "WvT": ("L0_attn_Wv", lambda a: a.T), "bv": ("L0_attn_bv", None),
    "WoT": ("L0_attn_Wo", lambda a: a.T), "bo": ("L0_attn_bo", None),
    "projT": ("L0_attn_proj", lambda a: a.T),
    "W1T": ("L0_attn_W1", lambda a: a.T), "b1": ("L0_attn_b1", _COL),
    "W2T": ("L0_attn_W2", lambda a: a.T), "b2": ("L0_attn_b2", None),
    "g2": ("L0_attn_g2", None), "be2": ("L0_attn_be2", None),
    "g3": ("L0_attn_g3", None), "be3": ("L0_attn_be3", None),
    "gateT": ("L0_ffn_gate_w", lambda a: a.T),
    "ln_w": ("L0_ffn_ln_w", None), "ln_b": ("L0_ffn_ln_b", None),
    "fc1T": ("L0_ffn_fc1s", lambda a: a.transpose(0, 2, 1)),
    "b1s": ("L0_ffn_b1s", lambda a: a.reshape(E, FC, P).transpose(2, 0, 1)),
    "fc2T": ("L0_ffn_fc2s", lambda a: a.transpose(0, 2, 1)),
    "b2s": ("L0_ffn_b2s", None),
}


def kernel(**inputs):
    import concourse.bacc as bacc
    from concourse.bass_utils import run_bass_kernel_spmd

    nc = bacc.Bacc("TRN2", target_bir_lowering=False, num_devices=1)
    arrays, args = {}, []
    for name, (source, layout) in _LAYOUT.items():
        a = np.asarray(inputs[source])
        a = np.ascontiguousarray(layout(a) if layout else a)
        arrays[name] = a
        args.append(nc.dram_tensor(name, a.shape, mybir.dt.from_np(a.dtype), kind="ExternalInput").ap())
    out = nc.dram_tensor("out", (T, D), F32, kind="ExternalOutput").ap()
    build(nc, *args, out)
    res = run_bass_kernel_spmd(nc, [arrays], core_ids=[0])
    return res.results[0]["out"].reshape(B, N, D)
```

```python
from contextlib import ExitStack

import numpy as np
import concourse.bass as bass
from concourse import mybir

ALU = mybir.AluOpType
ACT = mybir.ActivationFunctionType
F32 = mybir.dt.float32
BF16 = mybir.dt.bfloat16
I32 = mybir.dt.int32
U32 = mybir.dt.uint32
AX_X = mybir.AxisListType.X
RMAX = bass.bass_isa.ReduceOp.max

P = 128
B, N, D = 8, 512, 256
T = B * N
TT = N // P
C = D // P
H, DH, M = 16, 16, 64
G = 2
HG = H // G
PAIRS = H // 2
FF = 1024
FC = FF // P
EPS_K = 1e-4
N_CONST = 12
N_W, N_WFF = 8, 12
N_SEL = 15
LN_EPS = 1e-5
LNS = 6
NORM = DH ** -0.25
E = 8
KEEP = T // E
SEG = P // E
SEGW = T // SEG
ROW = D + E
GT = KEEP // P

ROUNDS, CANDS = 10, 7
SA, SB = 32, 16
SR = P // SA
M_JOBS, M_SLOTS = 12, 4
J_MX, J_MH, J_MY = 0, 2, 10

A_JOBS, X_JOBS, F_JOBS, U_JOBS = 26, 12, 12, 4
(J_XT, J_K, J_Q, J_V, J_DK, J_DQ, J_CTX, J_KSUM, J_CTXT, J_OUT, J_OT, J_AT, J_WO) = (
    0, 2, 4, 6, 8, 10, 12, 13, 14, 15, 18, 22, 24)
J_XK, J_XQ, J_TQ = 0, 4, 8
J_X2T, J_H, J_Y = 0, 2, 10
J_XFT, J_G = 0, 2


def wait(eng, sem, value):
    if isinstance(value, int) and value <= 0:
        return
    eng.wait_ge(sem, value)


class Steps:

    def __init__(self, eng, sem, per, i):
        self.eng, self.sem, self.per, self.i, self.n = eng, sem, per, i, 0

    def put(self, ins):
        ins.then_inc(self.sem, 1)
        self.n += 1

    def sync(self):
        self.eng.wait_ge(self.sem, self.i * self.per + self.n)

    def link(self, ins):
        self.put(ins)
        self.sync()

    def end(self):
        assert self.n == self.per, (self.sem, self.n, self.per)


def build(nc, video, WqT, bq, WkT, bk, WvT, bv, WoT, bo, projT, W1T, b1, W2T, b2, g2, be2, g3, be3,
          gateT, ln_w, ln_b, fc1T, b1s, fc2T, b2s, out, stop=None):
    with ExitStack() as ctx:
        def sb(name, shape, dt=F32):
            return ctx.enter_context(nc.sbuf_tensor(name, shape, dt))

        def sem(name):
            return ctx.enter_context(nc.semaphore(name))

        pA = [ctx.enter_context(nc.psum_tensor(f"pA{s}", [P, 512], F32)) for s in range(2)]
        pX = [ctx.enter_context(nc.psum_tensor(f"pX{s}", [P, 2, 512], F32)) for s in range(2)]
        pF = [ctx.enter_context(nc.psum_tensor(f"pF{s}", [P, 512], F32)) for s in range(2)]

        pM = [pX[k // 2][:, k % 2, :] for k in range(4)]
        x1_d = nc.dram_tensor("x1_scratch", (T, D), F32, kind="Internal").ap()
        acc_d = nc.dram_tensor("acc_scratch", (T, D), F32, kind="Internal").ap()
        row_d = nc.dram_tensor("row_scratch", (T, ROW), F32, kind="Internal").ap()

        wq, wk, wv, wo = (sb(n, [P, C, D]) for n in ("wq", "wk", "wv", "wo"))
        w1 = sb("w1", [P, C, FF])
        w2 = sb("w2", [P, FC, D])
        gate = sb("gate", [P, C, P])
        projbd = sb("projbd", [P, HG * M])
        bqk = sb("bqk", [P, 2, G])
        b1c = sb("b1c", [P, FC])
        bv_b, bo_b, b2_b, g2_b, be2_b, g3_b, be3_b, lnw_b, lnb_b = (
            sb(n, [P, D]) for n in ("bv_b", "bo_b", "b2_b", "g2_b", "be2_b", "g3_b", "be3_b", "lnw_b", "lnb_b"))
        ident = sb("ident", [P, P])
        ones32 = sb("ones32", [P, 32])
        mhalf = sb("mhalf", [P, TT])
        epsk_c = sb("epsk_c", [P, 1])
        headmask = sb("headmask", [P, 32])
        denmask = sb("denmask", [P, PAIRS, 32])
        xin = sb("xin", [P, TT, D])
        xn = sb("xn", [P, TT, D])
        xnb = sb("xnb", [P, TT, D])
        xT = sb("xT", [P, C, N])
        kT = sb("kT", [P, G, N])
        qT = sb("qT", [P, G, N])
        v = sb("v", [P, TT, D])
        sq = sb("sq", [P, 2, 2, D])
        dgk = sb("dgk", [P, TT, H])
        dgq = sb("dgq", [P, TT, H])
        mxk = sb("mxk", [P, TT, H])
        mxq = sb("mxq", [P, TT, H])
        kmax = sb("kmax", [P, H])
        stabk = sb("stabk", [P, H])
        kbias = sb("kbias", [P, TT, H])
        qbias = sb("qbias", [P, TT, H])
        kp = sb("kp", [P, TT, H * M])
        qe = sb("qe", [P, TT, H * M])
        qp = sb("qp", [P, PAIRS, N])
        cs = sb("cs", [P, 2, G * P])
        ctxbd = sb("ctxbd", [P, PAIRS, 32])
        denbd = sb("denbd", [P, PAIRS, 32])
        oT = sb("oT", [P, 3, N])
        rden = sb("rden", [P, TT, H])
        at = sb("at", [P, TT, D])
        aT = sb("aT", [P, C, N])
        r = sb("r", [P, TT, D])
        x2 = sb("x2", [P, TT, D])
        x2b = sb("x2b", [P, TT, D])
        x2T = sb("x2T", [P, C, N])
        h = sb("h", [P, FC, N])
        z = sb("z", [P, TT, D])
        z4 = sb("z4", [P, TT, D])
        xres = sb("xres", [P, TT, D])
        x1 = sb("x1", [P, TT, D])
        xf = sb("xf", [P, TT, D])
        y = sb("y", [P, TT, D])
        xfT = x2T
        lg = sb("lg", [P, TT, E])
        lmx = sb("lmx", [P, TT])
        lsum = sb("lsum", [P, TT])
        lrec = sb("lrec", [P, TT])
        sct = sb("sct", [P, TT, E])
        sc = sb("sc", [P, C, E, SEG])
        st = [sb(f"st{k}", [P, TT, 6]) for k in range(LNS)]
        mv = [sb(f"mv{k}", [P, TT, 2]) for k in range(LNS)]
        ve = [sb(f"ve{k}", [P, TT]) for k in range(LNS)]
        rstd = [sb(f"rstd{k}", [P, TT]) for k in range(LNS)]

        kp_f, qe_f, qp_f = (a[:].rearrange("p a b -> p (a b)") for a in (kp, qe, qp))
        S, gt, eq, gin, ein, place = (kp_f[:, k * SEGW:(k + 1) * SEGW] for k in range(6))
        flags = kp_f[:, 8 * SEGW:(8 + CANDS) * SEGW].rearrange("p (k j) -> p k j", k=CANDS)
        placei, dig_a, dig_b = (kp_f[:, k * SEGW:(k + 1) * SEGW].bitcast(I32).rearrange("p (c e s) -> p c e s", c=C, e=E) for k in (8, 9, 10))
        thr = sb("thr", [P, 1], U32)
        step = sb("step", [P, CANDS], U32)
        cand = sb("cand", [P, CANDS], U32)
        cnt = sb("cnt", [P, CANDS])
        passed = sb("passed", [P, CANDS])
        npass = sb("npass", [P, 1])
        up = sb("up", [P, 1], U32)
        ones_row = sb("ones_row", [P, SEGW])
        blockones = sb("blockones", [P, P])
        blockbelow = sb("blockbelow", [P, P])
        pair_cnt = sb("pair_cnt", [P, 2])
        offs = sb("offs", [P, 3])
        eoff = sb("eoff", [P, 1])
        iota_row = sb("iota_row", [P, SA], I32)
        iotaf = sb("iotaf", [P, SA])
        tilef = sb("tilef", [P, C, SEG])
        pcol = sb("pcol", [P, 1])
        oneA = qp_f.bitcast(BF16).rearrange("p (c s e a) -> p c s e a", c=C, s=SEG, e=E)
        oneB = qe_f.bitcast(BF16).rearrange("p (c s e k b) -> p c s e k b", c=C, s=SEG, e=E, k=2)
        spread = sb("spread", [P, P], BF16)
        rmask = sb("rmask", [P, SR])
        pmod = sb("pmod", [P, 1], I32)
        pmodf = sb("pmodf", [P, 1])
        spread_one = sb("spread_one", [P, SA])
        pint = sb("pint", [P, 1], I32)
        tint = sb("tint", [P, C, SEG], I32)
        Rbd = sb("Rbd", [P, 2, 4, 2 * SB], BF16)
        idm = sb("idm", [P, E * 2, SR, GT])
        idf = sb("idf", [P, E, 2, GT])
        idx = sb("idx", [P, E, GT])
        w1e, w2e, xgT, og = w1, w2, kT, at
        b1e = sb("b1e", [P, E, FC])
        b1cur = sb("b1cur", [P, FC])
        b2cur = sb("b2cur", [P, D])
        xg = sb("xg", [P, GT, ROW])
        idx_g = sb("idx_g", [P, GT], U32)
        idx_s = sb("idx_s", [P, GT], U32)
        wnext = sb("wnext", [P, GT])
        wcur = sb("wcur", [P, GT])
        zero4 = sb("zero4", [P, FC])
        acc_s, x1_s, o_s = (a.rearrange("p (k t d) -> p k t d", k=2, t=TT) for a in (qp_f[:, 0:2 * TT * D], qp_f[:, 2 * TT * D:], qe_f[:, 0:2 * TT * D]))
        stl = sb("stl", [P, 2, TT, 6])
        mvl = sb("mvl", [P, 2, TT, 2])
        vel = sb("vel", [P, 2, TT])
        rsl = sb("rsl", [P, 2, TT])


        w_in = sem("w_in")
        wff_in = sem("wff_in")
        wproj_in = sem("wproj_in")
        const_step, const_ready, proj_ready = sem("const_step"), sem("const_ready"), sem("proj_ready")
        a_ready, x_ready, f_ready, u_ready = sem("a_ready"), sem("x_ready"), sem("f_ready"), sem("u_ready")
        var_ready = [sem(f"var_ready{k}") for k in range(LNS)]
        ve_ready = [sem(f"ve_ready{k}") for k in range(LNS)]
        rstd_ready = [sem(f"rstd_ready{k}") for k in range(LNS)]
        xin_in, xres_in = sem("xin_in"), sem("xres_in")
        xn_ready, xnb_ready = sem("xn_ready"), sem("xnb_ready")
        xT_ready, kT_ready, qT_ready, v_ready = sem("xT_ready"), sem("kT_ready"), sem("qT_ready"), sem("v_ready")
        sq_ready, dg_ready = sem("sq_ready"), sem("dg_ready")
        xk_ready, kmx_ready, kmax_ready, stab_ready = sem("xk_ready"), sem("kmx_ready"), sem("kmax_ready"), sem("stab_ready")
        ks_ready, ke_ready, kp_ready = sem("ks_ready"), sem("ke_ready"), sem("kp_ready")
        qs_ready, qe_ready, qpa_ready, qpv_ready = sem("qs_ready"), sem("qe_ready"), sem("qpa_ready"), sem("qpv_ready")
        cs_ready, cx_ready, oT_ready = sem("cs_ready"), sem("cx_ready"), sem("oT_ready")
        at_ready, aT_ready, r_ready = sem("at_ready"), sem("aT_ready"), sem("r_ready")
        x2_ready, x2b_ready, x2T_ready, h_ready = sem("x2_ready"), sem("x2b_ready"), sem("x2T_ready"), sem("h_ready")
        zn_ready, zs_ready, za_ready, yn_ready, ys_ready = (
            sem("zn_ready"), sem("zs_ready"), sem("za_ready"), sem("yn_ready"), sem("ys_ready"))
        z_ready, x1_ready, xf_ready, y_ready = sem("z_ready"), sem("x1_ready"), sem("xf_ready"), sem("y_ready")
        xfT_ready, lg_ready = sem("xfT_ready"), sem("lg_ready")
        ls_ready, le_ready, sc_ready = sem("ls_ready"), sem("le_ready"), sem("sc_ready")
        x1_out, xf_out, y_out, sc_out = sem("x1_out"), sem("xf_out"), sem("y_out"), sem("sc_out")
        dve_n, dve_a, dve_f, dve_u = sem("dve_n"), sem("dve_a"), sem("dve_f"), sem("dve_u")
        sel_const, sel_step, s_turned, s_ready = sem("sel_const"), sem("sel_step"), sem("s_turned"), sem("s_ready")
        cnt_ready, tot_ready, dve_s = sem("cnt_ready"), sem("tot_ready"), sem("dve_s")
        pair_ready, off_ready, place_ready, place_turned = sem("pair_ready"), sem("off_ready"), sem("place_ready"), sem("place_turned")
        onehot_ready, ids_ready, rbd_ready, spread_ready, idx_ready = (
            sem("onehot_ready"), sem("ids_ready"), sem("rbd_ready"), sem("spread_ready"), sem("idx_ready"))
        m_ready, xgT_ready, he_ready, yo_ready = sem("m_ready"), sem("xgT_ready"), sem("he_ready"), sem("yo_ready")
        w1e_in, w2e_in, b1e_in, b2e_in = sem("w1e_in"), sem("w2e_in"), sem("b1e_in"), sem("b2e_in")
        idxg_ready, idxs_ready, b1cur_ready, wnext_ready, wcur_ready = (
            sem("idxg_ready"), sem("idxs_ready"), sem("b1cur_ready"), sem("wnext_ready"), sem("wcur_ready"))
        gathered, scattered, og_ready = sem("gathered"), sem("scattered"), sem("og_ready")
        acc_in = [sem(f"acc_in{k}") for k in range(2)]
        x1_in = [sem(f"x1_in{k}") for k in range(2)]
        out_done = [sem(f"out_done{k}") for k in range(2)]
        stl_ready, vl_ready, vel_ready, rl_ready, nl_ready, ol_ready = (
            sem("stl_ready"), sem("vl_ready"), sem("vel_ready"), sem("rl_ready"), sem("nl_ready"), sem("ol_ready"))
        STEPS_N, STEPS_A, STEPS_F, STEPS_U = 1, 13, 3, 8
        SEL_STEPS = 4

        vid_d = video.rearrange("(b t p) d -> b p t d", t=TT, p=P)
        x1_t = x1_d.rearrange("(b t p) d -> b p t d", t=TT, p=P)
        acc_t = acc_d.rearrange("(b t p) d -> b p t d", t=TT, p=P)
        row_t = row_d.rearrange("(b t p) r -> b p t r", t=TT, p=P)

        def batches(eng, body):
            body(0, None, None)
            body(1, 0, None)
            body(2, 1, 0)
            with eng.Fori(3, B - 1) as i:
                body(i, i - 1, i - 2)
            body(B - 1, B - 2, B - 3)
            body(None, B - 1, B - 2)
            body(None, None, B - 1)

        def at_first(f, pe_like):
            if isinstance(f, int) and f == 0:
                pe_like.wait_ge(wff_in, 16 * N_WFF)

        out_t = out.rearrange("(b t p) d -> b p t d", t=TT, p=P)

        def experts(eng, body):
            body(0, True)
            with eng.Fori(1, E - 1) as e:
                body(e, True)
            body(E - 1, False)

        waits_met = sem("waits_met")

        def settled(eng):
            eng.sem_inc(waits_met, 1)

        block = ctx.enter_context(nc.Block())

        @block.sync
        def _(sp):
            def load_x(i):
                wait(sp, xn_ready, i * TT)
                sp.dma_start(xin[:], vid_d[i]).then_inc(xin_in, 16)

            def body(i, f, u):
                if i is not None and not (isinstance(i, int) and i == B - 1):
                    load_x(i + 1)
                if u is not None:
                    wait(sp, x1_ready, u)
                    sp.dma_start(xres[:], vid_d[u]).then_inc(xres_in, 16)
                    for ready, done, dst, src in ((x1_ready, x1_out, x1_t[u], x1[:]), (xf_ready, xf_out, acc_t[u], xf[:]),
                                                  (y_ready, y_out, row_t[u][:, :, 0:D], y[:]),
                                                  (sc_ready, sc_out, row_t[u][:, :, D:ROW], sct[:])):
                        sp.wait_ge(ready, u + 1)
                        sp.dma_start(dst, src).then_inc(done, 16)

            load_x(0)
            for w, src in ((wk, WkT), (wq, WqT), (wv, WvT), (wo, WoT)):
                sp.dma_start(w[:], src.rearrange("(c p) n -> p c n", p=P)).then_inc(w_in, 16)
            for w, src in ((w1, W1T), (w2, W2T)):
                sp.dma_start(w[:], src.rearrange("(c p) n -> p c n", p=P)).then_inc(wff_in, 16)
            batches(sp, body)
            if stop != "x1":
                sp.dma_start(b1e[:], b1s).then_inc(b1e_in, 16)

                def load_expert(e):
                    wait(sp, m_ready, (e - 1) * M_JOBS + J_MY)
                    sp.dma_start(w1e[:], fc1T[e].rearrange("(c p) n -> p c n", p=P)).then_inc(w1e_in, 16)
                    wait(sp, m_ready, e * M_JOBS)
                    sp.dma_start(w2e[:], fc2T[e].rearrange("(c p) n -> p c n", p=P)).then_inc(w2e_in, 16)
                    wait(sp, yo_ready, e * 2)
                    sp.dma_start(b2cur[:], b2s[e].partition_broadcast(P)).then_inc(b2e_in, 16)

                sp.wait_ge(f_ready, (B - 1) * F_JOBS + J_Y + 2)
                load_expert(0)
                with sp.Fori(1, E) as e:
                    load_expert(e)

                for s in (x1_out, xf_out, y_out, sc_out):
                    sp.wait_ge(s, 16 * B)
                sp.wait_ge(scattered, 16 * GT * E)

                def last(j, k, q):
                    wait(sp, ol_ready, j - 1)
                    sp.dma_start(acc_s[:, k], acc_t[j]).then_inc(acc_in[k], 16)
                    sp.dma_start(x1_s[:, k], x1_t[j]).then_inc(x1_in[k], 16)

                def put(j, k):
                    sp.wait_ge(ol_ready, j + 1)
                    sp.dma_start(out_t[j], o_s[:, k]).then_inc(out_done[k], 16)

                last(0, 0, 0)
                last(1, 1, 0)
                with sp.Fori(0, B // 2 - 1) as j2:
                    for k in range(2):
                        put(j2 * 2 + k, k)
                        last(j2 * 2 + k + 2, k, 0)
                for k in range(2):
                    put(B - 2 + k, k)
                for k in range(2):
                    sp.wait_ge(out_done[k], 16 * (B // 2))
            if stop == "x1":
                for s in (x1_out, xf_out, y_out, sc_out):
                    sp.wait_ge(s, 16 * B)
                sp.dma_start(out, {"x1": x1_d}[stop]).then_inc(x1_out, 16)
                sp.wait_ge(x1_out, 16 * B + 16)

        @block.scalar
        def _(act):
            act.dma_start(bqk[:, 0, :], bq).then_inc(w_in, 16)
            act.dma_start(bqk[:, 1, :], bk).then_inc(w_in, 16)
            act.wait_ge(const_ready, 2)
            for g in range(HG):
                act.dma_start(projbd[DH * g:DH * g + DH, M * g:M * g + M], projT).then_inc(wproj_in, 16)
            act.dma_start(bv_b[:], bv.partition_broadcast(P)).then_inc(w_in, 16)
            act.dma_start(bo_b[:], bo.partition_broadcast(P)).then_inc(w_in, 16)
            for c in range(C):
                act.dma_start(gate[:, c, 0:E], gateT[c * P:(c + 1) * P, :]).then_inc(wff_in, 16)
            act.dma_start(b1c[:], b1).then_inc(wff_in, 16)
            for dst, src in ((b2_b, b2), (g2_b, g2), (be2_b, be2), (g3_b, g3), (be3_b, be3), (lnw_b, ln_w), (lnb_b, ln_b)):
                act.dma_start(dst[:], src.partition_broadcast(P)).then_inc(wff_in, 16)

            def take_a(i, n, dst, func, done, **kw):
                act.wait_ge(a_ready, i * A_JOBS + n + 1)
                nc.scalar.activation(dst, pA[n % 2][:], func, **kw).then_inc(done, 1)

            def take_f(f, n, dst, func, done, **kw):
                act.wait_ge(f_ready, f * F_JOBS + n + 1)
                nc.scalar.activation(dst, pF[n % 2][:], func, **kw).then_inc(done, 1)

            def xk_copy(i, t):
                act.wait_ge(x_ready, i * X_JOBS + J_XK + t + 1)
                nc.scalar.activation(kp[:, t, :], pX[t % 2][:].rearrange("p a b -> p (a b)"), ACT.Copy).then_inc(xk_ready, 1)

            def squares(i, m):
                wait(act, dg_ready, i * 4 + m - 1)
                take_a(i, J_DK + m, sq[:, m % 2].rearrange("p a b -> p (a b)"), ACT.Square, sq_ready)

            def take_u(u, n, k, dst, done):
                act.wait_ge(u_ready, u * U_JOBS + n + 1)
                nc.scalar.activation(dst, pF[k][:], ACT.Copy).then_inc(done, 1)

            def relu(f, n):
                take_f(f, J_H + n, h[:, n, :], ACT.Relu, h_ready, bias=b1c[:, n:n + 1])

            def exps(i, t):
                act.wait_ge(ks_ready, i * TT + t + 1)
                nc.scalar.activation(kp[:, t, :], kp[:, t, :], ACT.Exp).then_inc(ke_ready, 1)
                act.wait_ge(qs_ready, i * TT + t + 1)
                nc.scalar.activation(qe[:, t, :], qe[:, t, :], ACT.Exp).then_inc(qe_ready, 1)

            def body(i, f, u):
                at_first(f, act)
                if i is not None:
                    for c in range(C):
                        take_a(i, J_XT + c, xT[:, c, :], ACT.Copy, xT_ready)
                    for c in range(G):
                        take_a(i, J_K + c, kT[:, c, :], ACT.Identity, kT_ready, bias=bqk[:, 1, c:c + 1])
                    for c in range(G):
                        take_a(i, J_Q + c, qT[:, c, :], ACT.Identity, qT_ready, bias=bqk[:, 0, c:c + 1])
                    xk_copy(i, 0)
                    xk_copy(i, 1)
                    squares(i, 0)
                    squares(i, 1)
                    xk_copy(i, 2)
                    squares(i, 2)
                    squares(i, 3)
                    xk_copy(i, 3)
                if f is not None:
                    for c in range(C):
                        take_f(f, J_X2T + c, x2T[:, c, :], ACT.Copy, x2T_ready)
                    relu(f, 0)
                for t in range(TT):
                    if i is not None:
                        exps(i, t)
                    if f is not None:
                        relu(f, t + 1)
                if f is not None:
                    for n in range(TT + 1, FC):
                        relu(f, n)
                if i is not None:
                    for n in range(2):
                        act.wait_ge(a_ready, i * A_JOBS + J_CTX + n + 1)
                        nc.scalar.activation(cs[:, n, :], pA[n][:, 0:G * P], ACT.Copy).then_inc(cs_ready, 1)
                    for n in range(TT):
                        act.wait_ge(x_ready, i * X_JOBS + J_TQ + n + 1)
                        nc.scalar.activation(qp[:, 2 * n, :], pX[n % 2][:, 0, :], ACT.Identity, bias=epsk_c[:, 0:1]).then_inc(qpa_ready, 1)
                    for n in range(3):
                        take_a(i, J_OUT + n, oT[:, n, :], ACT.Copy, oT_ready)
                if u is not None:
                    take_u(u, J_XFT, 1, x2T[:, 0, :], xfT_ready)
                    take_u(u, J_XFT + 1, 0, x2T[:, 1, :], xfT_ready)
                if i is not None:
                    for c in range(C):
                        take_a(i, J_AT + c, aT[:, c, :], ACT.Copy, aT_ready)
                if u is not None:
                    act.wait_ge(ls_ready, u + 1)
                    nc.scalar.activation(lg[:], lg[:], ACT.Exp).then_inc(le_ready, 1)

            act.wait_ge(w_in, 16 * N_W)
            act.wait_ge(const_ready, N_CONST)
            batches(act, body)
            if stop == "x1":
                return

            def take_m(e, n, dst, func, done, **kw):
                act.wait_ge(m_ready, e * M_JOBS + n + 1)
                nc.scalar.activation(dst, pM[n % M_SLOTS], func, **kw).then_inc(done, 1)

            def turned(e):
                for c in range(C):
                    take_m(e, J_MX + c, xgT[:, c, :], ACT.Copy, xgT_ready)

            def expert(e, more):
                act.wait_ge(b1cur_ready, e + 1)
                for n in range(FC):
                    take_m(e, J_MH + n, h[:, n, :], ACT.Gelu_apprx_tanh, he_ready, bias=b1cur[:, n:n + 1])
                if more:
                    turned(e + 1)

            turned(0)
            experts(act, expert)

        @block.gpsimd
        def _(pool):
            nc.gpsimd.memset(projbd[:], 0.0).then_inc(const_ready, 1)
            nc.gpsimd.memset(gate[:], 0.0).then_inc(const_ready, 1)
            nc.gpsimd.memset(ident[:], 0.0).then_inc(const_step, 1)
            pool.wait_ge(const_step, 1)
            nc.gpsimd.affine_select(out=ident[:], in_=ident[:], compare_op=ALU.not_equal, fill=1.0, base=0,
                                    pattern=[[-1, P]], channel_multiplier=1).then_inc(const_ready, 1)
            nc.gpsimd.memset(ones32[:], 1.0).then_inc(const_ready, 1)
            nc.gpsimd.memset(mhalf[:], -0.5).then_inc(const_ready, 1)
            nc.gpsimd.memset(epsk_c[:], EPS_K).then_inc(const_ready, 1)
            nc.gpsimd.memset(headmask[:], 0.0).then_inc(const_step, 1)
            nc.gpsimd.memset(denmask[:], 0.0).then_inc(const_step, 1)
            pool.wait_ge(const_step, 3)
            for k in range(2):
                rows = slice(M * k, M * k + M)
                nc.gpsimd.memset(headmask[rows, DH * k:DH * k + DH], 1.0).then_inc(const_ready, 1)
                for g in range(G):
                    nc.gpsimd.memset(denmask[rows, 4 * g:4 * g + 4, 2 * g + k:2 * g + k + 1], 1.0).then_inc(const_ready, 1)

            def selection_constants():
                nc.gpsimd.memset(ones_row[:], 1.0).then_inc(sel_const, 1)
                nc.gpsimd.memset(zero4[:], 0.0).then_inc(sel_const, 1)
                nc.gpsimd.memset(Rbd[:], 0.0).then_inc(sel_const, 1)
                for k in range(CANDS):
                    nc.gpsimd.memset(step[:, k:k + 1], (k + 1) << 27).then_inc(sel_const, 1)
                nc.gpsimd.memset(thr[:], 0).then_inc(sel_const, 1)
                for m in (blockones, blockbelow, spread, rmask):
                    nc.gpsimd.memset(m[:], 1.0).then_inc(sel_step, 1)
                nc.gpsimd.iota(iota_row[:], [[1, SA]], base=0, channel_multiplier=0).then_inc(sel_step, 1)
                pool.wait_ge(sel_step, 5)

                def keep_where(m, view, pattern, base, mult, n):
                    nc.gpsimd.affine_select(out=view, in_=view, compare_op=ALU.is_ge, fill=0.0, base=base, pattern=pattern,
                                            channel_multiplier=mult).then_inc(sel_step, 1)
                    pool.wait_ge(sel_step, n)

                n = 5
                for m in (blockones, blockbelow):
                    v3 = m[:].rearrange("p (e s) -> p e s", s=SEG)
                    n += 1
                    keep_where(m, v3, [[-SEG, E], [0, SEG]], 0, 1, n)
                    n += 1
                    keep_where(m, v3, [[SEG, E], [0, SEG]], SEG - 1, -1, n)
                n += 1
                keep_where(blockbelow, blockbelow[:], [[1, P]], -1, -1, n)
                v4 = spread[:].rearrange("p (a r) -> p a r", r=SR)
                sp1 = spread_one
                nc.gpsimd.memset(sp1[:], 0.0).then_inc(sel_step, 1)
                n += 1
                pool.wait_ge(sel_step, n)
                for q in range(4):
                    nc.gpsimd.affine_select(out=sp1[:], in_=sp1[:], compare_op=ALU.not_equal, fill=1.0, base=-SA * q,
                                            pattern=[[-1, SA]], channel_multiplier=1).then_inc(sel_step, 1)
                    n += 1
                    pool.wait_ge(sel_step, n)
                nc.gpsimd.tensor_copy(v4, sp1[:].unsqueeze(2).to_broadcast([P, SA, SR])).then_inc(sel_const, 1)
                nc.gpsimd.iota(pint[:], [[0, 1]], base=0, channel_multiplier=1).then_inc(sel_step, 1)
                nc.gpsimd.iota(tint[:], [[1, C], [C, SEG]], base=0, channel_multiplier=0).then_inc(sel_step, 1)
                n += 2
                pool.wait_ge(sel_step, n)
                nc.gpsimd.tensor_copy(pcol[:], pint[:]).then_inc(sel_const, 1)
                nc.gpsimd.tensor_copy(tilef[:], tint[:]).then_inc(sel_const, 1)
                nc.gpsimd.tensor_copy(iotaf[:], iota_row[:]).then_inc(sel_const, 1)

            def root(k, i):
                pool.wait_ge(var_ready[k], i + 1)
                settled(pool)
                nc.gpsimd.tensor_scalar(ve[k][:], mv[k][:, :, 1], LN_EPS, None, ALU.add).then_inc(ve_ready[k], 1)
                pool.wait_ge(ve_ready[k], i + 1)
                nc.gpsimd.tensor_tensor(rstd[k][:], ve[k][:], mhalf[:], ALU.pow).then_inc(rstd_ready[k], 1)

            def affine(u, buf, normed_ready, scaled, done, w_, b_):
                pool.wait_ge(normed_ready, u + 1)
                nc.gpsimd.tensor_tensor(buf[:], buf[:], w_[:].unsqueeze(1).to_broadcast([P, TT, D]), ALU.mult).then_inc(scaled, 1)
                pool.wait_ge(scaled, u + 1)
                nc.gpsimd.tensor_tensor(buf[:], buf[:], b_[:].unsqueeze(1).to_broadcast([P, TT, D]), ALU.add).then_inc(done, 1)

            def body(i, f, u):
                at_first(f, pool)
                if f is not None:
                    root(1, f)
                if u is not None:
                    root(2, u)
                if i is not None:
                    wait(pool, r_ready, i * 2)
                    pool.wait_ge(xn_ready, (i + 1) * TT)
                    nc.gpsimd.tensor_tensor(xnb[:], xn[:], bo_b[:].unsqueeze(1).to_broadcast([P, TT, D]), ALU.add).then_inc(xnb_ready, 1)
                if u is not None:
                    affine(u, z, zn_ready, zs_ready, za_ready, g3_b, be3_b)
                if i is not None:
                    pool.wait_ge(kmax_ready, i + 1)
                    settled(pool)
                    nc.gpsimd.partition_all_reduce(stabk[:], kmax[:], P, RMAX).then_inc(stab_ready, 1)
                if u is not None:
                    root(3, u)
                if f is not None:
                    wait(pool, z_ready, f * 2)
                    pool.wait_ge(x2_ready, f + 1)
                    nc.gpsimd.tensor_tensor(x2b[:], x2[:], b2_b[:].unsqueeze(1).to_broadcast([P, TT, D]), ALU.add).then_inc(x2b_ready, 1)
                if i is not None:
                    for t in range(TT):
                        pool.wait_ge(ke_ready, i * TT + t + 1)
                        settled(pool)
                        nc.gpsimd.tensor_scalar(kp[:, t, :], kp[:, t, :], EPS_K, None, ALU.add).then_inc(kp_ready, 1)
                if u is not None:
                    root(4, u)
                if i is not None and not (isinstance(i, int) and i == B - 1):
                    root(0, i + 1)
                if u is not None:
                    root(5, u)
                    affine(u, y, yn_ready, ys_ready, y_ready, lnw_b, lnb_b)

            pool.wait_ge(w_in, 16 * N_W)
            root(0, 0)
            selection_constants()
            batches(pool, body)
            if stop == "x1":
                return

            def gather(e):
                pool.wait_ge(idxg_ready, e + 1)
                settled(pool)
                for g in range(GT):
                    pool.indirect_dma_start(xg[:, g, :], None, row_d, bass.IndirectOffsetOnAxis(ap=idx_g[:, g:g + 1], axis=0)
                                            ).then_inc(gathered, 16)

            def scatter(e):
                wait(pool, scattered, e * 16 * GT)
                pool.wait_ge(idxs_ready, e + 1)
                for g in range(GT):
                    pool.wait_ge(og_ready, e * GT + g + 1)
                    settled(pool)
                    pool.indirect_dma_start(acc_d, bass.IndirectOffsetOnAxis(ap=idx_s[:, g:g + 1], axis=0), og[:, g, :], None,
                                            compute_op=ALU.add).then_inc(scattered, 16)

            for s in (xf_out, y_out, sc_out):
                pool.wait_ge(s, 16 * B)
            gather(0)

            def expert(e, more):
                if more:
                    gather(e + 1)
                scatter(e)

            experts(pool, expert)

            def last(j, k):
                pool.wait_ge(vl_ready, j + 1)
                settled(pool)
                nc.gpsimd.tensor_scalar(vel[:, k], mvl[:, k, :, 1], LN_EPS, None, ALU.add).then_inc(vel_ready, 1)
                pool.wait_ge(vel_ready, j + 1)
                nc.gpsimd.tensor_tensor(rsl[:, k], vel[:, k], mhalf[:], ALU.pow).then_inc(rl_ready, 1)

            with pool.Fori(0, B // 2) as j2:
                for k in range(2):
                    last(j2 * 2 + k, k)

        @block.vector
        def _(dve):
            dve.wait_ge(wproj_in, 16 * HG)
            nc.vector.tensor_scalar(projbd[:], projbd[:], NORM, None, ALU.mult).then_inc(proj_ready, 1)
            dve.wait_ge(w_in, 16 * N_W)
            dve.wait_ge(const_ready, N_CONST)

            def over_tiles(row):
                return row[:].unsqueeze(1).to_broadcast([P, TT, D])

            def stats(k, steps, src):
                for t in range(TT):
                    ins = nc.vector.bn_stats(st[k][:, t, :], src[:, t, :])
                steps.link(ins)
                settled(dve)
                for t in range(TT):
                    ins = nc.vector.bn_aggr(mv[k][:, t, :], st[k][:, t, :])
                ins.then_inc(var_ready[k], 1)

            def normed(k, i, dst, src):
                dve.wait_ge(rstd_ready[k], i + 1)
                for t in range(TT):
                    ins = nc.vector.tensor_scalar(dst[:, t, :], src[:, t, :], mv[k][:, t, 0:1], rstd[k][:, t:t + 1],
                                                  ALU.subtract, ALU.mult)
                return ins

            def ln1_stats(i):
                steps = Steps(dve, dve_n, STEPS_N, i)
                dve.wait_ge(xin_in, (i + 1) * 16)
                stats(0, steps, xin)
                steps.end()

            def ln1_norm(i):
                wait(dve, xnb_ready, i)
                dve.wait_ge(rstd_ready[0], i + 1)
                for t in range(TT):
                    nc.vector.tensor_scalar(xn[:, t, :], xin[:, t, :], mv[0][:, t, 0:1], rstd[0][:, t:t + 1],
                                            ALU.subtract, ALU.mult).then_inc(xn_ready, 1)

            def k_max(i, t):
                dve.wait_ge(xk_ready, i * TT + t + 1)
                nc.vector.tensor_reduce(mxk[:, t, :], kp[:, t, :].rearrange("p (h m) -> p h m", m=M), AX_X,
                                        ALU.max).then_inc(kmx_ready, 1)

            def norms(i, m, dg):
                dve.wait_ge(sq_ready, i * 4 + m + 1)
                m2 = m % 2
                nc.vector.tensor_reduce(dg[:, 2 * m2:2 * m2 + 2, :], sq[:, m2].rearrange("p a (h d) -> p a h d", d=DH), AX_X,
                                        ALU.add).then_inc(dg_ready, 1)

            def k_shift(i, steps):
                dve.wait_ge(stab_ready, i + 1)
                steps.link(nc.vector.scalar_tensor_tensor(
                    out=kbias[:], in0=dgk[:], scalar=0.5 * NORM * NORM, in1=stabk[:].unsqueeze(1).to_broadcast([P, TT, H]),
                    op0=ALU.mult, op1=ALU.add))

            def k_sub(i, t):
                kt = kp[:, t, :].rearrange("p (h m) -> p h m", m=M)
                nc.vector.tensor_tensor(kt, kt, kbias[:, t, :].unsqueeze(2).to_broadcast([P, H, M]), ALU.subtract).then_inc(ks_ready, 1)

            def q_sub(i, t, steps):
                dve.wait_ge(x_ready, i * X_JOBS + J_XQ + t + 1)
                xq = pX[t % 2][:].rearrange("p a (h m) -> p (a h) m", m=M)
                steps.link(nc.vector.tensor_reduce(mxq[:, t, :], xq, AX_X, ALU.max))
                steps.link(nc.vector.scalar_tensor_tensor(out=qbias[:, t, :], in0=dgq[:, t, :], scalar=0.5 * NORM * NORM,
                                                          in1=mxq[:, t, :], op0=ALU.mult, op1=ALU.add))
                nc.vector.tensor_tensor(qe[:, t, :].rearrange("p (h m) -> p h m", m=M), xq,
                                        qbias[:, t, :].unsqueeze(2).to_broadcast([P, H, M]), ALU.subtract).then_inc(qs_ready, 1)

            def body(i, f, u):
                at_first(f, dve)
                more = i is not None and not (isinstance(i, int) and i == B - 1)
                if f is not None:
                    sf = Steps(dve, dve_f, STEPS_F, f)
                    dve.wait_ge(r_ready, 2 * (f + 1))
                    stats(1, sf, r)
                if u is not None:
                    su = Steps(dve, dve_u, STEPS_U, u)
                    dve.wait_ge(z_ready, 2 * (u + 1))
                    stats(2, su, z)
                if f is not None:
                    wait(dve, x2b_ready, f)
                    sf.link(normed(1, f, x2, r))
                    sf.link(nc.vector.tensor_tensor(x2[:], x2[:], over_tiles(g2_b), ALU.mult))
                    nc.vector.tensor_tensor(x2[:], x2[:], over_tiles(be2_b), ALU.add).then_inc(x2_ready, 1)
                    sf.end()
                if i is not None:
                    sa = Steps(dve, dve_a, STEPS_A, i)
                    for m in range(2):
                        dve.wait_ge(a_ready, i * A_JOBS + J_V + m + 1)
                        nc.vector.tensor_tensor(v[:, 2 * m:2 * m + 2, :], pA[m][:].rearrange("p (a b) -> p a b", a=2),
                                                bv_b[:].unsqueeze(1).to_broadcast([P, 2, D]), ALU.add).then_inc(v_ready, 1)
                if u is not None:
                    normed(2, u, z, z).then_inc(zn_ready, 1)
                if i is not None:
                    k_max(i, 0)
                    k_max(i, 1)
                    norms(i, 0, dgk)
                    norms(i, 1, dgk)
                    k_max(i, 2)
                    norms(i, 2, dgq)
                    norms(i, 3, dgq)
                    k_max(i, 3)
                    dve.wait_ge(kmx_ready, (i + 1) * TT)
                    nc.vector.tensor_reduce(kmax[:], mxk[:].rearrange("p t h -> p h t"), AX_X, ALU.max).then_inc(kmax_ready, 1)
                if u is not None:
                    dve.wait_ge(za_ready, u + 1)
                    stats(3, su, z)
                if i is not None:
                    dve.wait_ge(dg_ready, (i + 1) * 4)
                    k_shift(i, sa)
                    for t in range(TT):
                        k_sub(i, t)
                        q_sub(i, t, sa)
                if u is not None:
                    su.link(normed(3, u, z4, z))
                    dve.wait_ge(xres_in, 16 * (u + 1))
                    wait(dve, x1_out, 16 * u)
                    nc.vector.tensor_tensor(x1[:], z4[:], xres[:], ALU.add).then_inc(x1_ready, 1)
                    dve.wait_ge(x1_ready, u + 1)
                    stats(4, su, x1)
                if more:
                    ln1_stats(i + 1)
                if u is not None:
                    wait(dve, xf_out, 16 * u)
                    normed(4, u, xf, x1).then_inc(xf_ready, 1)
                if i is not None:
                    for n in range(TT):
                        dve.wait_ge(x_ready, i * X_JOBS + J_TQ + n + 1)
                        nc.vector.tensor_scalar(qp[:, 2 * n + 1, :], pX[n % 2][:, 1, :], EPS_K, None, ALU.add).then_inc(qpv_ready, 1)
                    dve.wait_ge(a_ready, i * A_JOBS + J_CTXT + 1)
                    nc.vector.tensor_tensor(ctxbd[:], pA[0][:, 0:G * P].rearrange("p (a b) -> p a b", b=32),
                                            headmask[:].unsqueeze(1).to_broadcast([P, PAIRS, 32]), ALU.mult).then_inc(cx_ready, 1)
                    nc.vector.tensor_tensor(denbd[:], pA[0][:, G * P:512].rearrange("p (a b) -> p a b", b=32),
                                            denmask[:], ALU.mult).then_inc(cx_ready, 1)

                def add_ff(m):
                    dve.wait_ge(f_ready, f * F_JOBS + J_Y + m + 1)
                    dve.wait_ge(x2b_ready, f + 1)
                    nc.vector.tensor_tensor(z[:, 2 * m:2 * m + 2, :], pF[m][:].rearrange("p (a b) -> p a b", a=2),
                                            x2b[:, 2 * m:2 * m + 2, :], ALU.add).then_inc(z_ready, 1)

                def heads_out(t):
                    dve.wait_ge(a_ready, i * A_JOBS + J_OT + t + 1)
                    s = pA[(J_OT + t) % 2]
                    sa.link(nc.vector.reciprocal(
                        rden[:, t, :].rearrange("p (g r k) -> p g r k", g=G, k=2),
                        s[:, 2 * P:3 * P].rearrange("p (r c) -> p r c", c=32)[:, :, 0:4].rearrange("p r (g k) -> p g r k", k=2)))
                    nc.vector.tensor_tensor(at[:, t, :].rearrange("p (h d) -> p h d", d=DH),
                                            s[:, 0:2 * P].rearrange("p (h d) -> p h d", d=DH),
                                            rden[:, t, :].unsqueeze(2).to_broadcast([P, H, DH]), ALU.mult).then_inc(at_ready, 1)

                if f is not None:
                    add_ff(0)
                if more:
                    ln1_norm(i + 1)
                if u is not None:
                    dve.wait_ge(xf_ready, u + 1)
                    stats(5, su, xf)
                if i is not None:
                    heads_out(0)
                    heads_out(1)
                if f is not None:
                    add_ff(1)
                if i is not None:
                    heads_out(2)
                    heads_out(3)
                if u is not None:
                    wait(dve, y_out, 16 * u)
                    normed(5, u, y, xf).then_inc(yn_ready, 1)
                    for m in range(2):
                        dve.wait_ge(u_ready, u * U_JOBS + J_G + m + 1)
                        nc.vector.tensor_copy(lg[:, 2 * m:2 * m + 2, :],
                                              pF[m][:, 0:2 * P].rearrange("p (a b) -> p a b", a=2)[:, :, 0:E]).then_inc(lg_ready, 1)
                    dve.wait_ge(lg_ready, 2 * (u + 1))
                    su.link(nc.vector.tensor_reduce(lmx[:], lg[:], AX_X, ALU.max))
                    nc.vector.tensor_tensor(lg[:], lg[:], lmx[:].unsqueeze(2).to_broadcast([P, TT, E]), ALU.subtract).then_inc(ls_ready, 1)
                if i is not None:
                    dve.wait_ge(xnb_ready, i + 1)
                    for m in range(2):
                        dve.wait_ge(a_ready, i * A_JOBS + J_WO + m + 1)
                        nc.vector.tensor_tensor(r[:, 2 * m:2 * m + 2, :], pA[m][:].rearrange("p (a b) -> p a b", a=2),
                                                xnb[:, 2 * m:2 * m + 2, :], ALU.add).then_inc(r_ready, 1)
                    sa.end()
                if u is not None:
                    dve.wait_ge(le_ready, u + 1)
                    su.link(nc.vector.tensor_reduce(lsum[:], lg[:], AX_X, ALU.add))
                    su.link(nc.vector.reciprocal(lrec[:], lsum[:]))
                    wait(dve, sc_out, 16 * u)
                    lr = lrec[:].unsqueeze(2).to_broadcast([P, TT, E])
                    for c in range(C):
                        nc.vector.tensor_tensor(sc[:, c, :, bass.ts(u, 2)].rearrange("p e s -> p s e"),
                                                lg[:].rearrange("p (s c) e -> p c s e", c=C)[:, c],
                                                lrec[:].rearrange("p (s c) -> p c s", c=C)[:, c].unsqueeze(2).to_broadcast([P, 2, E]), ALU.mult)
                    nc.vector.tensor_tensor(sct[:], lg[:], lr, ALU.mult).then_inc(sc_ready, 1)
                    su.end()

            ln1_stats(0)
            ln1_norm(0)
            batches(dve, body)
            if stop == "x1":
                return

            dve.wait_ge(sel_const, N_SEL)
            dve.wait_ge(s_turned, 1)
            nc.vector.tensor_copy(S, pA[0][:, 0:SEGW]).then_inc(s_ready, 1)
            dve.wait_ge(s_ready, 1)

            def search(rd):
                ss = Steps(dve, dve_s, SEL_STEPS, rd)
                ss.link(nc.vector.tensor_tensor(cand[:], step[:], thr[:].to_broadcast([P, CANDS]), ALU.bitwise_or))
                for k in range(CANDS):
                    nc.vector.tensor_scalar(flags[:, k], S, cand[:, k:k + 1].bitcast(F32), None, ALU.is_ge, ALU.add,
                                            accum_out=cnt[:, k:k + 1]).then_inc(cnt_ready, 1)
                dve.wait_ge(tot_ready, rd + 1)
                ss.link(nc.vector.tensor_scalar(passed[:], pA[1][:, 0:CANDS], KEEP - 0.5, None, ALU.is_ge, ALU.add,
                                                accum_out=npass[:]))
                ss.link(nc.vector.tensor_scalar(up[:], step[:, 0:1], npass[:, 0:1], None, ALU.mult))
                nc.vector.tensor_tensor(thr[:], thr[:], up[:], ALU.bitwise_or)
                ss.link(nc.vector.tensor_scalar(step[:], step[:], 3, None, ALU.logical_shift_right))
                ss.end()

            with dve.Fori(0, ROUNDS) as rd:
                search(rd)
            t0 = SEL_STEPS * ROUNDS
            done = Steps(dve, dve_s, 0, 0)
            done.n = t0
            cut = thr[:, 0:1].bitcast(F32)
            nc.vector.tensor_scalar(gt, S, cut, None, ALU.is_gt, ALU.add, accum_out=pair_cnt[:, 0:1])
            nc.vector.tensor_scalar(eq, S, cut, None, ALU.is_equal, ALU.add, accum_out=pair_cnt[:, 1:2]).then_inc(pair_ready, 1)
            dve.wait_ge(pair_ready, 1)
            nc.vector.tensor_tensor_scan(gin, ones_row[:], gt, 0.0, ALU.mult, ALU.add)
            nc.vector.tensor_tensor_scan(ein, ones_row[:], eq, 0.0, ALU.mult, ALU.add)
            dve.wait_ge(off_ready, 1)
            done.link(nc.vector.tensor_copy(offs[:], pA[0][:, 0:3]))
            done.link(nc.vector.tensor_tensor(eoff[:], offs[:, 1:2], offs[:, 2:3], ALU.add))
            done.link(nc.vector.tensor_scalar(ein, ein, eoff[:, 0:1], None, ALU.add))
            done.link(nc.vector.tensor_tensor(eq, eq, ein, ALU.mult))
            done.link(nc.vector.scalar_tensor_tensor(out=eq, in0=ein, scalar=KEEP + 0.5, in1=eq, op0=ALU.is_le, op1=ALU.mult))
            done.link(nc.vector.scalar_tensor_tensor(out=gin, in0=gin, scalar=offs[:, 0:1], in1=gt, op0=ALU.add, op1=ALU.mult))
            nc.vector.tensor_tensor(place, gin, eq, ALU.add).then_inc(place_ready, 1)
            dve.wait_ge(place_turned, 1)
            done.link(nc.vector.tensor_scalar(placei.rearrange("p c e s -> p (c e s)"), pA[1][:, 0:SEGW], 1.0, None, ALU.subtract))
            nc.vector.tensor_scalar(dig_a, placei, 4, None, ALU.arith_shift_right)
            done.link(nc.vector.tensor_scalar(dig_b, placei, SB - 1, None, ALU.bitwise_and))
            nc.vector.tensor_scalar(pmod[:], pint[:], SR - 1, None, ALU.bitwise_and)
            done.link(nc.vector.tensor_scalar(dig_b, dig_b, 0, None, ALU.add))
            done.link(nc.vector.tensor_copy(pmodf[:], pmod[:]))
            nc.vector.tensor_scalar(rmask[:], iotaf[:, 0:SR], pmodf[:, 0:1], None, ALU.is_equal)
            for c in range(C):
                for s0 in range(0, SEG, 4):
                    ss_ = slice(s0, s0 + 4)
                    nc.vector.tensor_tensor(oneA[:, c, ss_], dig_a[:, c, :, ss_].rearrange("p e s -> p s e").unsqueeze(3).to_broadcast([P, 4, E, SA]),
                                            iota_row[:].unsqueeze(1).unsqueeze(1).to_broadcast([P, 4, E, SA]), ALU.is_equal)
                    done.link(nc.vector.tensor_tensor(oneB[:, c, ss_, :, 0, :], dig_b[:, c, :, ss_].rearrange("p e s -> p s e").unsqueeze(3).to_broadcast([P, 4, E, SB]),
                                            iota_row[:, 0:SB].unsqueeze(1).unsqueeze(1).to_broadcast([P, 4, E, SB]), ALU.is_equal))
                    nc.vector.tensor_tensor(oneB[:, c, ss_, :, 1, :], oneB[:, c, ss_, :, 0, :],
                                            tilef[:, c, ss_].unsqueeze(2).unsqueeze(3).to_broadcast([P, 4, E, SB]), ALU.mult)
                    done.sync()
                    done.link(nc.vector.tensor_scalar(oneB[:, c, ss_, :, 0, :], oneB[:, c, ss_, :, 0, :], pcol[:, 0:1], None, ALU.mult))
                    nc.vector.tensor_scalar(zero4[:], zero4[:], 0.0, None, ALU.mult).then_inc(onehot_ready, 1)
            dve.wait_ge(ids_ready, 1)
            for k in range(2):
                for q in range(4):
                    ins = nc.vector.tensor_copy(Rbd[SA * q:SA * q + SA, k, q, :],
                                                pX[0][SA * q:SA * q + SA, k, 2 * SB * q:2 * SB * (q + 1)])
            ins.then_inc(rbd_ready, 1)
            dve.wait_ge(spread_ready, 1)
            done.link(nc.vector.tensor_tensor(idm[:], pX[1][:, 0, 0:E * 2 * SB].rearrange("p (x r g) -> p x r g", r=SR, g=GT),
                                              rmask[:].unsqueeze(1).unsqueeze(3).to_broadcast([P, E * 2, SR, GT]), ALU.mult))
            done.link(nc.vector.tensor_reduce(idf[:].rearrange("p e k g -> p (e k) g"), idm[:].rearrange("p x r g -> p x g r"), AX_X, ALU.add))
            nc.vector.scalar_tensor_tensor(out=idx[:], in0=idf[:, :, 1, :], scalar=float(P), in1=idf[:, :, 0, :], op0=ALU.mult,
                                           op1=ALU.add).then_inc(idx_ready, 1)
            dve.wait_ge(idx_ready, 1)

            def idx_for_gather(e):
                wait(dve, gathered, e * 16 * GT)
                nc.vector.tensor_tensor(idx_g[:], idx[:, bass.ds(e, 1), :].rearrange("p a g -> p (a g)"), zero4[:, 0:GT], ALU.add).then_inc(idxg_ready, 1)

            def next_weights(e):
                dve.wait_ge(gathered, (e + 1) * 16 * GT)
                wait(dve, wcur_ready, e)
                nc.vector.tensor_tensor(wnext[:], xg[:, :, bass.ds(e + D, 1)].rearrange("p g a -> p (g a)"), zero4[:, 0:GT], ALU.add).then_inc(wnext_ready, 1)

            def expert(e, more):
                if more:
                    dve.wait_ge(m_ready, e * M_JOBS + J_MX + 2)
                    idx_for_gather(e + 1)
                dve.wait_ge(wnext_ready, e + 1)
                wait(dve, og_ready, e * GT)
                nc.vector.tensor_copy(wcur[:], wnext[:]).then_inc(wcur_ready, 1)
                wait(dve, scattered, e * 16 * GT)
                nc.vector.tensor_tensor(idx_s[:], idx[:, bass.ds(e, 1), :].rearrange("p a g -> p (a g)"), zero4[:, 0:GT], ALU.add).then_inc(idxs_ready, 1)
                dve.wait_ge(b2e_in, 16 * (e + 1))
                dve.wait_ge(wcur_ready, e + 1)
                for m in range(2):
                    dve.wait_ge(m_ready, e * M_JOBS + J_MY + m + 1)
                    nc.vector.tensor_tensor(og[:, 2 * m:2 * m + 2, :], pM[(J_MY + m) % M_SLOTS].rearrange("p (a b) -> p a b", a=2),
                                            b2cur[:].unsqueeze(1).to_broadcast([P, 2, D]), ALU.add).then_inc(yo_ready, 1)
                    dve.wait_ge(yo_ready, e * 2 + m + 1)
                    for g in (2 * m, 2 * m + 1):
                        nc.vector.tensor_scalar(og[:, g, :], og[:, g, :], wcur[:, g:g + 1], None, ALU.mult).then_inc(og_ready, 1)
                    if m == 0 and more:
                        next_weights(e + 1)
                if more:
                    biases(e + 1)

            def biases(e):
                wait(dve, he_ready, e * FC)
                nc.vector.tensor_tensor(b1cur[:], b1e[:, bass.ds(e, 1), :].rearrange("p a n -> p (a n)"), zero4[:], ALU.add).then_inc(b1cur_ready, 1)

            dve.wait_ge(b1e_in, 16)
            idx_for_gather(0)
            biases(0)
            next_weights(0)
            experts(dve, expert)

            def last(j, k, j2):
                dve.wait_ge(acc_in[k], 16 * (j2 + 1))
                for t in range(TT):
                    ins = nc.vector.bn_stats(stl[:, k, t, :], acc_s[:, k, t, :])
                ins.then_inc(stl_ready, 1)
                dve.wait_ge(stl_ready, j + 1)
                settled(dve)
                for t in range(TT):
                    ins = nc.vector.bn_aggr(mvl[:, k, t, :], stl[:, k, t, :])
                ins.then_inc(vl_ready, 1)

            def last2(j, k, j2):
                dve.wait_ge(rl_ready, j + 1)
                for t in range(TT):
                    ins = nc.vector.tensor_scalar(acc_s[:, k, t, :], acc_s[:, k, t, :], mvl[:, k, t, 0:1], rsl[:, k, t:t + 1],
                                                  ALU.subtract, ALU.mult)
                ins.then_inc(nl_ready, 1)
                dve.wait_ge(nl_ready, j + 1)
                dve.wait_ge(x1_in[k], 16 * (j2 + 1))
                wait(dve, out_done[k], 16 * j2)
                nc.vector.tensor_tensor(o_s[:, k], acc_s[:, k], x1_s[:, k], ALU.add).then_inc(ol_ready, 1)

            def two_batches(j2):
                for k in range(2):
                    last(j2 * 2 + k, k, j2)
                for k in range(2):
                    last2(j2 * 2 + k, k, j2)

            two_batches(0)
            with dve.Fori(1, B // 2) as j2:
                two_batches(j2)

        @block.tensor
        def _(pe):
            a_taker = ([(xT_ready, 2, c) for c in range(2)] + [(kT_ready, 2, c) for c in range(2)] + [(qT_ready, 2, c) for c in range(2)]
                       + [(v_ready, 2, m) for m in range(2)] + [(sq_ready, 4, m) for m in range(4)] + [(cs_ready, 2, m) for m in range(2)]
                       + [(cx_ready, 2, 1)] + [(oT_ready, 3, m) for m in range(3)] + [(at_ready, 4, t) for t in range(4)]
                       + [(aT_ready, 2, c) for c in range(2)] + [(r_ready, 2, m) for m in range(2)])
            f_order = ([("f", x2T_ready, 2, c) for c in range(2)] + [("f", h_ready, FC, n) for n in range(FC)] + [("f", z_ready, 2, 0)]
                       + [("u", xfT_ready, 2, c) for c in range(2)] + [("f", z_ready, 2, 1)] + [("u", lg_ready, 2, m) for m in range(2)])
            f_place = {part: [k for k, x in enumerate(f_order) if x[0] == part] for part in "fu"}
            assert len(a_taker) == A_JOBS and len(f_place["f"]) == F_JOBS and len(f_place["u"]) == U_JOBS

            def slot(takers, jobs, i, n):
                if n < 2:
                    s, per, k = takers[jobs + n - 2]
                    wait(pe, s, (i - 1) * per + k + 1)
                else:
                    s, per, k = takers[n - 2]
                    wait(pe, s, i * per + k + 1)

            def slot_a(i, n):
                slot(a_taker, A_JOBS, i, n)
                return pA[n % 2]

            def slot_f(f, u, part, n):
                k = f_place[part][n]
                now, before = {"f": f, "u": u}, {"f": u if f is None else f - 1, "u": None if u is None else u - 1}
                for j in range(k - 2, k - 2 - 2 * len(f_order), -2):
                    p, s, per, m = f_order[j % len(f_order)]
                    b = (now if j >= 0 else before)[p]
                    if b is not None and not (isinstance(b, int) and b < 0):
                        wait(pe, s, b * per + m + 1)
                        break
                return pF[k % 2]

            def slot_x(i, n):
                if n < 2:
                    wait(pe, qpa_ready, (i - 1) * TT + TT - 1 + n)
                    wait(pe, qpv_ready, (i - 1) * TT + TT - 1 + n)
                elif n < 6:
                    pe.wait_ge(xk_ready, i * TT + n - 1)
                elif n < 10:
                    pe.wait_ge(qs_ready, i * TT + n - 5)
                else:
                    pe.wait_ge(qpa_ready, i * TT + n - 9)
                    pe.wait_ge(qpv_ready, i * TT + n - 9)
                return pX[n % 2]

            def turn(dst, src):
                return nc.tensor.transpose(dst, src, ident[:])

            def tok(t):
                return slice(t * P, (t + 1) * P)

            def turn_tokens(dst, src, c):
                for t in range(TT):
                    ins = turn(dst[:, tok(t)], src[:, t, tok(c)])
                return ins

            def by_tokens(dst, xt, w, m, ks):
                for t2 in range(2):
                    for k in range(ks):
                        ins = nc.tensor.matmul(dst[:, t2 * D:(t2 + 1) * D], xt[:, k, tok(2 * m + t2)], w[:, k, :],
                                               start=(k == 0), stop=(k == ks - 1))
                return ins

            def by_features(dst, w, xt, n, ks):
                for k in range(ks):
                    ins = nc.tensor.matmul(dst[:], w[:, k, tok(n)], xt[:, k, :], start=(k == 0), stop=(k == ks - 1))
                return ins

            def features(i, n, src, t):
                s = slot_x(i, n)
                for g in range(G):
                    ins = nc.tensor.matmul(s[:, g, :], src[:, g, tok(t)], projbd[:], start=True, stop=True)
                ins.then_inc(x_ready, 1)

            def turn_heads(i, m, src):
                s = slot_a(i, J_DK + m)
                for t2 in range(2):
                    for g in range(G):
                        ins = turn(s[:, t2 * D + g * P:t2 * D + (g + 1) * P], src[:, g, tok(2 * (m % 2) + t2)])
                ins.then_inc(a_ready, 1)

            def body(i, f, u):
                att, ff, gt_ = i is not None, f is not None, u is not None

                def hidden(n):
                    s = slot_f(f, u, "f", J_H + n)
                    by_features(s, w1, x2T, n, C).then_inc(f_ready, 1)

                def ff_out(m, slots, half):
                    if half == 0:
                        slots[m] = slot_f(f, u, "f", J_Y + m)
                    for k in range(FC):
                        ins = nc.tensor.matmul(slots[m][:, half * D:(half + 1) * D], h[:, k, tok(2 * m + half)], w2[:, k, :],
                                               start=(k == 0), stop=(k == FC - 1))
                    if half == 1:
                        ins.then_inc(f_ready, 1)

                def attention_out(j, w_, first, last_):
                    s = slot_a(i, j)
                    for g in range(first, last_ + 1):
                        for q in range(4):
                            ins = nc.tensor.matmul(s[32 * q:32 * q + 32, :], w_[:, 4 * g + q, :], qp[:, 4 * g + q, :],
                                                   start=(g == first), stop=(g == last_), tile_position=(0, 32 * q))
                    ins.then_inc(a_ready, 1)

                def turn_out(t):
                    s = slot_a(i, J_OT + t)
                    for n in range(3):
                        ins = turn(s[:, tok(n)], oT[:, n, tok(t)])
                    ins.then_inc(a_ready, 1)

                def gates(m):
                    s = slot_f(f, u, "u", J_G + m)
                    for t2 in range(2):
                        for c in range(C):
                            ins = nc.tensor.matmul(s[:, tok(t2)], x2T[:, c, tok(2 * m + t2)], gate[:, c, :],
                                                   start=(c == 0), stop=(c == C - 1))
                    ins.then_inc(u_ready, 1)

                at_first(f, pe)
                if att:
                    pe.wait_ge(xn_ready, (i + 1) * TT)
                    for c in range(C):
                        turn_tokens(slot_a(i, J_XT + c), xn, c).then_inc(a_ready, 1)
                    pe.wait_ge(xT_ready, (i + 1) * C)
                    for j0, w in ((J_K, wk), (J_Q, wq)):
                        for c in range(G):
                            by_features(slot_a(i, j0 + c), w, xT, c, C).then_inc(a_ready, 1)
                    for m in range(2):
                        by_tokens(slot_a(i, J_V + m), xT, wv, m, C).then_inc(a_ready, 1)
                    pe.wait_ge(kT_ready, (i + 1) * G)
                    features(i, J_XK, kT, 0)
                    features(i, J_XK + 1, kT, 1)
                    turn_heads(i, 0, kT)
                    turn_heads(i, 1, kT)
                    features(i, J_XK + 2, kT, 2)
                    pe.wait_ge(qT_ready, (i + 1) * G)
                    turn_heads(i, 2, qT)
                    turn_heads(i, 3, qT)
                    features(i, J_XK + 3, kT, 3)
                if ff:
                    pe.wait_ge(x2_ready, f + 1)
                    for c in range(C):
                        turn_tokens(slot_f(f, u, "f", J_X2T + c), x2, c).then_inc(f_ready, 1)
                    pe.wait_ge(x2T_ready, (f + 1) * C)
                    hidden(0)
                for t in range(TT):
                    if att:
                        features(i, J_XQ + t, qT, t)
                    if ff:
                        hidden(t + 1)
                if ff:
                    for n in range(TT + 1, FC):
                        hidden(n)
                if att:
                    pe.wait_ge(kp_ready, (i + 1) * TT)
                    pe.wait_ge(v_ready, (i + 1) * 2)
                    for j, lhs in ((J_CTX, v), (J_KSUM, None)):
                        s = slot_a(i, j)
                        for g in range(G):
                            for t in range(TT):
                                for q in range(4):
                                    pair = 4 * g + q
                                    ins = nc.tensor.matmul(
                                        s[32 * q:32 * q + 32, g * P:(g + 1) * P],
                                        ones32[:] if lhs is None else lhs[:, t, 32 * pair:32 * pair + 32],
                                        kp[:, t, P * pair:P * pair + P], start=(t == 0), stop=(t == TT - 1),
                                        tile_position=(0, 32 * q))
                        ins.then_inc(a_ready, 1)
                    pe.wait_ge(qe_ready, (i + 1) * TT)
                    for n in range(TT):
                        s = slot_x(i, J_TQ + n)
                        for k in range(2):
                            for t in range(TT):
                                ins = turn(s[:, k, tok(t)], qe[:, t, tok(2 * n + k)])
                        ins.then_inc(x_ready, 1)
                    pe.wait_ge(cs_ready, (i + 1) * 2)
                    s = slot_a(i, J_CTXT)
                    for n in range(2):
                        for g in range(G):
                            ins = turn(s[:, (2 * n + g) * P:(2 * n + g + 1) * P], cs[:, n, tok(g)])
                    ins.then_inc(a_ready, 1)
                slots = [None, None]
                if ff:
                    pe.wait_ge(h_ready, (f + 1) * FC)
                    for half in range(2):
                        ff_out(0, slots, half)
                if att:
                    pe.wait_ge(cx_ready, (i + 1) * 2)
                    pe.wait_ge(qpa_ready, (i + 1) * TT)
                    pe.wait_ge(qpv_ready, (i + 1) * TT)
                    attention_out(J_OUT, ctxbd, 0, 0)
                    attention_out(J_OUT + 1, ctxbd, 1, 1)
                    attention_out(J_OUT + 2, denbd, 0, 1)
                if gt_:
                    pe.wait_ge(xf_ready, u + 1)
                    for c in range(C):
                        turn_tokens(slot_f(f, u, "u", J_XFT + c), xf, c).then_inc(u_ready, 1)
                if ff:
                    ff_out(1, slots, 0)
                if att:
                    pe.wait_ge(oT_ready, (i + 1) * 3)
                    turn_out(0)
                    turn_out(1)
                if ff:
                    ff_out(1, slots, 1)
                if att:
                    turn_out(2)
                    turn_out(3)
                if gt_:
                    pe.wait_ge(xfT_ready, (u + 1) * C)
                    gates(0)
                    gates(1)
                if att:
                    pe.wait_ge(at_ready, (i + 1) * TT)
                    for c in range(C):
                        turn_tokens(slot_a(i, J_AT + c), at, c).then_inc(a_ready, 1)
                    pe.wait_ge(aT_ready, (i + 1) * C)
                    for m in range(2):
                        by_tokens(slot_a(i, J_WO + m), aT, wo, m, C).then_inc(a_ready, 1)

            pe.wait_ge(const_ready, N_CONST)
            pe.wait_ge(proj_ready, 1)
            pe.wait_ge(w_in, 16 * N_W)
            batches(pe, body)
            if stop == "x1":
                return

            pe.wait_ge(sel_const, N_SEL)
            pe.wait_ge(sc_ready, B)
            pe.wait_ge(r_ready, 2 * B)
            for c in range(C):
                ins = turn(pA[0][:, tok(c)], sc[:, c].rearrange("p e s -> p (e s)"))
            ins.then_inc(s_turned, 1)

            with pe.Fori(0, ROUNDS) as rd:
                pe.wait_ge(cnt_ready, (rd + 1) * CANDS)
                nc.tensor.matmul(pA[1][:, 0:CANDS], blockones[:], cnt[:], start=True, stop=True).then_inc(tot_ready, 1)
            pe.wait_ge(pair_ready, 1)
            pe.wait_ge(s_ready, 1)
            nc.tensor.matmul(pA[0][:, 0:2], blockbelow[:], pair_cnt[:], start=True, stop=True)
            nc.tensor.matmul(pA[0][:, 2:3], blockones[:], pair_cnt[:, 0:1], start=True, stop=True).then_inc(off_ready, 1)
            pe.wait_ge(place_ready, 1)
            for c in range(C):
                ins = turn(pA[1][:, tok(c)], place[:, tok(c)])
            ins.then_inc(place_turned, 1)
            n = 0
            for c in range(C):
                for s0 in range(0, SEG, 4):
                    n += 1
                    pe.wait_ge(onehot_ready, n)
                    for s_ in range(s0, s0 + 4):
                        first, final = n == 1 and s_ == 0, c == C - 1 and s_ == SEG - 1
                        for k in range(2):
                            ins = nc.tensor.matmul(pX[0][:, k, 0:P], oneA[:, c, s_, 4 * k:4 * k + 4, :].rearrange("p e a -> p (e a)"),
                                                   oneB[:, c, s_, 4 * k:4 * k + 4].rearrange("p e k b -> p (e k b)"), start=first, stop=final)
            ins.then_inc(ids_ready, 1)
            pe.wait_ge(rbd_ready, 1)
            for k in range(2):
                ins = nc.tensor.matmul(pX[1][:, 0, tok(k)], spread[:], Rbd[:, k].rearrange("p q b -> p (q b)"), start=True, stop=True)
            ins.then_inc(spread_ready, 1)
            pe.wait_ge(idx_ready, 1)

            m_taker = ([(xgT_ready, 2, c) for c in range(2)] + [(he_ready, FC, n) for n in range(FC)] + [(yo_ready, 2, m) for m in range(2)])

            def slot_m(e, n):
                s, per, k = m_taker[(n - M_SLOTS) % M_JOBS]
                wait(pe, s, (e if n >= M_SLOTS else e - 1) * per + k + 1)
                return pM[n % M_SLOTS]

            def turn_rows(e):
                pe.wait_ge(gathered, (e + 1) * 16 * GT)
                for c in range(C):
                    turn_tokens(slot_m(e, J_MX + c), xg, c).then_inc(m_ready, 1)

            def expert(e, more):
                pe.wait_ge(w1e_in, 16 * (e + 1))
                pe.wait_ge(xgT_ready, (e + 1) * C)
                for n in range(FC):
                    by_features(slot_m(e, J_MH + n), w1e, xgT, n, C).then_inc(m_ready, 1)
                pe.wait_ge(w2e_in, 16 * (e + 1))
                pe.wait_ge(he_ready, (e + 1) * FC)
                for m in range(2):
                    by_tokens(slot_m(e, J_MY + m), h, w2e, m, FC).then_inc(m_ready, 1)
                if more:
                    turn_rows(e + 1)

            turn_rows(0)
            experts(pe, expert)


_COL = lambda a: a.reshape(-1, P).T
_LAYOUT = {
    "video": ("L0_attn_video", lambda a: a.reshape(T, D)),
    "WqT": ("L0_attn_Wq", lambda a: a.T), "bq": ("L0_attn_bq", _COL),
    "WkT": ("L0_attn_Wk", lambda a: a.T), "bk": ("L0_attn_bk", _COL),
    "WvT": ("L0_attn_Wv", lambda a: a.T), "bv": ("L0_attn_bv", None),
    "WoT": ("L0_attn_Wo", lambda a: a.T), "bo": ("L0_attn_bo", None),
    "projT": ("L0_attn_proj", lambda a: a.T),
    "W1T": ("L0_attn_W1", lambda a: a.T), "b1": ("L0_attn_b1", _COL),
    "W2T": ("L0_attn_W2", lambda a: a.T), "b2": ("L0_attn_b2", None),
    "g2": ("L0_attn_g2", None), "be2": ("L0_attn_be2", None),
    "g3": ("L0_attn_g3", None), "be3": ("L0_attn_be3", None),
    "gateT": ("L0_ffn_gate_w", lambda a: a.T),
    "ln_w": ("L0_ffn_ln_w", None), "ln_b": ("L0_ffn_ln_b", None),
    "fc1T": ("L0_ffn_fc1s", lambda a: a.transpose(0, 2, 1)),
    "b1s": ("L0_ffn_b1s", lambda a: a.reshape(E, FC, P).transpose(2, 0, 1)),
    "fc2T": ("L0_ffn_fc2s", lambda a: a.transpose(0, 2, 1)),
    "b2s": ("L0_ffn_b2s", None),
}


def kernel(**inputs):
    import concourse.bacc as bacc
    from concourse.bass_utils import run_bass_kernel_spmd

    nc = bacc.Bacc("TRN2", target_bir_lowering=False, num_devices=1)
    arrays, args = {}, []
    for name, (source, layout) in _LAYOUT.items():
        a = np.asarray(inputs[source])
        a = np.ascontiguousarray(layout(a) if layout else a)
        arrays[name] = a
        args.append(nc.dram_tensor(name, a.shape, mybir.dt.from_np(a.dtype), kind="ExternalInput").ap())
    out = nc.dram_tensor("out", (T, D), F32, kind="ExternalOutput").ap()
    build(nc, *args, out)
    res = run_bass_kernel_spmd(nc, [arrays], core_ids=[0])
    return res.results[0]["out"].reshape(B, N, D)
```

```python
from contextlib import ExitStack

import numpy as np
import concourse.bass as bass
from concourse import mybir

ALU = mybir.AluOpType
ACT = mybir.ActivationFunctionType
F32 = mybir.dt.float32
F32R = mybir.dt.float32r
F16 = mybir.dt.float16
BF16 = mybir.dt.bfloat16
I32 = mybir.dt.int32
U32 = mybir.dt.uint32
AX_X = mybir.AxisListType.X
RMAX = bass.bass_isa.ReduceOp.max

P = 128
B, N, D = 8, 512, 256
T = B * N
TT = N // P
C = D // P
H, DH, M = 16, 16, 64
G = 2
HG = H // G
PAIRS = H // 2
FF = 1024
FC = FF // P
EPS_K = 1e-4
N_CONST = 12
N_WFF = 11
N_SEL = 15
LN_EPS = 1e-5
LNS = 6
NORM = DH ** -0.25
E = 8
KEEP = T // E
SEG = P // E
SEGW = T // SEG
ROW = D + E
GT = KEEP // P

ROUNDS, CANDS = 10, 7
HI_ROUNDS = 4
SA, SB = 32, 16
SR = P // SA
LQ = 4
M_JOBS, M_SLOTS = 10, 4
J_MH, J_MY = 0, 8

A_JOBS, X_JOBS, F_JOBS, U_JOBS = 24, 12, 12, 4
(J_K, J_Q, J_V, J_DK, J_DQ, J_CTX, J_KSUM, J_CTXT, J_OUT, J_OT, J_AT, J_WO) = (
    0, 2, 4, 6, 8, 10, 11, 12, 13, 16, 20, 22)
J_XK, J_XQ, J_TQ = 0, 4, 8
J_X2T, J_H, J_Y = 0, 2, 10
J_XFT, J_G = 0, 2


def wait(eng, sem, value):
    if isinstance(value, int) and value <= 0:
        return
    eng.wait_ge(sem, value)


class Steps:

    def __init__(self, eng, sem, per, i):
        self.eng, self.sem, self.per, self.i, self.n = eng, sem, per, i, 0

    def put(self, ins):
        ins.then_inc(self.sem, 1)
        self.n += 1

    def sync(self):
        self.eng.wait_ge(self.sem, self.i * self.per + self.n)

    def link(self, ins):
        self.put(ins)
        self.sync()

    def end(self):
        assert self.n == self.per, (self.sem, self.n, self.per)


def build(nc, video, WqT, bq, WkT, bk, WvT, bv, WoT, bo, projT, W1T, b1, W2T, b2, g2, be2, g3, be3,
          gateT, ln_w, ln_b, fc1T, b1s, fc2T, b2s, out, stop=None):
    with ExitStack() as ctx:
        def sb(name, shape, dt=F32):
            return ctx.enter_context(nc.sbuf_tensor(name, shape, dt))

        def sem(name):
            return ctx.enter_context(nc.semaphore(name))

        pA = [ctx.enter_context(nc.psum_tensor(f"pA{s}", [P, 512], F32)) for s in range(2)]
        pX = [ctx.enter_context(nc.psum_tensor(f"pX{s}", [P, 2, 512], F32)) for s in range(2)]
        pF = [ctx.enter_context(nc.psum_tensor(f"pF{s}", [P, 512], F32)) for s in range(2)]

        pM = [pX[k // 2][:, k % 2, :] for k in range(4)]
        x1_d = nc.dram_tensor("x1_scratch", (T, D), F32, kind="Internal").ap()
        acc_d = nc.dram_tensor("acc_scratch", (T, D), F32, kind="Internal").ap()
        row_d = nc.dram_tensor("row_scratch", (T, ROW), F32, kind="Internal").ap()

        wq, wk, wv, wo = (sb(n, [P, C, D]) for n in ("wq", "wk", "wv", "wo"))
        w1_hi = sb("w1_hi", [P, C, FF], F32R)
        w1_lo = sb("w1_lo", [P, C, FF], F32R)
        w2 = sb("w2", [P, FC, D])
        gate = sb("gate", [P, C, P])
        projbd = sb("projbd", [P, HG * M])
        bqk = sb("bqk", [P, 2, G])
        b1c = sb("b1c", [P, FC])
        bv_b, bo_b, b2_b, g2_b, be2_b, g3_b, be3_b, lnw_b, lnb_b = (
            sb(n, [P, D]) for n in ("bv_b", "bo_b", "b2_b", "g2_b", "be2_b", "g3_b", "be3_b", "lnw_b", "lnb_b"))
        ident = sb("ident", [P, P])
        ones32 = sb("ones32", [P, 32])
        mhalf = sb("mhalf", [P, TT])
        epsk_c = sb("epsk_c", [P, 1])
        headmask = sb("headmask", [P, 32])
        denmask = sb("denmask", [P, PAIRS, 32])
        sq = sb("sq", [P, 2, 2, D])
        ksum = sq[:].rearrange("p a b d -> p (a b d)")
        dgk = sb("dgk", [P, TT, H])
        dgq = sb("dgq", [P, TT, H])
        mxk = sb("mxk", [P, TT, H])
        mxq = sb("mxq", [P, TT, H])
        kmax = sb("kmax", [P, H])
        stabk = sb("stabk", [P, H])
        kbias = sb("kbias", [P, TT, H])
        qbias = sb("qbias", [P, TT, H])
        kp = sb("kp", [P, TT, H * M])
        qe = sb("qe", [P, TT, H * M])
        qp = sb("qp", [P, PAIRS, N])
        cs = sb("cs", [P, 2, G * P])
        ctxbd = sb("ctxbd", [P, PAIRS, 32])
        denbd = sb("denbd", [P, PAIRS, 32])
        oT = sb("oT", [P, 3, N])
        rden = sb("rden", [P, TT, H])
        at = sb("at", [P, TT, D])
        aT = sb("aT", [P, C, N])
        x2T_hi = sb("x2T_hi", [P, C, N], F32R)
        x2T_lo = sb("x2T_lo", [P, C, N], F32R)
        h = sb("h", [P, FC, N])
        w1_raw = h[:].rearrange("p a b -> p (a b)")[:, 0:C * FF].rearrange("p (c n) -> p c n", c=C)
        x1 = sb("x1", [P, TT, D])
        xfT = aT
        lg = sb("lg", [P, TT, E])
        lmx = sb("lmx", [P, TT])
        lsum = sb("lsum", [P, TT])
        lrec = sb("lrec", [P, TT])
        sct = sb("sct", [P, TT, E])
        sc = sb("sc", [P, C, E, SEG])
        st = [sb(f"st{k}", [P, TT, 6]) for k in range(LNS)]
        mv = [sb(f"mv{k}", [P, TT, 2]) for k in range(LNS)]
        ve = [sb(f"ve{k}", [P, TT]) for k in range(LNS)]
        rstd = [sb(f"rstd{k}", [P, TT]) for k in range(LNS)]

        kp_f, qe_f, qp_f = (a[:].rearrange("p a b -> p (a b)") for a in (kp, qe, qp))
        S, gt, eq, gin, ein, place = (kp_f[:, k * SEGW:(k + 1) * SEGW] for k in range(6))
        flags = qe_f[:, 8 * SEGW:(8 + CANDS) * SEGW].rearrange("p (k j) -> p k j", k=CANDS)
        flags_hi, S_hi = (qe_f[:, k * SEGW:(k + w) * SEGW].bitcast(BF16) for k, w in ((8, CANDS // 2 + 1), (15, 1)))
        flags_hi, S_hi = flags_hi[:, 0:CANDS * SEGW].rearrange("p (k j) -> p k j", k=CANDS), S_hi[:, 0:SEGW]
        dig_a, dig_b = (kp_f[:, 7 * SEGW:8 * SEGW].bitcast(F16)[:, k * SEGW:(k + 1) * SEGW].rearrange("p (c e s) -> p c e s", c=C, e=E)
                        for k in range(2))
        placei, digi_a, digi_b = (qe_f[:, k * SEGW:(k + 1) * SEGW].bitcast(I32).rearrange("p (c e s) -> p c e s", c=C, e=E)
                                  for k in (8, 9, 10))
        thr = sb("thr", [P, 1], U32)
        step = sb("step", [P, CANDS], U32)
        nstep = sb("nstep", [P, CANDS], U32)
        base = sb("base", [P, CANDS], U32)
        cand = sb("cand", [P, CANDS], U32)
        cnt = sb("cnt", [P, CANDS])
        passed = sb("passed", [P, CANDS])
        npass = sb("npass", [P, 1])
        up = sb("up", [P, 1], U32)
        ones_row = sb("ones_row", [P, SEGW])
        blockones = sb("blockones", [P, P])
        blockbelow = sb("blockbelow", [P, P])
        pair_cnt = sb("pair_cnt", [P, 2])
        offs = sb("offs", [P, 3])
        eoff = sb("eoff", [P, 1])
        iota_row = sb("iota_row", [P, SA], I32)
        iotaf = sb("iotaf", [P, SA])
        iotah = sb("iotah", [P, SA], F16)
        idval = sb("idval", [P, C, SEG])
        oneA = qp_f.bitcast(F16).rearrange("p (c s e a) -> p c s e a", c=C, s=SEG, e=E)
        oneB = qe_f.bitcast(F16)[:, 0:C * SEG * E * SB].rearrange("p (c s e b) -> p c s e b", c=C, s=SEG, e=E)
        spread = sb("spread", [P, P], F16)
        rmask = sb("rmask", [P, SR])
        pmod = sb("pmod", [P, 1], I32)
        pmodf = sb("pmodf", [P, 1])
        spread_one = sb("spread_one", [P, SA])
        pint = sb("pint", [P, 1], I32)
        tint = sb("tint", [P, C, SEG], I32)
        Rbd = sb("Rbd", [P, 2, 4, SB], F16)
        idm = sb("idm", [P, E, SR, GT])
        idf = sb("idf", [P, E, GT])
        idx = sb("idx", [P, E, GT])
        w2e, og = w2, at
        w1e = kp_f[:, C * FF:2 * C * FF].rearrange("p (c n) -> p c n", c=C)
        xgT_hi, xgT_lo = x2T_hi, x2T_lo
        b1e = sb("b1e", [P, E, FC])
        b1cur = sb("b1cur", [P, FC])
        b2cur = sb("b2cur", [P, D])
        xg = sb("xg", [P, GT, ROW])
        idx_g = sb("idx_g", [P, GT], U32)
        idx_s = sb("idx_s", [P, GT], U32)
        wnext = sb("wnext", [P, GT])
        wcur = sb("wcur", [P, GT])
        zero4 = sb("zero4", [P, FC])
        with ExitStack() as first_stages:
            def early(name, shape):
                return first_stages.enter_context(nc.sbuf_tensor(name, shape, F32))

            xin = early("xin", [P, TT, D])
            xn = early("xn", [P, TT, D])
            xnb = early("xnb", [P, TT, D])
            xT = early("xT", [P, C, N])
            kT = early("kT", [P, G, N])
            qT = early("qT", [P, G, N])
            v = early("v", [P, TT, D])
            r = early("r", [P, TT, D])
            x2 = early("x2", [P, TT, D])
            z = early("z", [P, TT, D])
            xf = early("xf", [P, TT, D])
            y = early("y", [P, TT, D])
        h_hi, h_lo = (sb(n, [P, FC, N], F32R) for n in ("h_hi", "h_lo"))
        w2_hi, w2_lo = (sb(n, [P, FC, D], F32R) for n in ("w2_hi", "w2_lo"))
        h_f = h[:].rearrange("p a b -> p (a b)")
        acc_s = [a.rearrange("p (k t d) -> p k t d", k=LQ, t=TT) for a in (kp_f, h_f)]
        x1_s = [a.rearrange("p (k t d) -> p k t d", k=LQ, t=TT) for a in (qp_f, qe_f)]
        sq_f = sq[:].rearrange("p a b d -> p (a b d)")
        stl = sq_f[:, 0:B * TT * 6].rearrange("p (k t s) -> p k t s", k=B, t=TT)
        mvl = sq_f[:, 256:256 + B * TT * 2].rearrange("p (k t s) -> p k t s", k=B, t=TT)
        vel, rsl, nmr = (sq_f[:, 384 + 64 * n:384 + 64 * n + B * TT].rearrange("p (k t) -> p k t", k=B) for n in range(3))


        wk_in, wq_in, wv_in, wo_in = (sem(f"w{n}_in") for n in "kqvo")
        bqk_in, bvo_in = sem("bqk_in"), sem("bvo_in")
        wff_in = sem("wff_in")
        wproj_in = sem("wproj_in")
        w1_in, w1_split = sem("w1_in"), sem("w1_split")
        const_step, const_ready, proj_ready = sem("const_step"), sem("const_ready"), sem("proj_ready")
        t_ready, a_ready, x_ready, f_ready, u_ready = sem("t_ready"), sem("a_ready"), sem("x_ready"), sem("f_ready"), sem("u_ready")
        var_ready = [sem(f"var_ready{k}") for k in range(LNS)]
        ve_ready = [sem(f"ve_ready{k}") for k in range(LNS)]
        rstd_ready = [sem(f"rstd_ready{k}") for k in range(LNS)]
        xin_in, xres_in = sem("xin_in"), sem("xres_in")
        xn_ready, xnb_ready = sem("xn_ready"), sem("xnb_ready")
        xT_ready, kT_ready, qT_ready, v_ready = sem("xT_ready"), sem("kT_ready"), sem("qT_ready"), sem("v_ready")
        sq_ready, dg_ready = sem("sq_ready"), sem("dg_ready")
        xk_ready, kmx_ready, kmax_ready, stab_ready = sem("xk_ready"), sem("kmx_ready"), sem("kmax_ready"), sem("stab_ready")
        kbias_ready, ksp_ready = sem("kbias_ready"), sem("ksp_ready")
        ksum_ready, ks_ready, ke_ready, kp_ready = sem("ksum_ready"), sem("ks_ready"), sem("ke_ready"), sem("kp_ready")
        qs_ready, qe_ready, qpa_ready, qpv_ready = sem("qs_ready"), sem("qe_ready"), sem("qpa_ready"), sem("qpv_ready")
        cs_ready, cx_ready, oT_ready = sem("cs_ready"), sem("cx_ready"), sem("oT_ready")
        at_ready, aT_ready, r_ready = sem("at_ready"), sem("aT_ready"), sem("r_ready")
        x2_ready, x2b_ready, x2T_ready, x2l_ready, h_ready = sem("x2_ready"), sem("x2b_ready"), sem("x2T_ready"), sem("x2l_ready"), sem("h_ready")
        zn_ready, zs_ready, za_ready, yn_ready, ys_ready = (
            sem("zn_ready"), sem("zs_ready"), sem("za_ready"), sem("yn_ready"), sem("ys_ready"))
        z_ready, x1_ready, xf_ready, y_ready = sem("z_ready"), sem("x1_ready"), sem("xf_ready"), sem("y_ready")
        xfT_ready, lg_ready = sem("xfT_ready"), sem("lg_ready")
        ls_ready, le_ready, sc_ready = sem("ls_ready"), sem("le_ready"), sem("sc_ready")
        x1_out, xf_out, y_out, sc_out = sem("x1_out"), sem("xf_out"), sem("y_out"), sem("sc_out")
        dve_n, dve_a, dve_f, dve_u = sem("dve_n"), sem("dve_a"), sem("dve_f"), sem("dve_u")
        sel_const, sel_step, s_turned, s_ready = sem("sel_const"), sem("sel_step"), sem("s_turned"), sem("s_ready")
        cnt_ready, tot_ready, dve_s, dve_r = sem("cnt_ready"), sem("tot_ready"), sem("dve_s"), sem("dve_r")
        pair_ready, off_ready, place_ready, place_turned = sem("pair_ready"), sem("off_ready"), sem("place_ready"), sem("place_turned")
        oneb_ready, onea_ready, onehot_ready, ids_ready, rbd_ready, spread_ready, idx_ready = (
            sem("oneb_ready"), sem("onea_ready"), sem("onehot_ready"), sem("ids_ready"), sem("rbd_ready"), sem("spread_ready"), sem("idx_ready"))
        w1e_hi_ready, w1e_ready, xgl_ready, rows_turned, m_ready, xgT_ready, he_ready, yo_ready = sem("w1e_hi_ready"), sem("w1e_ready"), sem("xgl_ready"), sem("rows_turned"), sem("m_ready"), sem("xgT_ready"), sem("he_ready"), sem("yo_ready")
        w1e_in, w2e_in, b1e_in, b2e_in = sem("w1e_in"), sem("w2e_in"), sem("b1e_in"), sem("b2e_in")
        idxg_ready, idxs_ready, b1cur_ready, wnext_ready, wcur_ready = (
            sem("idxg_ready"), sem("idxs_ready"), sem("b1cur_ready"), sem("wnext_ready"), sem("wcur_ready"))
        gathered, scattered, og_ready = sem("gathered"), sem("scattered"), sem("og_ready")
        acc_in = [sem(f"acc_in{j}") for j in range(B)]
        x1_in, out_done = sem("x1_in"), sem("out_done")
        w2_hi_ready, w2_ready, h_hi_ready, h_lo_ready = sem("w2_hi_ready"), sem("w2_ready"), sem("h_hi_ready"), sem("h_lo_ready")
        stl_ready, vl_ready, vel_ready, rl_ready, nmr_ready, nl_ready, olv_ready, olp_ready = (
            sem("stl_ready"), sem("vl_ready"), sem("vel_ready"), sem("rl_ready"), sem("nmr_ready"), sem("nl_ready"),
            sem("olv_ready"), sem("olp_ready"))
        STEPS_N, STEPS_A, STEPS_F, STEPS_U = 1, 12, 3, 8
        SEL_STEPS = 7

        vid_d = video.rearrange("(b t p) d -> b p t d", t=TT, p=P)
        x1_t = x1_d.rearrange("(b t p) d -> b p t d", t=TT, p=P)
        acc_t = acc_d.rearrange("(b t p) d -> b p t d", t=TT, p=P)
        row_t = row_d.rearrange("(b t p) r -> b p t r", t=TT, p=P)

        def batches(eng, body):
            body(0, None, None)
            body(1, 0, None)
            body(2, 1, 0)
            with eng.Fori(3, B - 1) as i:
                body(i, i - 1, i - 2)
            body(B - 1, B - 2, B - 3)
            body(None, B - 1, B - 2)
            body(None, None, B - 1)

        def at_first(f, pe_like):
            if isinstance(f, int) and f == 0:
                pe_like.wait_ge(wff_in, 16 * N_WFF)

        out_t = out.rearrange("(b t p) d -> b p t d", t=TT, p=P)

        def experts(eng, body):
            body(0, 2)
            with eng.Fori(1, E - 2) as e:
                body(e, 2)
            body(E - 2, 1)
            body(E - 1, 0)

        waits_met = sem("waits_met")

        def settled(eng):
            eng.sem_inc(waits_met, 1)

        block = ctx.enter_context(nc.Block())

        @block.sync
        def _(sp):
            def load_x(i):
                wait(sp, xn_ready, i * TT)
                sp.dma_start(xin[:], vid_d[i]).then_inc(xin_in, 16)

            def body(i, f, u):
                if i is not None and not (isinstance(i, int) and i == B - 1):
                    load_x(i + 1)
                if u is not None:
                    wait(sp, x1_out, 16 * u)
                    wait(sp, xf_ready, u)
                    sp.dma_start(x1[:], vid_d[u]).then_inc(xres_in, 16)
                    for ready, done, dst, src in ((x1_ready, x1_out, x1_t[u], x1[:]), (xf_ready, xf_out, acc_t[u], xf[:]),
                                                  (y_ready, y_out, row_t[u][:, :, 0:D], y[:]),
                                                  (sc_ready, sc_out, row_t[u][:, :, D:ROW], sct[:])):
                        sp.wait_ge(ready, u + 1)
                        sp.dma_start(dst, src).then_inc(done, 16)

            load_x(0)
            for w, src, done in ((wk, WkT, wk_in), (wq, WqT, wq_in), (wv, WvT, wv_in), (wo, WoT, wo_in)):
                sp.dma_start(w[:], src.rearrange("(c p) n -> p c n", p=P)).then_inc(done, 16)
            sp.dma_start(w1_raw, W1T.rearrange("(c p) n -> p c n", p=P)).then_inc(w1_in, 16)
            sp.dma_start(w2[:], W2T.rearrange("(c p) n -> p c n", p=P)).then_inc(wff_in, 16)
            sp.wait_ge(const_ready, 2)
            for c in range(C):
                sp.dma_start(gate[:, c, 0:E], gateT[c * P:(c + 1) * P, :]).then_inc(wff_in, 16)
            sp.dma_start(b1c[:], b1).then_inc(wff_in, 16)
            for dst, src in ((b2_b, b2), (g2_b, g2), (be2_b, be2), (g3_b, g3), (be3_b, be3), (lnw_b, ln_w), (lnb_b, ln_b)):
                sp.dma_start(dst[:], src.partition_broadcast(P)).then_inc(wff_in, 16)
            batches(sp, body)
            if stop != "x1":
                sp.dma_start(b1e[:], b1s).then_inc(b1e_in, 16)

                def load_expert(e, x1_part=None):
                    wait(sp, w1e_ready, e)
                    sp.dma_start(w1e, fc1T[e].rearrange("(c p) n -> p c n", p=P)).then_inc(w1e_in, 16)
                    if x1_part is not None:
                        b0, (q, k) = x1_part * 2 * N, divmod(x1_part * 2, LQ)
                        sp.dma_start(x1_s[q][:, k:k + 2], x1_d[b0:b0 + 2 * N].rearrange("(k t p) d -> p k t d", t=TT, p=P)).then_inc(x1_in, 16)
                    wait(sp, w2_ready, e)
                    sp.dma_start(w2e[:], fc2T[e].rearrange("(c p) n -> p c n", p=P)).then_inc(w2e_in, 16)
                    wait(sp, yo_ready, e * 2)
                    sp.dma_start(b2cur[:], b2s[e].partition_broadcast(P)).then_inc(b2e_in, 16)

                sp.wait_ge(f_ready, (B - 1) * F_JOBS + J_Y + 2)
                load_expert(0)
                sp.wait_ge(x1_out, 16 * B)
                sp.wait_ge(idx_ready, 1)
                for part in range(B // 2):
                    load_expert(1 + part, part)
                with sp.Fori(1 + B // 2, E) as e:
                    load_expert(e)

                for s in (xf_out, y_out, sc_out):
                    sp.wait_ge(s, 16 * B)
                sp.wait_ge(scattered, 16 * GT * E)
                for j in range(B):
                    sp.dma_start(acc_s[j // LQ][:, j % LQ], acc_t[j]).then_inc(acc_in[j], 16)
                for j in range(B):
                    sp.wait_ge(olv_ready, j + 1)
                    sp.wait_ge(olp_ready, j + 1)
                    sp.dma_start(out_t[j], x1_s[j // LQ][:, j % LQ]).then_inc(out_done, 16)
                sp.wait_ge(out_done, 16 * B)
            if stop == "x1":
                for s in (x1_out, xf_out, y_out, sc_out):
                    sp.wait_ge(s, 16 * B)
                sp.dma_start(out, {"x1": x1_d}[stop]).then_inc(x1_out, 16)
                sp.wait_ge(x1_out, 16 * B + 16)

        @block.scalar
        def _(act):
            act.dma_start(bqk[:, 0, :], bq).then_inc(bqk_in, 16)
            act.dma_start(bqk[:, 1, :], bk).then_inc(bqk_in, 16)
            act.wait_ge(const_ready, 1)
            for g in range(HG):
                act.dma_start(projbd[DH * g:DH * g + DH, M * g:M * g + M], projT).then_inc(wproj_in, 16)
            act.dma_start(bv_b[:], bv.partition_broadcast(P)).then_inc(bvo_in, 16)
            act.dma_start(bo_b[:], bo.partition_broadcast(P)).then_inc(bvo_in, 16)

            def take_a(i, n, dst, func, done, **kw):
                act.wait_ge(a_ready, i * A_JOBS + n + 1)
                nc.scalar.activation(dst, pA[n % 2][:], func, **kw).then_inc(done, 1)

            def take_f(f, n, dst, func, done, **kw):
                act.wait_ge(f_ready, f * F_JOBS + n + 1)
                nc.scalar.activation(dst, pF[n % 2][:], func, **kw).then_inc(done, 1)

            def xT_copy(i):
                for c in range(C):
                    act.wait_ge(t_ready, i * C + c + 1)
                    nc.scalar.activation(xT[:, c, :], pA[c][:], ACT.Copy).then_inc(xT_ready, 1)

            def xk_copy(i, t):
                act.wait_ge(x_ready, i * X_JOBS + J_XK + t + 1)
                nc.scalar.activation(kp[:, t, :], pX[t % 2][:].rearrange("p a b -> p (a b)"), ACT.Copy).then_inc(xk_ready, 1)

            def squares(i, m):
                wait(act, dg_ready, i * 4 + m - 1)
                take_a(i, J_DK + m, sq[:, m % 2].rearrange("p a b -> p (a b)"), ACT.Square, sq_ready)

            def take_u(u, n, k, dst, done):
                act.wait_ge(u_ready, u * U_JOBS + n + 1)
                nc.scalar.activation(dst, pF[k][:], ACT.Copy).then_inc(done, 1)

            def relu(f, n):
                take_f(f, J_H + n, h[:, n, :], ACT.Relu, h_ready, bias=b1c[:, n:n + 1])

            def cs_copy(i, n):
                act.wait_ge(a_ready, i * A_JOBS + J_CTX + n + 1)
                nc.scalar.activation(cs[:, n, :], pA[n][:, 0:G * P], ACT.Copy).then_inc(cs_ready, 1)

            def exp_k(i, t):
                if t < TT // 2:
                    act.wait_ge(ks_ready, i * (TT // 2) + t + 1)
                else:
                    act.wait_ge(ksp_ready, i * (TT // 2) + t - TT // 2 + 1)
                nc.scalar.activation(kp[:, t, :], kp[:, t, :], ACT.Exp).then_inc(ke_ready, 1)

            def eps_k(i, t):
                act.wait_ge(ke_ready, i * TT + t + 1)
                nc.scalar.activation(kp[:, t, :], kp[:, t, :], ACT.Identity, bias=epsk_c[:, 0:1]).then_inc(kp_ready, 1)

            def exp_q(i, t):
                act.wait_ge(qs_ready, i * TT + t + 1)
                nc.scalar.activation(qe[:, t, :], qe[:, t, :], ACT.Exp).then_inc(qe_ready, 1)

            def body(i, f, u):
                at_first(f, act)
                if i is not None:
                    for c in range(G):
                        take_a(i, J_K + c, kT[:, c, :], ACT.Identity, kT_ready, bias=bqk[:, 1, c:c + 1])
                    for c in range(G):
                        take_a(i, J_Q + c, qT[:, c, :], ACT.Identity, qT_ready, bias=bqk[:, 0, c:c + 1])
                    xk_copy(i, 0)
                    xk_copy(i, 1)
                    squares(i, 0)
                    squares(i, 1)
                if f is not None:
                    for c in range(C):
                        take_f(f, J_X2T + c, x2T_hi[:, c, :], ACT.Copy, x2T_ready)
                if i is not None:
                    xk_copy(i, 2)
                    squares(i, 2)
                    squares(i, 3)
                    xk_copy(i, 3)
                for step, part, k in ((relu, f, 0), (exp_q, i, 0), (exp_k, i, 0), (relu, f, 1), (relu, f, 2),
                                      (exp_k, i, 1), (relu, f, 3), (exp_q, i, 1), (relu, f, 4), (eps_k, i, 0),
                                      (relu, f, 5), (exp_k, i, 2), (relu, f, 6), (exp_q, i, 2), (relu, f, 7),
                                      (eps_k, i, 1), (exp_k, i, 3), (eps_k, i, 2), (eps_k, i, 3), (exp_q, i, 3)):
                    if part is not None:
                        step(part, k)
                if i is not None:
                    cs_copy(i, 0)
                    for n in range(TT):
                        act.wait_ge(x_ready, i * X_JOBS + J_TQ + n + 1)
                        nc.scalar.activation(qp[:, 2 * n, :], pX[n % 2][:, 0, :], ACT.Identity, bias=epsk_c[:, 0:1]).then_inc(qpa_ready, 1)
                        if n == TT - 2:
                            cs_copy(i, 1)
                if i is not None:
                    for n in range(3):
                        take_a(i, J_OUT + n, oT[:, n, :], ACT.Copy, oT_ready)
                if u is not None:
                    for c in range(C):
                        take_u(u, J_XFT + c, c, xfT[:, c, :], xfT_ready)
                if i is not None:
                    for c in range(C):
                        take_a(i, J_AT + c, aT[:, c, :], ACT.Copy, aT_ready)
                    if not (isinstance(i, int) and i == B - 1):
                        xT_copy(i + 1)
                if u is not None:
                    act.wait_ge(ls_ready, u + 1)
                    nc.scalar.activation(lg[:], lg[:], ACT.Exp).then_inc(le_ready, 1)

            act.wait_ge(const_ready, N_CONST)
            xT_copy(0)
            act.wait_ge(bqk_in, 16 * 2)
            batches(act, body)
            if stop == "x1":
                return

            def turned(e):
                for c in range(C):
                    act.wait_ge(rows_turned, e * C + c + 1)
                    nc.scalar.activation(xgT_hi[:, c, :], pM[c], ACT.Copy).then_inc(xgT_ready, 1)

            def hidden_hi(e, n):
                act.wait_ge(he_ready, e * FC + n + 1)
                nc.scalar.activation(h_hi[:, n, :], h[:, n, :], ACT.Copy).then_inc(h_hi_ready, 1)

            def expert(e, after):
                act.wait_ge(b1cur_ready, e + 1)
                for n in range(FC):
                    act.wait_ge(m_ready, e * M_JOBS + J_MH + n + 1)
                    wait(act, h_lo_ready, e * FC)
                    nc.scalar.activation(h[:, n, :], pM[n % M_SLOTS], ACT.Gelu_apprx_tanh, bias=b1cur[:, n:n + 1]).then_inc(he_ready, 1)
                    if n >= 1:
                        hidden_hi(e, n - 1)
                hidden_hi(e, FC - 1)
                if after:
                    turned(e + 1)

            turned(0)
            experts(act, expert)

            for j in range(B):
                acc = acc_s[j // LQ][:, j % LQ]
                act.wait_ge(nmr_ready, j + 1)
                for t in range(TT):
                    ins = nc.scalar.activation(acc[:, t, :], acc[:, t, :], ACT.Identity, bias=nmr[:, j, t:t + 1], scale=rsl[:, j, t:t + 1])
                ins.then_inc(nl_ready, 1)

        @block.gpsimd
        def _(pool):
            nc.gpsimd.memset(projbd[:], 0.0).then_inc(const_ready, 1)
            nc.gpsimd.memset(gate[:], 0.0).then_inc(const_ready, 1)
            nc.gpsimd.memset(ident[:], 0.0).then_inc(const_step, 1)
            pool.wait_ge(const_step, 1)
            nc.gpsimd.affine_select(out=ident[:], in_=ident[:], compare_op=ALU.not_equal, fill=1.0, base=0,
                                    pattern=[[-1, P]], channel_multiplier=1).then_inc(const_ready, 1)
            nc.gpsimd.memset(ones32[:], 1.0).then_inc(const_ready, 1)
            nc.gpsimd.memset(mhalf[:], -0.5).then_inc(const_ready, 1)
            nc.gpsimd.memset(epsk_c[:], EPS_K).then_inc(const_ready, 1)
            nc.gpsimd.memset(headmask[:], 0.0).then_inc(const_step, 1)
            nc.gpsimd.memset(denmask[:], 0.0).then_inc(const_step, 1)
            pool.wait_ge(const_step, 3)
            for k in range(2):
                rows = slice(M * k, M * k + M)
                nc.gpsimd.memset(headmask[rows, DH * k:DH * k + DH], 1.0).then_inc(const_ready, 1)
                for g in range(G):
                    nc.gpsimd.memset(denmask[rows, 4 * g:4 * g + 4, 2 * g + k:2 * g + k + 1], 1.0).then_inc(const_ready, 1)

            def selection_constants():
                nc.gpsimd.memset(ones_row[:], 1.0).then_inc(sel_const, 1)
                nc.gpsimd.memset(zero4[:], 0.0).then_inc(sel_const, 1)
                nc.gpsimd.memset(Rbd[:], 0.0).then_inc(sel_const, 1)
                for k in range(CANDS):
                    nc.gpsimd.memset(step[:, k:k + 1], (k + 1) << 27).then_inc(sel_const, 1)
                nc.gpsimd.memset(thr[:], 0).then_inc(sel_const, 1)
                for m in (blockones, blockbelow, spread, rmask):
                    nc.gpsimd.memset(m[:], 1.0).then_inc(sel_step, 1)
                nc.gpsimd.iota(iota_row[:], [[1, SA]], base=0, channel_multiplier=0).then_inc(sel_step, 1)
                pool.wait_ge(sel_step, 5)

                def keep_where(m, view, pattern, base, mult, n):
                    nc.gpsimd.affine_select(out=view, in_=view, compare_op=ALU.is_ge, fill=0.0, base=base, pattern=pattern,
                                            channel_multiplier=mult).then_inc(sel_step, 1)
                    pool.wait_ge(sel_step, n)

                n = 5
                for m in (blockones, blockbelow):
                    v3 = m[:].rearrange("p (e s) -> p e s", s=SEG)
                    n += 1
                    keep_where(m, v3, [[-SEG, E], [0, SEG]], 0, 1, n)
                    n += 1
                    keep_where(m, v3, [[SEG, E], [0, SEG]], SEG - 1, -1, n)
                n += 1
                keep_where(blockbelow, blockbelow[:], [[1, P]], -1, -1, n)
                v4 = spread[:].rearrange("p (a r) -> p a r", r=SR)
                sp1 = spread_one
                nc.gpsimd.memset(sp1[:], 0.0).then_inc(sel_step, 1)
                n += 1
                pool.wait_ge(sel_step, n)
                for q in range(4):
                    nc.gpsimd.affine_select(out=sp1[:], in_=sp1[:], compare_op=ALU.not_equal, fill=1.0, base=-SA * q,
                                            pattern=[[-1, SA]], channel_multiplier=1).then_inc(sel_step, 1)
                    n += 1
                    pool.wait_ge(sel_step, n)
                nc.gpsimd.tensor_copy(v4, sp1[:].unsqueeze(2).to_broadcast([P, SA, SR])).then_inc(sel_const, 1)
                nc.gpsimd.iota(pint[:], [[0, 1]], base=0, channel_multiplier=1).then_inc(sel_step, 1)
                nc.gpsimd.iota(tint[:], [[P, C], [C * P, SEG]], base=-(T // 2), channel_multiplier=1).then_inc(sel_step, 1)
                n += 2
                pool.wait_ge(sel_step, n)
                nc.gpsimd.tensor_copy(iotah[:], iota_row[:]).then_inc(sel_const, 1)
                nc.gpsimd.tensor_copy(idval[:], tint[:]).then_inc(sel_const, 1)
                nc.gpsimd.tensor_copy(iotaf[:], iota_row[:]).then_inc(sel_const, 1)

            def root(k, i):
                pool.wait_ge(var_ready[k], i + 1)
                settled(pool)
                nc.gpsimd.tensor_scalar(ve[k][:], mv[k][:, :, 1], LN_EPS, None, ALU.add).then_inc(ve_ready[k], 1)
                pool.wait_ge(ve_ready[k], i + 1)
                nc.gpsimd.tensor_tensor(rstd[k][:], ve[k][:], mhalf[:], ALU.pow).then_inc(rstd_ready[k], 1)

            def affine(u, buf, normed_ready, scaled, done, w_, b_):
                pool.wait_ge(normed_ready, u + 1)
                nc.gpsimd.tensor_tensor(buf[:], buf[:], w_[:].unsqueeze(1).to_broadcast([P, TT, D]), ALU.mult).then_inc(scaled, 1)
                pool.wait_ge(scaled, u + 1)
                nc.gpsimd.tensor_tensor(buf[:], buf[:], b_[:].unsqueeze(1).to_broadcast([P, TT, D]), ALU.add).then_inc(done, 1)

            def body(i, f, u):
                at_first(f, pool)
                if f is not None:
                    root(1, f)
                if u is not None:
                    root(2, u)
                if i is not None:
                    wait(pool, r_ready, i * 2)
                    pool.wait_ge(xn_ready, (i + 1) * TT)
                    nc.gpsimd.tensor_tensor(xnb[:], xn[:], bo_b[:].unsqueeze(1).to_broadcast([P, TT, D]), ALU.add).then_inc(xnb_ready, 1)
                if u is not None and f is not None:
                    affine(u, z, zn_ready, zs_ready, za_ready, g3_b, be3_b)
                if i is not None:
                    pool.wait_ge(kmax_ready, i + 1)
                    settled(pool)
                    nc.gpsimd.partition_all_reduce(stabk[:], kmax[:], P, RMAX).then_inc(stab_ready, 1)
                    pool.wait_ge(kbias_ready, i + 1)
                    for t in (TT - 2, TT - 1):
                        kt = kp[:, t, :].rearrange("p (h m) -> p h m", m=M)
                        nc.gpsimd.tensor_tensor(kt, kt, kbias[:, t, :].unsqueeze(2).to_broadcast([P, H, M]), ALU.subtract).then_inc(ksp_ready, 1)
                if u is not None:
                    root(3, u)
                if f is not None:
                    pool.wait_ge(f_ready, f * F_JOBS + J_X2T + 2)
                    nc.gpsimd.tensor_tensor(x2[:], x2[:], b2_b[:].unsqueeze(1).to_broadcast([P, TT, D]), ALU.add).then_inc(x2b_ready, 1)
                if i is not None:
                    for t in range(1, TT):
                        pool.wait_ge(kp_ready, i * TT + t + 1)
                        if t > 1:
                            pool.wait_ge(ksum_ready, i * (TT - 1) + t - 1)
                        nc.gpsimd.tensor_tensor(ksum, kp[:, 0, :] if t == 1 else ksum, kp[:, t, :], ALU.add).then_inc(ksum_ready, 1)
                if u is not None:
                    root(4, u)
                if i is not None and not (isinstance(i, int) and i == B - 1):
                    root(0, i + 1)
                if isinstance(i, int) and i == 0:
                    pool.wait_ge(w1_in, 16)
                    nc.gpsimd.tensor_copy(w1_hi[:], w1_raw).then_inc(w1_split, 1)
                    pool.wait_ge(w1_split, 1)
                    nc.gpsimd.tensor_tensor(w1_lo[:], w1_raw, w1_hi[:].bitcast(F32), ALU.subtract).then_inc(w1_split, 1)
                if u is not None:
                    root(5, u)
                    affine(u, y, yn_ready, ys_ready, y_ready, lnw_b, lnb_b)

            pool.wait_ge(const_ready, N_CONST)
            root(0, 0)
            pool.wait_ge(bvo_in, 16 * 2)
            selection_constants()
            batches(pool, body)
            if stop == "x1":
                return

            def gather(e):
                pool.wait_ge(idxg_ready, e + 1)
                settled(pool)
                for g in range(GT):
                    pool.indirect_dma_start(xg[:, g, :], None, row_d, bass.IndirectOffsetOnAxis(ap=idx_g[:, g:g + 1], axis=0)
                                            ).then_inc(gathered, 16)

            def scatter(e, tiles):
                for g in tiles:
                    pool.wait_ge(og_ready, e * GT + g + 1)
                    settled(pool)
                    pool.indirect_dma_start(acc_d, bass.IndirectOffsetOnAxis(ap=idx_s[:, g:g + 1], axis=0), og[:, g, :], None,
                                            compute_op=ALU.add).then_inc(scattered, 16)

            n = 0
            for c in range(C):
                for s0 in range(0, SEG, 4):
                    n += 1
                    ss_ = slice(s0, s0 + 4)
                    pool.wait_ge(oneb_ready, n)
                    nc.gpsimd.tensor_tensor(oneB[:, c, ss_], oneB[:, c, ss_],
                                            idval[:, c, ss_].unsqueeze(2).unsqueeze(3).to_broadcast([P, 4, E, SB]), ALU.mult).then_inc(onehot_ready, 1)

            for s in (xf_out, y_out, sc_out):
                pool.wait_ge(s, 16 * B)
            gather(0)

            def expert(e, after):
                wait(pool, scattered, e * 16 * GT)
                pool.wait_ge(idxs_ready, e + 1)
                scatter(e, range(GT // 2))
                if after == 2:
                    gather(e + 2)
                scatter(e, range(GT // 2, GT))

            gather(1)
            experts(pool, expert)

            def root_last(j):
                pool.wait_ge(vl_ready, j + 1)
                nc.gpsimd.tensor_scalar(vel[:, j], mvl[:, j, :, 1], LN_EPS, None, ALU.add).then_inc(vel_ready, 1)
                pool.wait_ge(vel_ready, j + 1)
                nc.gpsimd.tensor_tensor(rsl[:, j], vel[:, j], mhalf[:], ALU.pow).then_inc(rl_ready, 1)

            def add_last(j):
                k, half = j % LQ, slice(TT // 2, TT)
                pool.wait_ge(nl_ready, j + 1)
                pool.wait_ge(x1_in, 16 * (B // 2))
                x = x1_s[j // LQ][:, k, half]
                nc.gpsimd.tensor_tensor(x, x, acc_s[j // LQ][:, k, half], ALU.add).then_inc(olp_ready, 1)

            for j in range(B + 1):
                if j < B:
                    root_last(j)
                if j >= 1:
                    add_last(j - 1)

        @block.vector
        def _(dve):

            def over_tiles(row):
                return row[:].unsqueeze(1).to_broadcast([P, TT, D])

            def stats(k, steps, src):
                for t in range(TT):
                    ins = nc.vector.bn_stats(st[k][:, t, :], src[:, t, :])
                steps.link(ins)
                settled(dve)
                for t in range(TT):
                    ins = nc.vector.bn_aggr(mv[k][:, t, :], st[k][:, t, :])
                ins.then_inc(var_ready[k], 1)

            def normed(k, i, dst, src):
                dve.wait_ge(rstd_ready[k], i + 1)
                for t in range(TT):
                    ins = nc.vector.tensor_scalar(dst[:, t, :], src[:, t, :], mv[k][:, t, 0:1], rstd[k][:, t:t + 1],
                                                  ALU.subtract, ALU.mult)
                return ins

            def ln1_stats(i):
                steps = Steps(dve, dve_n, STEPS_N, i)
                dve.wait_ge(xin_in, (i + 1) * 16)
                stats(0, steps, xin)
                steps.end()

            def ln1_norm(i):
                wait(dve, xnb_ready, i)
                dve.wait_ge(rstd_ready[0], i + 1)
                for t in range(TT):
                    nc.vector.tensor_scalar(xn[:, t, :], xin[:, t, :], mv[0][:, t, 0:1], rstd[0][:, t:t + 1],
                                            ALU.subtract, ALU.mult).then_inc(xn_ready, 1)

            def k_max(i, t):
                dve.wait_ge(xk_ready, i * TT + t + 1)
                nc.vector.tensor_reduce(mxk[:, t, :], kp[:, t, :].rearrange("p (h m) -> p h m", m=M), AX_X,
                                        ALU.max).then_inc(kmx_ready, 1)

            def norms(i, m, dg):
                dve.wait_ge(sq_ready, i * 4 + m + 1)
                m2 = m % 2
                nc.vector.tensor_reduce(dg[:, 2 * m2:2 * m2 + 2, :], sq[:, m2].rearrange("p a (h d) -> p a h d", d=DH), AX_X,
                                        ALU.add).then_inc(dg_ready, 1)

            def k_shift(i):
                dve.wait_ge(stab_ready, i + 1)
                nc.vector.scalar_tensor_tensor(
                    out=kbias[:], in0=dgk[:], scalar=0.5 * NORM * NORM, in1=stabk[:].unsqueeze(1).to_broadcast([P, TT, H]),
                    op0=ALU.mult, op1=ALU.add).then_inc(kbias_ready, 1)
                dve.wait_ge(kbias_ready, i + 1)

            def k_sub(i, t):
                kt = kp[:, t, :].rearrange("p (h m) -> p h m", m=M)
                nc.vector.tensor_tensor(kt, kt, kbias[:, t, :].unsqueeze(2).to_broadcast([P, H, M]), ALU.subtract).then_inc(ks_ready, 1)

            def q_sub(i, t, steps):
                dve.wait_ge(x_ready, i * X_JOBS + J_XQ + t + 1)
                xq = pX[t % 2][:].rearrange("p a (h m) -> p (a h) m", m=M)
                steps.link(nc.vector.tensor_reduce(mxq[:, t, :], xq, AX_X, ALU.max))
                steps.link(nc.vector.scalar_tensor_tensor(out=qbias[:, t, :], in0=dgq[:, t, :], scalar=0.5 * NORM * NORM,
                                                          in1=mxq[:, t, :], op0=ALU.mult, op1=ALU.add))
                nc.vector.tensor_tensor(qe[:, t, :].rearrange("p (h m) -> p h m", m=M), xq,
                                        qbias[:, t, :].unsqueeze(2).to_broadcast([P, H, M]), ALU.subtract).then_inc(qs_ready, 1)

            def body(i, f, u):
                at_first(f, dve)
                more = i is not None and not (isinstance(i, int) and i == B - 1)
                if f is not None:
                    sf = Steps(dve, dve_f, STEPS_F, f)
                    dve.wait_ge(r_ready, 2 * (f + 1))
                    stats(1, sf, r)
                if u is not None:
                    su = Steps(dve, dve_u, STEPS_U, u)
                    dve.wait_ge(z_ready, 2 * (u + 1))
                    stats(2, su, z)
                if f is not None:
                    sf.link(normed(1, f, x2, r))
                    sf.link(nc.vector.tensor_tensor(x2[:], x2[:], over_tiles(g2_b), ALU.mult))
                    nc.vector.tensor_tensor(x2[:], x2[:], over_tiles(be2_b), ALU.add).then_inc(x2_ready, 1)
                    sf.end()
                if i is not None:
                    sa = Steps(dve, dve_a, STEPS_A, i)
                    for m in range(2):
                        dve.wait_ge(a_ready, i * A_JOBS + J_V + m + 1)
                        nc.vector.tensor_tensor(v[:, 2 * m:2 * m + 2, :], pA[m][:].rearrange("p (a b) -> p a b", a=2),
                                                bv_b[:].unsqueeze(1).to_broadcast([P, 2, D]), ALU.add).then_inc(v_ready, 1)
                if u is not None:
                    normed(2, u, z, z).then_inc(zn_ready, 1)
                    if f is None:
                        dve.wait_ge(zn_ready, u + 1)
                        nc.vector.tensor_tensor(z[:], z[:], over_tiles(g3_b), ALU.mult).then_inc(zs_ready, 1)
                        dve.wait_ge(zs_ready, u + 1)
                        nc.vector.tensor_tensor(z[:], z[:], over_tiles(be3_b), ALU.add).then_inc(za_ready, 1)
                if i is not None:
                    k_max(i, 0)
                    k_max(i, 1)
                    norms(i, 0, dgk)
                    norms(i, 1, dgk)
                if f is not None:
                    for c in range(C):
                        dve.wait_ge(x2T_ready, f * C + c + 1)
                        nc.vector.tensor_tensor(x2T_lo[:, c, :], pF[c][:], x2T_hi[:, c, :].bitcast(F32), ALU.subtract).then_inc(x2l_ready, 1)
                if i is not None:
                    k_max(i, 2)
                    norms(i, 2, dgq)
                    norms(i, 3, dgq)
                    k_max(i, 3)
                    dve.wait_ge(kmx_ready, (i + 1) * TT)
                    nc.vector.tensor_reduce(kmax[:], mxk[:].rearrange("p t h -> p h t"), AX_X, ALU.max).then_inc(kmax_ready, 1)
                if i is not None:
                    dve.wait_ge(dg_ready, (i + 1) * 4)
                    q_sub(i, 0, sa)
                    k_shift(i)
                    k_sub(i, 0)
                    q_sub(i, 1, sa)
                    k_sub(i, 1)
                    q_sub(i, 2, sa)
                    if u is not None:
                        dve.wait_ge(za_ready, u + 1)
                        stats(3, su, z)
                    q_sub(i, 3, sa)
                elif u is not None:
                    dve.wait_ge(za_ready, u + 1)
                    stats(3, su, z)
                if u is not None:
                    su.link(normed(3, u, z, z))
                    dve.wait_ge(xres_in, 16 * (u + 1))
                    nc.vector.tensor_tensor(x1[:], x1[:], z[:], ALU.add).then_inc(x1_ready, 1)
                    dve.wait_ge(x1_ready, u + 1)
                    stats(4, su, x1)
                if more:
                    ln1_stats(i + 1)
                def add_ff(m):
                    dve.wait_ge(f_ready, f * F_JOBS + J_Y + m + 1)
                    dve.wait_ge(x2b_ready, f + 1)
                    nc.vector.tensor_tensor(z[:, 2 * m:2 * m + 2, :], pF[m][:].rearrange("p (a b) -> p a b", a=2),
                                            x2[:, 2 * m:2 * m + 2, :], ALU.add).then_inc(z_ready, 1)

                def norm_y():
                    wait(dve, y_out, 16 * u)
                    normed(5, u, y, xf).then_inc(yn_ready, 1)

                def heads_out(t):
                    dve.wait_ge(a_ready, i * A_JOBS + J_OT + t + 1)
                    s = pA[(J_OT + t) % 2]
                    sa.link(nc.vector.reciprocal(
                        rden[:, t, :].rearrange("p (g r k) -> p g r k", g=G, k=2),
                        s[:, 2 * P:3 * P].rearrange("p (r c) -> p r c", c=32)[:, :, 0:4].rearrange("p r (g k) -> p g r k", k=2)))
                    nc.vector.tensor_tensor(at[:, t, :].rearrange("p (h d) -> p h d", d=DH),
                                            s[:, 0:2 * P].rearrange("p (h d) -> p h d", d=DH),
                                            rden[:, t, :].unsqueeze(2).to_broadcast([P, H, DH]), ALU.mult).then_inc(at_ready, 1)

                if f is not None:
                    add_ff(0)
                if i is not None:
                    for n in range(TT):
                        dve.wait_ge(x_ready, i * X_JOBS + J_TQ + n + 1)
                        nc.vector.tensor_scalar(qp[:, 2 * n + 1, :], pX[n % 2][:, 1, :], EPS_K, None, ALU.add).then_inc(qpv_ready, 1)
                    dve.wait_ge(a_ready, i * A_JOBS + J_CTXT + 1)
                    nc.vector.tensor_tensor(ctxbd[:], pA[0][:, 0:G * P].rearrange("p (a b) -> p a b", b=32),
                                            headmask[:].unsqueeze(1).to_broadcast([P, PAIRS, 32]), ALU.mult).then_inc(cx_ready, 1)
                    nc.vector.tensor_tensor(denbd[:], pA[0][:, G * P:512].rearrange("p (a b) -> p a b", b=32),
                                            denmask[:], ALU.mult).then_inc(cx_ready, 1)
                if u is not None:
                    wait(dve, xf_out, 16 * u)
                    normed(4, u, xf, x1).then_inc(xf_ready, 1)
                if more:
                    ln1_norm(i + 1)
                if u is not None:
                    dve.wait_ge(xf_ready, u + 1)
                    stats(5, su, xf)
                if f is not None:
                    add_ff(1)
                if i is not None:
                    for t in range(TT):
                        heads_out(t)
                if u is not None:
                    if f is not None:
                        norm_y()
                    for m in range(2):
                        dve.wait_ge(u_ready, u * U_JOBS + J_G + m + 1)
                        nc.vector.tensor_copy(lg[:, 2 * m:2 * m + 2, :],
                                              pF[m][:, 0:2 * P].rearrange("p (a b) -> p a b", a=2)[:, :, 0:E]).then_inc(lg_ready, 1)
                    dve.wait_ge(lg_ready, 2 * (u + 1))
                    su.link(nc.vector.tensor_reduce(lmx[:], lg[:], AX_X, ALU.max))
                    nc.vector.tensor_tensor(lg[:], lg[:], lmx[:].unsqueeze(2).to_broadcast([P, TT, E]), ALU.subtract).then_inc(ls_ready, 1)
                if i is not None:
                    dve.wait_ge(xnb_ready, i + 1)
                    for m in range(2):
                        dve.wait_ge(a_ready, i * A_JOBS + J_WO + m + 1)
                        nc.vector.tensor_tensor(r[:, 2 * m:2 * m + 2, :], pA[m][:].rearrange("p (a b) -> p a b", a=2),
                                                xnb[:, 2 * m:2 * m + 2, :], ALU.add).then_inc(r_ready, 1)
                    sa.end()
                if u is not None:
                    dve.wait_ge(le_ready, u + 1)
                    su.link(nc.vector.tensor_reduce(lsum[:], lg[:], AX_X, ALU.add))
                    su.link(nc.vector.reciprocal(lrec[:], lsum[:]))
                    wait(dve, sc_out, 16 * u)
                    lr = lrec[:].unsqueeze(2).to_broadcast([P, TT, E])
                    for c in range(C):
                        nc.vector.tensor_tensor(sc[:, c, :, bass.ts(u, 2)].rearrange("p e s -> p s e"),
                                                lg[:].rearrange("p (s c) e -> p c s e", c=C)[:, c],
                                                lrec[:].rearrange("p (s c) -> p c s", c=C)[:, c].unsqueeze(2).to_broadcast([P, 2, E]), ALU.mult)
                    nc.vector.tensor_tensor(sct[:], lg[:], lr, ALU.mult).then_inc(sc_ready, 1)
                    if f is None:
                        norm_y()
                    su.end()

            ln1_stats(0)
            ln1_norm(0)
            dve.wait_ge(wproj_in, 16 * HG)
            nc.vector.tensor_scalar(projbd[:], projbd[:], NORM, None, ALU.mult).then_inc(proj_ready, 1)
            dve.wait_ge(bvo_in, 16 * 2)
            dve.wait_ge(const_ready, N_CONST)
            batches(dve, body)
            if stop == "x1":
                return

            dve.wait_ge(sel_const, N_SEL)
            done = Steps(dve, dve_s, 0, 0)
            done.link(nc.vector.tensor_scalar(pmod[:], pint[:], SR - 1, None, ALU.bitwise_and))
            done.link(nc.vector.tensor_copy(pmodf[:], pmod[:]))
            done.link(nc.vector.tensor_scalar(rmask[:], iotaf[:, 0:SR], pmodf[:, 0:1], None, ALU.is_equal))
            dve.wait_ge(s_turned, 1)
            nc.vector.tensor_copy(S, pA[0][:, 0:SEGW]).then_inc(s_ready, 1)
            dve.wait_ge(s_ready, 1)

            done.link(nc.vector.tensor_copy(S_hi, S.bitcast(BF16).rearrange("p (j h) -> p j h", h=2)[:, :, 1]))

            def search(rd, s, fl):
                ss = Steps(dve, dve_r, SEL_STEPS, rd)
                for k in range(CANDS):
                    nc.vector.tensor_scalar(fl[:, k], s, cand[:, k:k + 1].bitcast(F32), None, ALU.is_ge, ALU.add,
                                            accum_out=cnt[:, k:k + 1]).then_inc(cnt_ready, 1)
                ss.link(nc.vector.tensor_scalar(nstep[:], step[:], 3, None, ALU.logical_shift_right))
                ss.put(nc.vector.tensor_tensor(base[:], nstep[:], thr[:].to_broadcast([P, CANDS]), ALU.bitwise_or))
                dve.wait_ge(tot_ready, rd + 1)
                ss.link(nc.vector.tensor_scalar(passed[:], pA[1][:, 0:CANDS], KEEP - 0.5, None, ALU.is_ge, ALU.add,
                                                accum_out=npass[:]))
                ss.link(nc.vector.tensor_scalar(up[:], step[:, 0:1], npass[:, 0:1], None, ALU.mult))
                ss.put(nc.vector.tensor_tensor(cand[:], base[:], up[:].to_broadcast([P, CANDS]), ALU.bitwise_or))
                ss.put(nc.vector.tensor_tensor(thr[:], thr[:], up[:], ALU.bitwise_or))
                ss.link(nc.vector.tensor_copy(step[:], nstep[:]))
                ss.end()

            done.link(nc.vector.tensor_copy(cand[:], step[:]))
            with dve.Fori(0, HI_ROUNDS // 2) as r2:
                search(r2 * 2, S_hi, flags_hi)
                search(r2 * 2 + 1, S_hi, flags_hi)
            with dve.Fori(HI_ROUNDS // 2, ROUNDS // 2) as r2:
                search(r2 * 2, S, flags)
                search(r2 * 2 + 1, S, flags)
            cut = thr[:, 0:1].bitcast(F32)
            nc.vector.tensor_scalar(gt, S, cut, None, ALU.is_gt, ALU.add, accum_out=pair_cnt[:, 0:1])
            nc.vector.tensor_scalar(eq, S, cut, None, ALU.is_equal, ALU.add, accum_out=pair_cnt[:, 1:2]).then_inc(pair_ready, 1)
            dve.wait_ge(pair_ready, 1)
            nc.vector.tensor_tensor_scan(gin, ones_row[:], gt, 0.0, ALU.mult, ALU.add)
            nc.vector.tensor_tensor_scan(ein, ones_row[:], eq, 0.0, ALU.mult, ALU.add)
            dve.wait_ge(off_ready, 1)
            done.link(nc.vector.tensor_copy(offs[:], pA[0][:, 0:3]))
            done.link(nc.vector.tensor_tensor(eoff[:], offs[:, 1:2], offs[:, 2:3], ALU.add))
            done.link(nc.vector.tensor_scalar(ein, ein, eoff[:, 0:1], None, ALU.add))
            done.link(nc.vector.tensor_tensor(eq, eq, ein, ALU.mult))
            done.link(nc.vector.scalar_tensor_tensor(out=eq, in0=ein, scalar=KEEP + 0.5, in1=eq, op0=ALU.is_le, op1=ALU.mult))
            done.link(nc.vector.scalar_tensor_tensor(out=gin, in0=gin, scalar=offs[:, 0:1], in1=gt, op0=ALU.add, op1=ALU.mult))
            nc.vector.tensor_tensor(place, gin, eq, ALU.add).then_inc(place_ready, 1)
            dve.wait_ge(place_turned, 1)
            done.link(nc.vector.tensor_scalar(placei.rearrange("p c e s -> p (c e s)"), pA[1][:, 0:SEGW], 1.0, None, ALU.subtract))
            nc.vector.tensor_scalar(digi_a, placei, 4, None, ALU.arith_shift_right)
            done.link(nc.vector.tensor_scalar(digi_b, placei, SB - 1, None, ALU.bitwise_and))
            nc.vector.tensor_copy(dig_a, digi_a)
            done.link(nc.vector.tensor_copy(dig_b, digi_b))
            for c in range(C):
                for s0 in range(0, SEG, 4):
                    ss_ = slice(s0, s0 + 4)
                    nc.vector.tensor_tensor(oneB[:, c, ss_], dig_b[:, c, :, ss_].rearrange("p e s -> p s e").unsqueeze(3).to_broadcast([P, 4, E, SB]),
                                            iotah[:, 0:SB].unsqueeze(1).unsqueeze(1).to_broadcast([P, 4, E, SB]), ALU.is_equal).then_inc(oneb_ready, 1)
                    nc.vector.tensor_tensor(oneA[:, c, ss_], dig_a[:, c, :, ss_].rearrange("p e s -> p s e").unsqueeze(3).to_broadcast([P, 4, E, SA]),
                                            iotah[:].unsqueeze(1).unsqueeze(1).to_broadcast([P, 4, E, SA]), ALU.is_equal).then_inc(onea_ready, 1)
            dve.wait_ge(ids_ready, 1)
            for k in range(2):
                for q in range(4):
                    ins = nc.vector.tensor_copy(Rbd[SA * q:SA * q + SA, k, q, :], pX[0][SA * q:SA * q + SA, k, SB * q:SB * (q + 1)])
            ins.then_inc(rbd_ready, 1)
            dve.wait_ge(spread_ready, 1)
            done.link(nc.vector.tensor_tensor(idm[:], pX[1][:, 0, 0:E * SB].rearrange("p (x r g) -> p x r g", r=SR, g=GT),
                                              rmask[:].unsqueeze(1).unsqueeze(3).to_broadcast([P, E, SR, GT]), ALU.mult))
            done.link(nc.vector.tensor_reduce(idf[:], idm[:].rearrange("p x r g -> p x g r"), AX_X, ALU.add))
            nc.vector.tensor_scalar(idx[:], idf[:], float(T // 2), None, ALU.add).then_inc(idx_ready, 1)
            dve.wait_ge(idx_ready, 1)

            def idx_for_gather(e):
                wait(dve, gathered, e * 16 * GT)
                wait(dve, rows_turned, e * C)
                nc.vector.tensor_tensor(idx_g[:], idx[:, bass.ds(e, 1), :].rearrange("p a g -> p (a g)"), zero4[:, 0:GT], ALU.add).then_inc(idxg_ready, 1)

            def next_weights(e):
                dve.wait_ge(gathered, (e + 1) * 16 * GT)
                wait(dve, wcur_ready, e)
                nc.vector.tensor_tensor(wnext[:], xg[:, :, bass.ds(e + D, 1)].rearrange("p g a -> p (g a)"), zero4[:, 0:GT], ALU.add).then_inc(wnext_ready, 1)

            def expert(e, after):
                dve.wait_ge(wnext_ready, e + 1)
                wait(dve, og_ready, e * GT)
                nc.vector.tensor_copy(wcur[:], wnext[:]).then_inc(wcur_ready, 1)
                split_w2(e)
                for n in range(FC):
                    dve.wait_ge(h_hi_ready, e * FC + n + 1)
                    nc.vector.tensor_tensor(h_lo[:, n, :], h[:, n, :], h_hi[:, n, :].bitcast(F32), ALU.subtract).then_inc(h_lo_ready, 1)
                wait(dve, scattered, e * 16 * GT)
                nc.vector.tensor_tensor(idx_s[:], idx[:, bass.ds(e, 1), :].rearrange("p a g -> p (a g)"), zero4[:, 0:GT], ALU.add).then_inc(idxs_ready, 1)
                if after:
                    dve.wait_ge(m_ready, e * M_JOBS + J_MY)
                    split_w1(e + 1)
                    rest_of_rows(e + 1)
                dve.wait_ge(b2e_in, 16 * (e + 1))
                dve.wait_ge(wcur_ready, e + 1)
                for m in range(2):
                    dve.wait_ge(m_ready, e * M_JOBS + J_MY + m + 1)
                    nc.vector.tensor_tensor(og[:, 2 * m:2 * m + 2, :], pM[2 + m].rearrange("p (a b) -> p a b", a=2),
                                            b2cur[:].unsqueeze(1).to_broadcast([P, 2, D]), ALU.add).then_inc(yo_ready, 1)
                    dve.wait_ge(yo_ready, e * 2 + m + 1)
                    for g in (2 * m, 2 * m + 1):
                        nc.vector.tensor_scalar(og[:, g, :], og[:, g, :], wcur[:, g:g + 1], None, ALU.mult).then_inc(og_ready, 1)
                    if m == 0 and after:
                        next_weights(e + 1)
                        if after == 2:
                            idx_for_gather(e + 2)
                if after:
                    biases(e + 1)

            def biases(e):
                wait(dve, he_ready, e * FC)
                nc.vector.tensor_tensor(b1cur[:], b1e[:, bass.ds(e, 1), :].rearrange("p a n -> p (a n)"), zero4[:], ALU.add).then_inc(b1cur_ready, 1)

            def split_w1(e):
                dve.wait_ge(w1e_in, 16 * (e + 1))
                nc.vector.tensor_copy(w1_hi[:], w1e).then_inc(w1e_hi_ready, 1)
                dve.wait_ge(w1e_hi_ready, e + 1)
                nc.vector.tensor_tensor(w1_lo[:], w1e, w1_hi[:].bitcast(F32), ALU.subtract).then_inc(w1e_ready, 1)

            def split_w2(e):
                dve.wait_ge(w2e_in, 16 * (e + 1))
                wait(dve, m_ready, e * M_JOBS)
                nc.vector.tensor_copy(w2_hi[:], w2e[:]).then_inc(w2_hi_ready, 1)
                dve.wait_ge(w2_hi_ready, e + 1)
                nc.vector.tensor_tensor(w2_lo[:], w2e[:], w2_hi[:].bitcast(F32), ALU.subtract).then_inc(w2_ready, 1)

            def rest_of_rows(e):
                for c in range(C):
                    dve.wait_ge(xgT_ready, e * C + c + 1)
                    nc.vector.tensor_tensor(xgT_lo[:, c, :], pM[c], xgT_hi[:, c, :].bitcast(F32), ALU.subtract).then_inc(xgl_ready, 1)

            dve.wait_ge(b1e_in, 16)
            idx_for_gather(0)
            split_w1(0)
            biases(0)
            rest_of_rows(0)
            next_weights(0)
            idx_for_gather(1)
            experts(dve, expert)

            def stats_last(j):
                dve.wait_ge(acc_in[j], 16)
                for t in range(TT):
                    ins = nc.vector.bn_stats(stl[:, j, t, :], acc_s[j // LQ][:, j % LQ, t, :])
                ins.then_inc(stl_ready, 1)
                dve.wait_ge(stl_ready, j + 1)
                for t in range(TT):
                    ins = nc.vector.bn_aggr(mvl[:, j, t, :], stl[:, j, t, :])
                ins.then_inc(vl_ready, 1)

            def shift_last(j):
                dve.wait_ge(rl_ready, j + 1)
                nc.vector.scalar_tensor_tensor(out=nmr[:, j], in0=mvl[:, j, :, 0], scalar=-1.0, in1=rsl[:, j], op0=ALU.mult,
                                               op1=ALU.mult).then_inc(nmr_ready, 1)

            def add_last(j):
                k, half = j % LQ, slice(0, TT // 2)
                dve.wait_ge(nl_ready, j + 1)
                dve.wait_ge(x1_in, 16 * (B // 2))
                x = x1_s[j // LQ][:, k, half]
                nc.vector.tensor_tensor(x, x, acc_s[j // LQ][:, k, half], ALU.add).then_inc(olv_ready, 1)

            for j in range(B + 2):
                if j < B:
                    stats_last(j)
                if 1 <= j < B + 1:
                    shift_last(j - 1)
                if j >= 2:
                    add_last(j - 2)

        @block.tensor
        def _(pe):
            a_taker = ([(kT_ready, 2, c) for c in range(2)] + [(qT_ready, 2, c) for c in range(2)]
                       + [(v_ready, 2, m) for m in range(2)] + [(sq_ready, 4, m) for m in range(4)] + [(cs_ready, 2, m) for m in range(2)]
                       + [(cx_ready, 2, 1)] + [(oT_ready, 3, m) for m in range(3)] + [(at_ready, 4, t) for t in range(4)]
                       + [(aT_ready, 2, c) for c in range(2)] + [(r_ready, 2, m) for m in range(2)])
            f_order = ([("f", x2l_ready, 2, c) for c in range(2)] + [("f", h_ready, FC, n) for n in range(FC)] + [("f", z_ready, 2, m) for m in range(2)]
                       + [("u", xfT_ready, 2, c) for c in range(2)] + [("u", lg_ready, 2, m) for m in range(2)])
            f_place = {part: [k for k, x in enumerate(f_order) if x[0] == part] for part in "fu"}
            assert len(a_taker) == A_JOBS and len(f_place["f"]) == F_JOBS and len(f_place["u"]) == U_JOBS

            def slot_a(i, n):
                if J_WO <= n and not (isinstance(i, int) and i == B - 1):
                    pe.wait_ge(xT_ready, (i + 1) * C + n - J_WO + 1)
                elif n < 2:
                    s, per, k = a_taker[A_JOBS + n - 2]
                    wait(pe, s, (i - 1) * per + k + 1)
                else:
                    s, per, k = a_taker[n - 2]
                    pe.wait_ge(s, i * per + k + 1)
                return pA[n % 2]

            def turn_x(i):
                pe.wait_ge(xn_ready, (i + 1) * TT)
                for c in range(C):
                    wait(pe, aT_ready, (i - 1) * C + c + 1)
                    turn_tokens(pA[c], xn, c).then_inc(t_ready, 1)

            def slot_f(f, u, part, n):
                k = f_place[part][n]
                now, before = {"f": f, "u": u}, {"f": u if f is None else f - 1, "u": None if u is None else u - 1}
                for j in range(k - 2, k - 2 - 2 * len(f_order), -2):
                    p, s, per, m = f_order[j % len(f_order)]
                    b = (now if j >= 0 else before)[p]
                    if b is not None and not (isinstance(b, int) and b < 0):
                        wait(pe, s, b * per + m + 1)
                        break
                return pF[k % 2]

            def slot_x(i, n):
                if n < 2:
                    wait(pe, qpa_ready, (i - 1) * TT + TT - 1 + n)
                    wait(pe, qpv_ready, (i - 1) * TT + TT - 1 + n)
                elif n < 6:
                    pe.wait_ge(xk_ready, i * TT + n - 1)
                elif n < 10:
                    pe.wait_ge(qs_ready, i * TT + n - 5)
                else:
                    pe.wait_ge(qpa_ready, i * TT + n - 9)
                    pe.wait_ge(qpv_ready, i * TT + n - 9)
                return pX[n % 2]

            def turn(dst, src):
                return nc.tensor.transpose(dst, src, ident[:])

            def tok(t):
                return slice(t * P, (t + 1) * P)

            def turn_tokens(dst, src, c):
                for t in range(TT):
                    ins = turn(dst[:, tok(t)], src[:, t, tok(c)])
                return ins

            def by_tokens(dst, xt, w, m, ks):
                for t2 in range(2):
                    for k in range(ks):
                        ins = nc.tensor.matmul(dst[:, t2 * D:(t2 + 1) * D], xt[:, k, tok(2 * m + t2)], w[:, k, :],
                                               start=(k == 0), stop=(k == ks - 1))
                return ins

            def by_features(dst, w, xt, n, ks):
                for k in range(ks):
                    ins = nc.tensor.matmul(dst[:], w[:, k, tok(n)], xt[:, k, :], start=(k == 0), stop=(k == ks - 1))
                return ins

            def by_halves(dst, w_hi, w_lo, x_hi, x_lo, n):
                parts = [(k, w_, x_) for k in range(C) for w_, x_ in ((w_lo, x_hi), (w_hi, x_lo), (w_hi, x_hi))]
                for m, (k, w_, x_) in enumerate(parts):
                    ins = nc.tensor.matmul(dst[:], w_[:, k, tok(n)], x_[:, k, :], start=(m == 0), stop=(m == len(parts) - 1))
                return ins

            def features(i, n, src, t):
                s = slot_x(i, n)
                for g in range(G):
                    ins = nc.tensor.matmul(s[:, g, :], src[:, g, tok(t)], projbd[:], start=True, stop=True)
                ins.then_inc(x_ready, 1)

            def turn_heads(i, m, src):
                s = slot_a(i, J_DK + m)
                for t2 in range(2):
                    for g in range(G):
                        ins = turn(s[:, t2 * D + g * P:t2 * D + (g + 1) * P], src[:, g, tok(2 * (m % 2) + t2)])
                ins.then_inc(a_ready, 1)

            def body(i, f, u):
                att, ff, gt_ = i is not None, f is not None, u is not None

                def first_batch(w_in):
                    if isinstance(i, int) and i == 0:
                        pe.wait_ge(w_in, 16)

                def hidden(n):
                    s = slot_f(f, u, "f", J_H + n)
                    by_halves(s, w1_hi, w1_lo, x2T_hi, x2T_lo, n).then_inc(f_ready, 1)

                def ff_out(m, slots, half):
                    if half == 0:
                        slots[m] = slot_f(f, u, "f", J_Y + m)
                    for k in range(FC):
                        if m == half == 0:
                            pe.wait_ge(h_ready, f * FC + k + 1)
                        ins = nc.tensor.matmul(slots[m][:, half * D:(half + 1) * D], h[:, k, tok(2 * m + half)], w2[:, k, :],
                                               start=(k == 0), stop=(k == FC - 1))
                    if half == 1:
                        ins.then_inc(f_ready, 1)

                def attention_out(j, w_, first, last_):
                    s = slot_a(i, j)
                    for g in range(first, last_ + 1):
                        for q in range(4):
                            ins = nc.tensor.matmul(s[32 * q:32 * q + 32, :], w_[:, 4 * g + q, :], qp[:, 4 * g + q, :],
                                                   start=(g == first), stop=(g == last_), tile_position=(0, 32 * q))
                    ins.then_inc(a_ready, 1)

                def turn_q(n):
                    s = slot_x(i, J_TQ + n)
                    for k in range(2):
                        for t in range(TT):
                            ins = turn(s[:, k, tok(t)], qe[:, t, tok(2 * n + k)])
                    ins.then_inc(x_ready, 1)

                def turn_out(t):
                    s = slot_a(i, J_OT + t)
                    for n in range(3):
                        ins = turn(s[:, tok(n)], oT[:, n, tok(t)])
                    ins.then_inc(a_ready, 1)

                def gates(m):
                    s = slot_f(f, u, "u", J_G + m)
                    for t2 in range(2):
                        for c in range(C):
                            ins = nc.tensor.matmul(s[:, tok(t2)], xfT[:, c, tok(2 * m + t2)], gate[:, c, :],
                                                   start=(c == 0), stop=(c == C - 1))
                    ins.then_inc(u_ready, 1)

                at_first(f, pe)
                if att:
                    pe.wait_ge(xT_ready, (i + 1) * C)
                    for j0, w, w_in in ((J_K, wk, wk_in), (J_Q, wq, wq_in)):
                        first_batch(w_in)
                        for c in range(G):
                            by_features(slot_a(i, j0 + c), w, xT, c, C).then_inc(a_ready, 1)
                    first_batch(wv_in)
                    for m in range(2):
                        by_tokens(slot_a(i, J_V + m), xT, wv, m, C).then_inc(a_ready, 1)
                    pe.wait_ge(kT_ready, (i + 1) * G)
                    if isinstance(i, int) and i == 0:
                        pe.wait_ge(proj_ready, 1)
                    features(i, J_XK, kT, 0)
                    features(i, J_XK + 1, kT, 1)
                    turn_heads(i, 0, kT)
                    turn_heads(i, 1, kT)
                if ff:
                    pe.wait_ge(x2_ready, f + 1)
                    for c in range(C):
                        turn_tokens(slot_f(f, u, "f", J_X2T + c), x2, c).then_inc(f_ready, 1)
                if att:
                    features(i, J_XK + 2, kT, 2)
                    pe.wait_ge(qT_ready, (i + 1) * G)
                    turn_heads(i, 2, qT)
                    turn_heads(i, 3, qT)
                    features(i, J_XK + 3, kT, 3)
                if ff:
                    pe.wait_ge(x2l_ready, (f + 1) * C)
                    if isinstance(f, int) and f == 0:
                        pe.wait_ge(w1_split, 2)
                done_h = 0
                for t, until in ((0, 1), (1, 3), (2, 6), (3, FC)):
                    if att:
                        features(i, J_XQ + t, qT, t)
                    if ff:
                        for n in range(done_h, until):
                            hidden(n)
                    done_h = until
                slots = [None, None]
                if ff:
                    for half in range(2):
                        ff_out(0, slots, half)
                if att:
                    pe.wait_ge(kp_ready, (i + 1) * TT)
                    pe.wait_ge(v_ready, (i + 1) * 2)
                    s = slot_a(i, J_CTX)
                    for g in range(G):
                        for t in range(TT):
                            for q in range(4):
                                pair = 4 * g + q
                                ins = nc.tensor.matmul(s[32 * q:32 * q + 32, g * P:(g + 1) * P], v[:, t, 32 * pair:32 * pair + 32],
                                                       kp[:, t, P * pair:P * pair + P], start=(t == 0), stop=(t == TT - 1),
                                                       tile_position=(0, 32 * q))
                    ins.then_inc(a_ready, 1)
                    pe.wait_ge(qe_ready, (i + 1) * TT)
                    for n in range(TT - 1):
                        turn_q(n)
                    pe.wait_ge(ksum_ready, (i + 1) * (TT - 1))
                    s = slot_a(i, J_KSUM)
                    for g in range(G):
                        for q in range(4):
                            pair = 4 * g + q
                            ins = nc.tensor.matmul(s[32 * q:32 * q + 32, g * P:(g + 1) * P], ones32[:], ksum[:, P * pair:P * pair + P],
                                                   start=True, stop=True, tile_position=(0, 32 * q))
                    ins.then_inc(a_ready, 1)
                    turn_q(TT - 1)
                    pe.wait_ge(cs_ready, (i + 1) * 2)
                    s = slot_a(i, J_CTXT)
                    for n in range(2):
                        for g in range(G):
                            ins = turn(s[:, (2 * n + g) * P:(2 * n + g + 1) * P], cs[:, n, tok(g)])
                    ins.then_inc(a_ready, 1)
                if ff:
                    ff_out(1, slots, 0)
                if att:
                    pe.wait_ge(cx_ready, (i + 1) * 2)
                    pe.wait_ge(qpa_ready, (i + 1) * TT)
                    pe.wait_ge(qpv_ready, (i + 1) * TT)
                    attention_out(J_OUT, ctxbd, 0, 0)
                    attention_out(J_OUT + 1, ctxbd, 1, 1)
                    attention_out(J_OUT + 2, denbd, 0, 1)
                if ff:
                    ff_out(1, slots, 1)
                if att:
                    pe.wait_ge(oT_ready, (i + 1) * 3)
                    turn_out(0)
                    turn_out(1)
                if gt_:
                    pe.wait_ge(xf_ready, u + 1)
                    for c in range(C):
                        turn_tokens(slot_f(f, u, "u", J_XFT + c), xf, c).then_inc(u_ready, 1)
                if att:
                    turn_out(2)
                    turn_out(3)
                if gt_:
                    pe.wait_ge(xfT_ready, (u + 1) * C)
                    gates(0)
                    gates(1)
                if att:
                    pe.wait_ge(at_ready, (i + 1) * TT)
                    for c in range(C):
                        turn_tokens(slot_a(i, J_AT + c), at, c).then_inc(a_ready, 1)
                    if not (isinstance(i, int) and i == B - 1):
                        turn_x(i + 1)
                    pe.wait_ge(aT_ready, (i + 1) * C)
                    first_batch(wo_in)
                    for m in range(2):
                        by_tokens(slot_a(i, J_WO + m), aT, wo, m, C).then_inc(a_ready, 1)

            pe.wait_ge(const_ready, N_CONST)
            turn_x(0)
            batches(pe, body)
            if stop == "x1":
                return

            pe.wait_ge(sel_const, N_SEL)
            pe.wait_ge(sc_ready, B)
            pe.wait_ge(r_ready, 2 * B)
            for c in range(C):
                ins = turn(pA[0][:, tok(c)], sc[:, c].rearrange("p e s -> p (e s)"))
            ins.then_inc(s_turned, 1)

            with pe.Fori(0, ROUNDS) as rd:
                pe.wait_ge(cnt_ready, (rd + 1) * CANDS)
                nc.tensor.matmul(pA[1][:, 0:CANDS], blockones[:], cnt[:], start=True, stop=True).then_inc(tot_ready, 1)
            pe.wait_ge(pair_ready, 1)
            pe.wait_ge(s_ready, 1)
            nc.tensor.matmul(pA[0][:, 0:2], blockbelow[:], pair_cnt[:], start=True, stop=True)
            nc.tensor.matmul(pA[0][:, 2:3], blockones[:], pair_cnt[:, 0:1], start=True, stop=True).then_inc(off_ready, 1)
            pe.wait_ge(place_ready, 1)
            for c in range(C):
                ins = turn(pA[1][:, tok(c)], place[:, tok(c)])
            ins.then_inc(place_turned, 1)
            n = 0
            for c in range(C):
                for s0 in range(0, SEG, 4):
                    n += 1
                    pe.wait_ge(onea_ready, n)
                    pe.wait_ge(onehot_ready, n)
                    for s_ in range(s0, s0 + 4):
                        first, final = n == 1 and s_ == 0, c == C - 1 and s_ == SEG - 1
                        for k in range(2):
                            ins = nc.tensor.matmul(pX[0][:, k, 0:4 * SB], oneA[:, c, s_, 4 * k:4 * k + 4, :].rearrange("p e a -> p (e a)"),
                                                   oneB[:, c, s_, 4 * k:4 * k + 4].rearrange("p e b -> p (e b)"), start=first, stop=final)
            ins.then_inc(ids_ready, 1)
            pe.wait_ge(rbd_ready, 1)
            nc.tensor.matmul(pX[1][:, 0, 0:P], spread[:], Rbd[:].rearrange("p k q b -> p (k q b)"), start=True, stop=True).then_inc(spread_ready, 1)
            pe.wait_ge(idx_ready, 1)

            def rows_by_halves(e, m):
                for t2 in range(2):
                    for k in range(FC):
                        if m == 0 and t2 == 0:
                            pe.wait_ge(h_lo_ready, e * FC + k + 1)
                        for j, (h_, w_) in enumerate(((h_hi, w2_lo), (h_lo, w2_hi), (h_hi, w2_hi))):
                            ins = nc.tensor.matmul(pM[2 + m][:, t2 * D:(t2 + 1) * D], h_[:, k, tok(2 * m + t2)], w_[:, k, :],
                                                   start=(k == 0 and j == 0), stop=(k == FC - 1 and j == 2))
                return ins

            def turn_rows(e):
                pe.wait_ge(gathered, (e + 1) * 16 * GT)
                for c in range(C):
                    wait(pe, he_ready, (e - 1) * FC + FC - M_SLOTS + c + 1)
                    turn_tokens(pM[c], xg, c).then_inc(rows_turned, 1)

            def expert(e, after):
                pe.wait_ge(w1e_ready, e + 1)
                pe.wait_ge(xgl_ready, (e + 1) * C)
                for n in range(FC):
                    if n >= M_SLOTS:
                        pe.wait_ge(he_ready, e * FC + n - M_SLOTS + 1)
                    elif n >= 2:
                        wait(pe, yo_ready, (e - 1) * 2 + n - 2 + 1)
                    by_halves(pM[n % M_SLOTS], w1_hi, w1_lo, xgT_hi, xgT_lo, n).then_inc(m_ready, 1)
                if after:
                    turn_rows(e + 1)
                pe.wait_ge(w2_ready, e + 1)
                pe.wait_ge(he_ready, (e + 1) * FC)
                for m in range(2):
                    rows_by_halves(e, m).then_inc(m_ready, 1)

            turn_rows(0)
            experts(pe, expert)


_COL = lambda a: a.reshape(-1, P).T
_LAYOUT = {
    "video": ("L0_attn_video", lambda a: a.reshape(T, D)),
    "WqT": ("L0_attn_Wq", lambda a: a.T), "bq": ("L0_attn_bq", _COL),
    "WkT": ("L0_attn_Wk", lambda a: a.T), "bk": ("L0_attn_bk", _COL),
    "WvT": ("L0_attn_Wv", lambda a: a.T), "bv": ("L0_attn_bv", None),
    "WoT": ("L0_attn_Wo", lambda a: a.T), "bo": ("L0_attn_bo", None),
    "projT": ("L0_attn_proj", lambda a: a.T),
    "W1T": ("L0_attn_W1", lambda a: a.T), "b1": ("L0_attn_b1", _COL),
    "W2T": ("L0_attn_W2", lambda a: a.T), "b2": ("L0_attn_b2", None),
    "g2": ("L0_attn_g2", None), "be2": ("L0_attn_be2", None),
    "g3": ("L0_attn_g3", None), "be3": ("L0_attn_be3", None),
    "gateT": ("L0_ffn_gate_w", lambda a: a.T),
    "ln_w": ("L0_ffn_ln_w", None), "ln_b": ("L0_ffn_ln_b", None),
    "fc1T": ("L0_ffn_fc1s", lambda a: a.transpose(0, 2, 1)),
    "b1s": ("L0_ffn_b1s", lambda a: a.reshape(E, FC, P).transpose(2, 0, 1)),
    "fc2T": ("L0_ffn_fc2s", lambda a: a.transpose(0, 2, 1)),
    "b2s": ("L0_ffn_b2s", None),
}


def kernel(**inputs):
    import concourse.bacc as bacc
    from concourse.bass_utils import run_bass_kernel_spmd

    nc = bacc.Bacc("TRN2", target_bir_lowering=False, num_devices=1)
    arrays, args = {}, []
    for name, (source, layout) in _LAYOUT.items():
        a = np.asarray(inputs[source])
        a = np.ascontiguousarray(layout(a) if layout else a)
        arrays[name] = a
        args.append(nc.dram_tensor(name, a.shape, mybir.dt.from_np(a.dtype), kind="ExternalInput").ap())
    out = nc.dram_tensor("out", (T, D), F32, kind="ExternalOutput").ap()
    build(nc, *args, out)
    res = run_bass_kernel_spmd(nc, [arrays], core_ids=[0])
    return res.results[0]["out"].reshape(B, N, D)
```
